# Optimizing a Trainium2 kernel written in Bass

```python
import numpy as np
import jax
import jax.numpy as jnp

def _softmax(x, axis=-1):
    return jax.nn.softmax(x, axis=axis)

def _gelu(x):
    return jax.nn.gelu(x, approximate=True)

def _silu(x):
    return jax.nn.silu(x)

def _sigmoid(x):
    return jax.nn.sigmoid(x)

def _layernorm(x, axis=-1, eps=1e-05):
    m = jnp.mean(x, axis=axis, keepdims=True)
    v = jnp.var(x, axis=axis, keepdims=True)
    return (x - m) / jnp.sqrt(v + eps)

def _scatter_add(tgt, idx, src, axis=0):
    return tgt.at[idx].add(src)

def _segment_sum(src, seg, n):
    return jax.ops.segment_sum(src, seg, n)
kernel_name = 'mk_seq_postln_d2_jaxref_r8_af3cf1'

def setup_inputs(seed: int=0):
    np.random.seed(seed)
    _w = jnp.asarray

    def _L0_attn_setup():
        import jax, jax.numpy as jnp
        import numpy as np
        B, L, DM = (4, 256, 128)
        EXPAND, N, W = (2, 16, 4)
        DIN = EXPAND * DM

        def _ssm_fft_conv(x, log_dt, A_re, A_im, C_re, C_im, D_skip):
            Ll = x.shape[-1]
            dt = jnp.exp(log_dt)[:, None]
            A = A_re + 1j * A_im
            C = C_re + 1j * C_im
            dtA = dt * A
            dB = (jnp.exp(dtA) - 1.0) / A
            ell = jnp.arange(Ll, dtype=jnp.float32)
            vand = jnp.exp(dtA[:, :, None] * ell)
            K = 2.0 * jnp.real(jnp.einsum('hn,hnl->hl', C * dB, vand))
            n_fft = 2 * Ll
            y = jnp.fft.irfft(jnp.fft.rfft(x, n=n_fft) * jnp.fft.rfft(K, n=n_fft)[None], n=n_fft)[..., :Ll]
            return y + D_skip[None, :, None] * x
        key = jax.random.key(seed)
        ks = jax.random.split(key, 9)
        hidden_states = jax.random.normal(ks[0], (B, L, DM), dtype=jnp.float32)
        in_proj_w = jax.random.normal(ks[1], (2 * DIN, DM), dtype=jnp.float32) * 0.02
        conv_w = jax.random.normal(ks[2], (DIN, W), dtype=jnp.float32) * 0.2
        conv_b = jnp.zeros((DIN,), dtype=jnp.float32)
        out_proj_w = jax.random.normal(ks[3], (DM, DIN), dtype=jnp.float32) * 0.02
        log_dt = jax.random.uniform(ks[4], (DIN,), dtype=jnp.float32, minval=jnp.log(0.001), maxval=jnp.log(0.1))
        A_re = -0.5 * jnp.ones((DIN, N), dtype=jnp.float32)
        A_im = jnp.broadcast_to(jnp.pi * jnp.arange(N, dtype=jnp.float32), (DIN, N)).copy()
        C_re = jax.random.normal(ks[5], (DIN, N), dtype=jnp.float32) * 0.5
        C_im = jax.random.normal(ks[6], (DIN, N), dtype=jnp.float32) * 0.5
        D_skip = jax.random.normal(ks[7], (DIN,), dtype=jnp.float32)
        return {'hidden_states': hidden_states, 'in_proj_w': in_proj_w, 'conv_w': conv_w, 'conv_b': conv_b, 'out_proj_w': out_proj_w, 'log_dt': log_dt, 'A_re': A_re, 'A_im': A_im, 'C_re': C_re, 'C_im': C_im, 'D_skip': D_skip}
    _L0_attn_in = _L0_attn_setup()

    def _L0_ffn_setup():
        import jax, jax.numpy as jnp
        import numpy as np
        B, S, D = (4, 64, 128)
        E, K, H = (64, 8, 32)
        ES, HS = (2, 256)
        key = jax.random.key(seed)
        ks = jax.random.split(key, 8)
        scale = 0.02
        rn = lambda k, shape, s: jax.random.normal(k, shape, jnp.float32) * s
        return {'x': rn(ks[0], (B, S, D), 1.0), 'router_w': rn(ks[1], (D, E), scale), 'router_b': jnp.zeros((E,), jnp.float32), 'w1': rn(ks[2], (E, D, H), scale), 'b1': jnp.zeros((E, H), jnp.float32), 'w2': rn(ks[3], (E, H, D), scale), 'b2': jnp.zeros((E, D), jnp.float32), 'sw1': rn(ks[4], (ES, D, HS), scale), 'sb1': jnp.zeros((ES, HS), jnp.float32), 'sw2': rn(ks[5], (ES, HS, D), scale), 'sb2': jnp.zeros((ES, D), jnp.float32)}
    _L0_ffn_in = _L0_ffn_setup()

    def _L1_attn_setup():
        import jax, jax.numpy as jnp
        import numpy as np
        D = 128
        H = 16
        KVH = 4
        HD = D // H
        LAT = 32
        WIN = 32
        B, S = (1, 256)
        BASE_G, BASE_L = (1000000.0, 10000.0)
        EPS = 1e-06

        def rmsnorm(x, w):
            return x * jax.lax.rsqrt(jnp.mean(x * x, axis=-1, keepdims=True) + EPS) * w

        def qk_norm(x):
            return x * jax.lax.rsqrt(jnp.mean(x * x, axis=-1, keepdims=True) + EPS)

        def rope(x, base):
            s, hd = (x.shape[-2], x.shape[-1])
            inv_freq = 1.0 / base ** (jnp.arange(0, hd, 2, dtype=jnp.float32) / hd)
            freqs = jnp.arange(s, dtype=jnp.float32)[:, None] * inv_freq[None, :]
            cos, sin = (jnp.cos(freqs), jnp.sin(freqs))
            xe, xo = (x[..., ::2], x[..., 1::2])
            out = jnp.stack([xe * cos - xo * sin, xe * sin + xo * cos], axis=-1)
            return out.reshape(x.shape)

        def split_heads(x, n_heads):
            b, s, _ = x.shape
            return x.reshape(b, s, n_heads, HD).transpose(0, 2, 1, 3)

        def repeat_kv(x):
            return jnp.repeat(x, H // KVH, axis=1)

        def sdpa(q, k, v, mask):
            scores = jnp.einsum('bhqd,bhkd->bhqk', q, k) / np.sqrt(HD).astype(np.float32)
            scores = jnp.where(mask, scores, jnp.float32(-1e+30))
            probs = jax.nn.softmax(scores, axis=-1)
            return jnp.einsum('bhqk,bhkd->bhqd', probs, v)

        def merge_heads(x):
            b, h, s, hd = x.shape
            return x.transpose(0, 2, 1, 3).reshape(b, s, h * hd)

        def global_latent_attn(x, wq, w_kv_down, w_k_up, w_v_up, wo):
            q = split_heads(x @ wq, H)
            latent = x @ w_kv_down
            k = split_heads(latent @ w_k_up, KVH)
            v = split_heads(latent @ w_v_up, KVH)
            q, k = (rope(q, BASE_G), rope(k, BASE_G))
            q, k = (qk_norm(q), qk_norm(k))
            k, v = (repeat_kv(k), repeat_kv(v))
            i = jnp.arange(x.shape[1])
            causal = i[:, None] >= i[None, :]
            return merge_heads(sdpa(q, k, v, causal)) @ wo

        def local_gqa_attn(x, wq, wk, wv, wo):
            q = split_heads(x @ wq, H)
            k = split_heads(x @ wk, KVH)
            v = split_heads(x @ wv, KVH)
            q, k = (rope(q, BASE_L), rope(k, BASE_L))
            q, k = (qk_norm(q), qk_norm(k))
            k, v = (repeat_kv(k), repeat_kv(v))
            i = jnp.arange(x.shape[1])
            diff = i[:, None] - i[None, :]
            mask = (diff >= 0) & (diff < WIN)
            return merge_heads(sdpa(q, k, v, mask)) @ wo
        key = jax.random.key(seed)
        ks = jax.random.split(key, 12)
        std = 0.02
        return {'hidden': jax.random.normal(ks[0], (B, S, D), dtype=jnp.float32), 'norm1_w': jnp.ones((D,), jnp.float32), 'norm2_w': jnp.ones((D,), jnp.float32), 'g_wq': jax.random.normal(ks[1], (D, H * HD), jnp.float32) * std, 'g_kv_down': jax.random.normal(ks[2], (D, LAT), jnp.float32) * std, 'g_k_up': jax.random.normal(ks[3], (LAT, KVH * HD), jnp.float32) * std, 'g_v_up': jax.random.normal(ks[4], (LAT, KVH * HD), jnp.float32) * std, 'g_wo': jax.random.normal(ks[5], (D, D), jnp.float32) * std, 'l_wq': jax.random.normal(ks[6], (D, H * HD), jnp.float32) * std, 'l_wk': jax.random.normal(ks[7], (D, KVH * HD), jnp.float32) * std, 'l_wv': jax.random.normal(ks[8], (D, KVH * HD), jnp.float32) * std, 'l_wo': jax.random.normal(ks[9], (D, D), jnp.float32) * std}
    _L1_attn_in = _L1_attn_setup()

    def _L1_ffn_setup():
        import jax, jax.numpy as jnp
        import numpy as np
        B, S, H, FFN, E = (2, 256, 128, 512, 8)
        key = jax.random.key(seed)
        k0, k1, k2, k3 = jax.random.split(key, 4)
        return {'hidden_states': jax.random.normal(k0, (B, S, H), dtype=jnp.float32), 'Wr': jax.random.normal(k1, (H, E), dtype=jnp.float32) * 0.02, 'br': jnp.zeros((E,), dtype=jnp.float32), 'W1': jax.random.normal(k2, (E, H, FFN), dtype=jnp.float32) * 0.02, 'W2': jax.random.normal(k3, (E, FFN, H), dtype=jnp.float32) * 0.02}
    _L1_ffn_in = _L1_ffn_setup()
    _d = {'L0_attn_hidden_states': _L0_attn_in['hidden_states'], 'L0_attn_in_proj_w': _L0_attn_in['in_proj_w'], 'L0_attn_conv_w': _L0_attn_in['conv_w'], 'L0_attn_conv_b': _L0_attn_in['conv_b'], 'L0_attn_out_proj_w': _L0_attn_in['out_proj_w'], 'L0_attn_log_dt': _L0_attn_in['log_dt'], 'L0_attn_A_re': _L0_attn_in['A_re'], 'L0_attn_A_im': _L0_attn_in['A_im'], 'L0_attn_C_re': _L0_attn_in['C_re'], 'L0_attn_C_im': _L0_attn_in['C_im'], 'L0_attn_D_skip': _L0_attn_in['D_skip'], 'L0_ffn_router_w': _L0_ffn_in['router_w'], 'L0_ffn_router_b': _L0_ffn_in['router_b'], 'L0_ffn_w1': _L0_ffn_in['w1'], 'L0_ffn_b1': _L0_ffn_in['b1'], 'L0_ffn_w2': _L0_ffn_in['w2'], 'L0_ffn_b2': _L0_ffn_in['b2'], 'L0_ffn_sw1': _L0_ffn_in['sw1'], 'L0_ffn_sb1': _L0_ffn_in['sb1'], 'L0_ffn_sw2': _L0_ffn_in['sw2'], 'L0_ffn_sb2': _L0_ffn_in['sb2'], 'L1_attn_norm1_w': _L1_attn_in['norm1_w'], 'L1_attn_norm2_w': _L1_attn_in['norm2_w'], 'L1_attn_g_wq': _L1_attn_in['g_wq'], 'L1_attn_g_kv_down': _L1_attn_in['g_kv_down'], 'L1_attn_g_k_up': _L1_attn_in['g_k_up'], 'L1_attn_g_v_up': _L1_attn_in['g_v_up'], 'L1_attn_g_wo': _L1_attn_in['g_wo'], 'L1_attn_l_wq': _L1_attn_in['l_wq'], 'L1_attn_l_wk': _L1_attn_in['l_wk'], 'L1_attn_l_wv': _L1_attn_in['l_wv'], 'L1_attn_l_wo': _L1_attn_in['l_wo'], 'L1_ffn_Wr': _L1_ffn_in['Wr'], 'L1_ffn_br': _L1_ffn_in['br'], 'L1_ffn_W1': _L1_ffn_in['W1'], 'L1_ffn_W2': _L1_ffn_in['W2']}
    _x0 = _d['L0_attn_hidden_states']
    _d['L0_attn_hidden_states'] = jax.random.normal(jax.random.fold_in(jax.random.key(seed), 1), (2, 1024, 128), dtype=_x0.dtype)
    del _x0
    return _d

def reference(L0_attn_hidden_states, L0_attn_in_proj_w, L0_attn_conv_w, L0_attn_conv_b, L0_attn_out_proj_w, L0_attn_log_dt, L0_attn_A_re, L0_attn_A_im, L0_attn_C_re, L0_attn_C_im, L0_attn_D_skip, L0_ffn_router_w, L0_ffn_router_b, L0_ffn_w1, L0_ffn_b1, L0_ffn_w2, L0_ffn_b2, L0_ffn_sw1, L0_ffn_sb1, L0_ffn_sw2, L0_ffn_sb2, L1_attn_norm1_w, L1_attn_norm2_w, L1_attn_g_wq, L1_attn_g_kv_down, L1_attn_g_k_up, L1_attn_g_v_up, L1_attn_g_wo, L1_attn_l_wq, L1_attn_l_wk, L1_attn_l_wv, L1_attn_l_wo, L1_ffn_Wr, L1_ffn_br, L1_ffn_W1, L1_ffn_W2):

    def _L0_attn_ref(hidden_states, in_proj_w, conv_w, conv_b, out_proj_w, log_dt, A_re, A_im, C_re, C_im, D_skip):
        import jax, jax.numpy as jnp
        import numpy as np
        B, L, DM = (4, 256, 128)
        EXPAND, N, W = (2, 16, 4)
        DIN = EXPAND * DM

        def _ssm_fft_conv(x, log_dt, A_re, A_im, C_re, C_im, D_skip):
            Ll = x.shape[-1]
            dt = jnp.exp(log_dt)[:, None]
            A = A_re + 1j * A_im
            C = C_re + 1j * C_im
            dtA = dt * A
            dB = (jnp.exp(dtA) - 1.0) / A
            ell = jnp.arange(Ll, dtype=jnp.float32)
            vand = jnp.exp(dtA[:, :, None] * ell)
            K = 2.0 * jnp.real(jnp.einsum('hn,hnl->hl', C * dB, vand))
            n_fft = 2 * Ll
            y = jnp.fft.irfft(jnp.fft.rfft(x, n=n_fft) * jnp.fft.rfft(K, n=n_fft)[None], n=n_fft)[..., :Ll]
            return y + D_skip[None, :, None] * x
        b, l, d = hidden_states.shape
        xz = jnp.einsum('bld,ed->bel', hidden_states, in_proj_w)
        x, z = jnp.split(xz, 2, axis=1)
        xp = jnp.pad(x, ((0, 0), (0, 0), (W - 1, 0)))
        x = jax.lax.conv_general_dilated(xp, conv_w[:, None, :], window_strides=(1,), padding='VALID', dimension_numbers=('NCH', 'OIH', 'NCH'), feature_group_count=x.shape[1])
        x = jax.nn.silu(x + conv_b[None, :, None])
        x = _ssm_fft_conv(x, log_dt, A_re, A_im, C_re, C_im, D_skip)
        x = x * jax.nn.silu(z)
        out = jnp.einsum('bel,de->bld', x, out_proj_w)
        return out

    def _L0_ffn_ref(x, router_w, router_b, w1, b1, w2, b2, sw1, sb1, sw2, sb2):
        import jax, jax.numpy as jnp
        import numpy as np
        B, S, D = (4, 64, 128)
        E, K, H = (64, 8, 32)
        ES, HS = (2, 256)
        b_, s_, d_ = x.shape
        xf = x.reshape(-1, d_)
        probs = jax.nn.softmax(xf @ router_w + router_b, axis=-1)
        tw, ti = jax.lax.top_k(probs, K)
        tw = tw / jnp.sum(tw, axis=-1, keepdims=True)

        def body(acc, p):
            W1, B1, W2, B2, e = p
            h = jax.nn.silu(xf @ W1 + B1) @ W2 + B2
            cw = jnp.sum(jnp.where(ti == e, tw, 0.0), axis=-1)
            return (acc + cw[:, None] * h, None)
        routed, _ = jax.lax.scan(body, jnp.zeros_like(xf), (w1, b1, w2, b2, jnp.arange(w1.shape[0])))

        def shared_mlp(W1, B1, W2, B2):
            return jax.nn.silu(xf @ W1 + B1) @ W2 + B2
        shared = jnp.sum(jax.vmap(shared_mlp)(sw1, sb1, sw2, sb2), axis=0)
        return (routed + shared).reshape(b_, s_, d_)

    def _L1_attn_ref(hidden, norm1_w, norm2_w, g_wq, g_kv_down, g_k_up, g_v_up, g_wo, l_wq, l_wk, l_wv, l_wo):
        import jax, jax.numpy as jnp
        import numpy as np
        D = 128
        H = 16
        KVH = 4
        HD = D // H
        LAT = 32
        WIN = 32
        B, S = (1, 256)
        BASE_G, BASE_L = (1000000.0, 10000.0)
        EPS = 1e-06

        def rmsnorm(x, w):
            return x * jax.lax.rsqrt(jnp.mean(x * x, axis=-1, keepdims=True) + EPS) * w

        def qk_norm(x):
            return x * jax.lax.rsqrt(jnp.mean(x * x, axis=-1, keepdims=True) + EPS)

        def rope(x, base):
            s, hd = (x.shape[-2], x.shape[-1])
            inv_freq = 1.0 / base ** (jnp.arange(0, hd, 2, dtype=jnp.float32) / hd)
            freqs = jnp.arange(s, dtype=jnp.float32)[:, None] * inv_freq[None, :]
            cos, sin = (jnp.cos(freqs), jnp.sin(freqs))
            xe, xo = (x[..., ::2], x[..., 1::2])
            out = jnp.stack([xe * cos - xo * sin, xe * sin + xo * cos], axis=-1)
            return out.reshape(x.shape)

        def split_heads(x, n_heads):
            b, s, _ = x.shape
            return x.reshape(b, s, n_heads, HD).transpose(0, 2, 1, 3)

        def repeat_kv(x):
            return jnp.repeat(x, H // KVH, axis=1)

        def sdpa(q, k, v, mask):
            scores = jnp.einsum('bhqd,bhkd->bhqk', q, k) / np.sqrt(HD).astype(np.float32)
            scores = jnp.where(mask, scores, jnp.float32(-1e+30))
            probs = jax.nn.softmax(scores, axis=-1)
            return jnp.einsum('bhqk,bhkd->bhqd', probs, v)

        def merge_heads(x):
            b, h, s, hd = x.shape
            return x.transpose(0, 2, 1, 3).reshape(b, s, h * hd)

        def global_latent_attn(x, wq, w_kv_down, w_k_up, w_v_up, wo):
            q = split_heads(x @ wq, H)
            latent = x @ w_kv_down
            k = split_heads(latent @ w_k_up, KVH)
            v = split_heads(latent @ w_v_up, KVH)
            q, k = (rope(q, BASE_G), rope(k, BASE_G))
            q, k = (qk_norm(q), qk_norm(k))
            k, v = (repeat_kv(k), repeat_kv(v))
            i = jnp.arange(x.shape[1])
            causal = i[:, None] >= i[None, :]
            return merge_heads(sdpa(q, k, v, causal)) @ wo

        def local_gqa_attn(x, wq, wk, wv, wo):
            q = split_heads(x @ wq, H)
            k = split_heads(x @ wk, KVH)
            v = split_heads(x @ wv, KVH)
            q, k = (rope(q, BASE_L), rope(k, BASE_L))
            q, k = (qk_norm(q), qk_norm(k))
            k, v = (repeat_kv(k), repeat_kv(v))
            i = jnp.arange(x.shape[1])
            diff = i[:, None] - i[None, :]
            mask = (diff >= 0) & (diff < WIN)
            return merge_heads(sdpa(q, k, v, mask)) @ wo
        x = hidden
        x = x + global_latent_attn(rmsnorm(x, norm1_w), g_wq, g_kv_down, g_k_up, g_v_up, g_wo)
        x = x + local_gqa_attn(rmsnorm(x, norm2_w), l_wq, l_wk, l_wv, l_wo)
        return x

    def _L1_ffn_ref(hidden_states, Wr, br, W1, W2):
        import jax, jax.numpy as jnp
        import numpy as np
        B, S, H, FFN, E = (2, 256, 128, 512, 8)
        b, s, h = hidden_states.shape
        x = hidden_states.reshape(-1, h)
        route = jax.nn.sigmoid(x @ Wr + br)
        max_prob = jnp.max(route, axis=1, keepdims=True)
        max_ind = jnp.argmax(route, axis=1)
        out = jnp.zeros_like(x)
        n_experts = Wr.shape[1]
        for e in range(n_experts):
            mask = (max_ind == e)[:, None].astype(x.dtype)
            y = jax.nn.gelu(x @ W1[e], approximate=False) @ W2[e]
            out = out + mask * y
        out = out * max_prob
        return out.reshape(b, s, h)
    x = L0_attn_hidden_states
    x = _layernorm(x + _L0_attn_ref(x, L0_attn_in_proj_w, L0_attn_conv_w, L0_attn_conv_b, L0_attn_out_proj_w, L0_attn_log_dt, L0_attn_A_re, L0_attn_A_im, L0_attn_C_re, L0_attn_C_im, L0_attn_D_skip), axis=-1)
    x = _layernorm(x + _L0_ffn_ref(x, L0_ffn_router_w, L0_ffn_router_b, L0_ffn_w1, L0_ffn_b1, L0_ffn_w2, L0_ffn_b2, L0_ffn_sw1, L0_ffn_sb1, L0_ffn_sw2, L0_ffn_sb2), axis=-1)
    x = _layernorm(x + _L1_attn_ref(x, L1_attn_norm1_w, L1_attn_norm2_w, L1_attn_g_wq, L1_attn_g_kv_down, L1_attn_g_k_up, L1_attn_g_v_up, L1_attn_g_wo, L1_attn_l_wq, L1_attn_l_wk, L1_attn_l_wv, L1_attn_l_wo), axis=-1)
    x = _layernorm(x + _L1_ffn_ref(x, L1_ffn_Wr, L1_ffn_br, L1_ffn_W1, L1_ffn_W2), axis=-1)
    return x

_drawn_inputs = setup_inputs


def setup_inputs(seed=0):
    import zlib

    import numpy as np

    out = dict(_drawn_inputs(seed))
    spreads = {'L0_attn_conv_b': (0.0, 0.8),
     'L0_attn_A_re': (-0.5, 0.6),
     'L0_ffn_router_b': (0.0, 0.322),
     'L0_ffn_b1': (0.0, 0.8),
     'L0_ffn_b2': (0.0, 0.1),
     'L0_ffn_sb1': (0.0, 0.349),
     'L0_ffn_sb2': (0.0, 0.1),
     'L1_attn_norm1_w': (1.0, 0.6),
     'L1_attn_norm2_w': (1.0, 0.6),
     'L1_ffn_br': (0.0, 1.039)}
    factors = {'L0_attn_in_proj_w': 8.0,
     'L0_attn_conv_w': 8.0,
     'L0_attn_out_proj_w': 8.0,
     'L0_attn_log_dt': 64.0,
     'L0_attn_A_im': 64.0,
     'L0_attn_C_re': 64.0,
     'L0_attn_C_im': 64.0,
     'L0_attn_D_skip': 8.0,
     'L0_ffn_w1': 8.0,
     'L0_ffn_w2': 8.0,
     'L1_attn_g_wq': 8.0,
     'L1_attn_g_kv_down': 8.0,
     'L1_attn_g_k_up': 8.0,
     'L1_attn_g_v_up': 8.0,
     'L1_attn_g_wo': 8.0,
     'L1_attn_l_wq': 8.0,
     'L1_attn_l_wk': 8.0,
     'L1_attn_l_wv': 6.581,
     'L1_attn_l_wo': 6.571}
    for name, (base, spread) in spreads.items():
        noise = np.random.default_rng([zlib.crc32(name.encode()), seed]).standard_normal(out[name].shape)
        drawn = base * np.exp(spread * noise) if base else spread * noise
        out[name] = jnp.asarray(drawn.astype(out[name].dtype))
    for name, factor in factors.items():
        out[name] = (out[name] * factor).astype(out[name].dtype)
    return out
```

```python
import numpy as np
from contextlib import ExitStack

import concourse.bass as bass
from concourse import mybir

B, L, DM = 2, 1024, 128
T = B * L
CH = 512
NCH = T // CH
DIN, NST = 256, 16
MH = DIN // 128
Q = 32
NJ = L // Q
GC = 8
NG = MH * 32 // GC
E1, H1, ES, HS1 = 64, 32, 2, 256
KB1 = E1 * H1 // 128
KBS = ES * HS1 // 128
E2, FF2 = 8, 512
H, KVH, HD, LAT, WIN = 16, 4, 8, 32, 32
QL = 128 - WIN
NL = -(-L // QL)
LP = WIN + NL * QL
NQT = L // 128
NT = T // 128
EPS_LN, EPS_RMS = 1e-5, 1e-6
MAGIC = 12582912.0
TWO_PI = 6.283185
C1, C2 = 6.28125, 0.0019350051879882812
C3 = 2 * np.pi - C1 - C2
LOG_EXP = "natural_log_exp_and_others"
LOG2E, LN2H, LN2L = 1.4426950408889634, 0.693359375, -2.12194440e-4

K_Q31, K_MRE, K_MIM, K_LROW, K_JROW, K_SEL = 0, 1, 2, 3, 36, 68
K_MEAN, K_HEAD, K_DEN, K_ID, K_CAUS, K_BAND, K_N = 72, 200, 328, 456, 584, 712, 808


def constants():
    c = np.zeros((128, K_N), np.float32)
    p = np.arange(128)
    c[:, K_Q31] = Q - 1 - p % 32
    c[:, K_MRE] = p % 32 < NST
    c[:, K_MIM] = p % 32 >= NST
    c[:, K_LROW:K_LROW + Q + 1] = np.arange(Q + 1)
    c[:, K_JROW:K_JROW + NJ] = np.arange(NJ) * Q
    for g in range(4):
        c[32 * g:32 * g + NST, K_SEL + g] = 1.0
    c[:, K_MEAN:K_MEAN + 128] = 1.0 / 128
    c[:, K_HEAD:K_HEAD + 128] = (p[:, None] // HD == p[None] // HD) / HD
    c[:, K_DEN:K_DEN + 128] = p[:, None] == p[None] // 32 * 32 + HD
    c[:, K_ID:K_ID + 128] = np.eye(128)
    c[:, K_CAUS:K_CAUS + 128] = p[:, None] <= p[None]
    diff = np.arange(QL)[None] + WIN - p[:, None]
    c[:, K_BAND:K_BAND + QL] = (diff >= 0) & (diff < WIN)
    rope = np.zeros((2, 2, 128, L), np.float32)
    for n, base in enumerate((1000000.0, 10000.0)):
        inv = 1.0 / np.float32(base) ** (np.arange(0, HD, 2, dtype=np.float32) / HD)
        ang = np.arange(L, dtype=np.float32)[:, None] * inv[None].astype(np.float32)
        cos, sin = np.cos(ang).T, np.sin(ang).T
        d = p % HD
        rope[n, 0] = cos[d // 2]
        rope[n, 1] = sin[d // 2] * np.where(d % 2 == 0, -1.0, 1.0)[:, None]
    sel1 = np.zeros((2, E1, KB1, 128), np.float32)
    for kb in range(KB1):
        sel1[:, 4 * kb + p // 32, kb, p] = 1.0
    sel2 = np.zeros((2 * E2, E2 + 1, 128), np.float32)
    for e in range(E2):
        sel2[e, e, :] = 1.0
    sel2[E2:, E2, :] = 1.0
    first = np.tile(np.arange(E2, 0, -1, dtype=np.float32), (128, NT))
    kept = rope[:, :, :32].reshape(2, 2, 32, 2, CH)
    kept = np.concatenate([kept[:, :, :, n % 2] for n in range(NCH)], 2)
    rope = np.concatenate([rope, kept], 3).transpose(0, 2, 1, 3)
    return {"consts": c, "rope": rope, "sel1": sel1.reshape(128, -1),
            "sel2": sel2.reshape(2 * E2, -1), "first": first}


def lay_out(x):
    a = {}
    a["h_t"] = x["L0_attn_hidden_states"].reshape(T, DM).T
    a["w_in"] = x["L0_attn_in_proj_w"].T
    cw = x["L0_attn_conv_w"].reshape(MH, 128, 4)
    cb = x["L0_attn_conv_b"].reshape(MH, 128, 1)
    ds = x["L0_attn_D_skip"].reshape(MH, 128, 1)
    a["ssm_col"] = np.concatenate([cw, cb, ds], 2).transpose(1, 0, 2).reshape(128, -1)
    a["w_out"] = x["L0_attn_out_proj_w"].T.reshape(MH, 128, DM).transpose(1, 0, 2).reshape(128, -1)
    names = ("L0_attn_A_re", "L0_attn_A_im", "L0_attn_C_re", "L0_attn_C_im")
    by_state = []
    for n in names:
        v = x[n].reshape(MH, 4, 32, NST).transpose(1, 3, 0, 2)
        by_state.append(np.broadcast_to(v[:, None], (4, 2, NST, MH, 32)).reshape(128, 64))
    ld = x["L0_attn_log_dt"].reshape(MH, 4, 32).transpose(1, 0, 2)
    ld = np.broadcast_to(ld[:, None], (4, 32, MH, 32)).reshape(128, 64)
    a["par_state"] = np.concatenate(by_state + [ld], 1)
    by_step = []
    for n in names[:2]:
        v = x[n].reshape(MH, 4, 32, NST).transpose(1, 0, 2, 3)
        by_step.append(np.broadcast_to(v[:, None], (4, 32, MH, 32, NST)).reshape(128, -1))
    a["par_step"] = np.concatenate(by_step, 1)
    a["r1_w"] = x["L0_ffn_router_w"]
    a["r1_b"] = np.broadcast_to(x["L0_ffn_router_b"], (128, E1))
    a["m1_w1"] = np.concatenate([x["L0_ffn_w1"].transpose(1, 0, 2).reshape(DM, -1),
                                 x["L0_ffn_sw1"].transpose(1, 0, 2).reshape(DM, -1)], 1)
    a["m1_b1"] = np.concatenate([x["L0_ffn_b1"].reshape(KB1, 128), x["L0_ffn_sb1"].reshape(KBS, 128)]).T
    w2 = np.concatenate([x["L0_ffn_w2"].reshape(KB1, 128, DM), x["L0_ffn_sw2"].reshape(KBS, 128, DM)])
    a["m1_w2"] = w2.transpose(1, 0, 2).reshape(128, -1)
    a["m1_b2"] = np.concatenate([x["L0_ffn_b2"], x["L0_ffn_sb2"]])
    swap = np.arange(128) ^ 1
    a["norm_w"] = np.stack([x["L1_attn_norm1_w"], x["L1_attn_norm2_w"]], 1)
    for n in "gl":
        wq = x[f"L1_attn_{n}_wq"]
        a[f"{n}_q"] = np.concatenate([wq, wq[:, swap]], 1)
        wo = np.zeros((4, 32, 4, DM), np.float32)
        wo[:, :HD] = x[f"L1_attn_{n}_wo"].reshape(KVH, 4, HD, DM).transpose(0, 2, 1, 3)
        a[f"{n}_o"] = wo.reshape(128, -1)
    up, wk = x["L1_attn_g_k_up"], x["L1_attn_l_wk"]
    a["g_down"] = x["L1_attn_g_kv_down"]
    a["g_kv"] = np.concatenate([up, up[:, swap[:32]], x["L1_attn_g_v_up"]], 1)
    a["l_kv"] = np.concatenate([wk, wk[:, swap[:32]], x["L1_attn_l_wv"]], 1)
    a["r2_w"] = x["L1_ffn_Wr"]
    a["r2_b"] = np.tile(x["L1_ffn_br"], (128, 1))
    a["m2_w1"] = x["L1_ffn_W1"].transpose(1, 0, 2).reshape(DM, -1)
    a["m2_w2"] = x["L1_ffn_W2"].reshape(E2 * 4, 128, DM).transpose(1, 0, 2).reshape(128, -1)
    a.update(constants())
    return {k: np.ascontiguousarray(v) for k, v in a.items()}


def spread(ap, axis, n):
    dims = [list(d) for d in ap.ap]
    return bass.AP(tensor=ap.tensor, offset=ap.offset, ap=dims[:axis] + [[0, n]] + dims[axis:])


def build(nc, dram, out, stages=99):
    f32, bf16, i32 = mybir.dt.float32, mybir.dt.bfloat16, mybir.dt.int32
    ALU, ACT, AX = mybir.AluOpType, mybir.ActivationFunctionType, mybir.AxisListType
    ADD, SUB, MUL = ALU.add, ALU.subtract, ALU.mult
    stack = ExitStack()

    def sem(name):
        return stack.enter_context(nc.semaphore(name))

    def sb(name, shape, dt=f32):
        return stack.enter_context(nc.sbuf_tensor(name, shape, dt))

    with stack:
        cst = sb("cst", [128, K_N])
        X = sb("X", [128, T])
        xn = sb("xn", [128, B, LP])
        work = sb("work", [128, 4 * T + 256])
        dev, sq, y0 = (work[:, n * T:(n + 1) * T] for n in range(3))
        arena = sb("arena", [128, 33000])
        wts = {name: sb("w_" + name, list(dram[name].shape)) for name in dram
               if name.split("_")[0] in ("r1", "m1", "norm", "g", "l", "r2", "sel2", "first")
               and name != "m1_w2"}
        two = [stack.enter_context(nc.psum_tensor(f"banks{i}", [128, 2, CH], f32)) for i in range(4)]
        bank = [two[i // 2][:, i % 2, :] for i in range(8)]

        def place(at, *shape, dt=f32):
            n = int(np.prod(shape))
            words = n // (2 if dt == bf16 else 1)
            assert at + words <= 33000, (at, shape)
            v = arena[:, at:at + words]
            if dt != f32:
                v = v.bitcast(dt)
            names = "abcd"[:len(shape)]
            return v.rearrange(f"p ({' '.join(names)}) -> p {' '.join(names)}",
                               **{k: s for k, s in zip(names, shape)})

        def const(at, n, rows=128):
            return cst[0:rows, at:at + n]

        chain = {}

        def link(eng, ins):
            s = chain[eng.engine]
            s[1] += 1
            ins.then_inc(s[0], 1)
            eng.wait_ge(s[0], s[1])

        for e, n in ((nc.vector, "vector_step"), (nc.scalar, "scalar_step"), (nc.gpsimd, "pool_step")):
            chain[e.engine] = [sem(n), 0]

        consts_in, first_in, par_in, wout_in = sem("consts_in"), sem("first_in"), sem("par_in"), sem("wout_in")
        m1_in, attn_in, m2_in = sem("m1_in"), sem("attn_in"), sem("m2_in")

        resid_ready = sem("resid_ready")
        mean_ready = sem("mean_ready")
        dev_ready = sem("dev_ready")
        square_ready = sem("square_ready")
        var_ready = sem("var_ready")
        guess_ready = sem("guess_ready")
        normed = sem("normed")

        def tok(c):
            return slice(c * CH, (c + 1) * CH)

        def xn_tok(c):
            return xn[:, c // 2, WIN + c % 2 * CH:WIN + (c % 2 + 1) * CH]

        def pe_norm(pe, k, rms):
            if not rms:
                for c in range(NCH):
                    pe.wait_ge(resid_ready, NCH * resid_index[k] + c + 1)
                    pe.matmul(bank[c][:, :], const(K_MEAN, 128), X[:, tok(c)], start=True, stop=True)\
                        .then_inc(mean_ready, 1)
            for c in range(NCH):
                pe.wait_ge(square_ready, NCH * k + c + 1)
                pe.matmul(bank[4 + c][:, :], const(K_MEAN, 128), sq[:, tok(c)], start=True, stop=True)\
                    .then_inc(var_ready, 1)

        def act_norm(act, k, rms):
            for c in range(NCH):
                if rms:
                    if k == 2:
                        act.wait_ge(normed, NCH * k - NCH + c + 1)
                    else:
                        act.wait_ge(resid_ready, NCH * resid_index[k] + c + 1)
                else:
                    act.wait_ge(dev_ready, ln_index[k] * NCH + c + 1)
                act.activation(sq[:, tok(c)], X[:, tok(c)] if rms else dev[:, tok(c)], ACT.Square)\
                    .then_inc(square_ready, 1)
            act.preload_act_table_set(LOG_EXP)
            for c in range(NCH):
                act.wait_ge(var_ready, NCH * k + c + 1)
                link(act, act.activation(y0[:, tok(c)], bank[4 + c][:, :], ACT.Ln,
                                         bias=eps[:, rms:rms + 1]))
                act.activation(y0[:, tok(c)], y0[:, tok(c)], ACT.Exp, scale=-0.5).then_inc(guess_ready, 1)

        def rsqrt_step(dve, guess, square, tmp, eps_value):
            link(dve, dve.scalar_tensor_tensor(tmp, guess, -0.5, guess, MUL, MUL))
            link(dve, dve.scalar_tensor_tensor(tmp, square, eps_value, tmp, ADD, MUL))
            link(dve, dve.scalar_tensor_tensor(guess, tmp, 1.5, guess, ADD, MUL))

        def dve_norm(dve, k, rms):
            if not rms:
                for c in range(NCH):
                    dve.wait_ge(mean_ready, ln_index[k] * NCH + c + 1)
                    dve.tensor_tensor(dev[:, tok(c)], X[:, tok(c)], bank[c][:, :], SUB).then_inc(dev_ready, 1)
            for c in range(NCH):
                dve.wait_ge(guess_ready, NCH * k + c + 1)
                y = y0[:, tok(c)]
                rsqrt_step(dve, y, bank[4 + c][:, :], sq[:, tok(c)], EPS_RMS if rms else EPS_LN)
                if rms:
                    dve.scalar_tensor_tensor(xn_tok(c), X[:, tok(c)], wts["norm_w"][:, k - 2:k - 1], y, MUL, MUL)\
                        .then_inc(normed, 1)
                else:
                    dve.tensor_tensor(X[:, tok(c)], dev[:, tok(c)], y, MUL).then_inc(normed, 1)

        ln_index = {0: 0, 1: 1, 4: 2, 5: 3}
        resid_index = {0: 0, 1: 1, 3: 2, 4: 3, 5: 4}
        eps = sb("eps", [128, 2])
        eps_set = sem("eps_set")
        sem_out = sem("sem_out")

        h_t = X
        w_in = place(0, 512)
        ssm_col = sb("ssm_col", [128, MH * 6])
        w_out = sb("w_out", [128, MH * 128])
        u = place(0, MH, T)
        at = MH * T
        w_in = place(at, 512); at += 512
        sz = place(at, MH, T); at += MH * T
        xpad = place(at, MH, B, L + 3)
        y_t = place(at, MH, B * NJ, Q); at += MH * B * (L + 3)
        EU = place(at, 64, 32); at += 2048
        EV = place(at, 64, 32); at += 2048
        F1 = place(at, 64, Q + 1); at += 64 * (Q + 1)
        F2 = place(at, 64, Q + 1); at += 64 * (Q + 1)
        TP = place(at, 64, Q); at += 2048
        cos_j = place(at, 64, NJ); at += 2048
        sin_j = place(at, 64, NJ); at += 2048
        rho_g = place(at, GC * B * NJ); at += 512
        pa = place(at, GC * B * NJ); at += 512
        pb_ = place(at, GC * B * NJ); at += 512
        hc = [place(at + 512 * n, GC, B, NJ) for n in range(2)]; at += 1024
        hs = [place(at + 512 * n, GC, B, NJ) for n in range(2)]; at += 1024
        par_state = place(at, 5, 64); at += 320
        small = place(at, 26, 64); at += 26 * 64
        tmpw = [work[:, n * 2112:(n + 1) * 2112] for n in range(4)]
        xq = work[:, 0:MH * T].rearrange("p (m b c) -> p m b c", m=MH, c=32)
        ysb = work[:, MH * T:2 * MH * T].rearrange("p (m b c) -> p m b c", m=MH, c=32)
        par_step = sz
        par_step = place(MH * T + 512 + MH * T, 2, 64, NST)
        kpad = place(0, 64, 64)[0:4]
        kd = nc.dram_tensor("taps", (4, 64, 64), f32, kind="Internal").ap()

        xz_ready, xz_out = sem("xz_ready"), sem("xz_out")
        conv_done, u_ready, xq_ready = sem("conv_done"), sem("u_ready"), sem("xq_ready")
        tables = sem("tables")
        looked_up = sem("looked_up")
        f_ready, e_ready, taps_ready, taps_copied = sem("f_ready"), sem("e_ready"), sem("taps_ready"), sem("taps_copied")
        taps_out, toeplitz_in = sem("taps_out"), sem("toeplitz_in")
        uv_ready, uv_used, state_ready, y_ready, y_copied = (
            sem(n) for n in ("uv_ready", "uv_used", "state_ready", "y_ready", "y_copied"))
        gated, out_ready = sem("gated"), sem("out_ready")
        coef_ready = sem("coef_ready")

        def sp_ssm(sp):
            sp.dma_start(cst[:, :], dram["consts"]).then_inc(consts_in, 16)
            sp.dma_start(par_state, dram["par_state"].rearrange("p (a b) -> p a b", a=5)).then_inc(par_in, 16)
            sp.dma_start(par_step, dram["par_step"].rearrange("p (a b c) -> p a b c", a=2, c=NST)).then_inc(par_in, 16)
            sp.dma_start(h_t[:, :], dram["h_t"]).then_inc(first_in, 16)
            sp.dma_start(w_in, dram["w_in"]).then_inc(first_in, 16)
            sp.dma_start(ssm_col[:, :], dram["ssm_col"]).then_inc(first_in, 16)
            sp.dma_start(w_out[:, :], dram["w_out"]).then_inc(wout_in, 16)
            sp.wait_ge(taps_copied, 5)
            sp.dma_start(kd, kpad[:, :, :]).then_inc(taps_out, 16)
            sp.wait_ge(taps_out, 16)
            for q in range(Q):
                sp.dma_start(TP[q::Q], kd[:, :, Q - 1 - q:2 * Q - 1 - q]).then_inc(toeplitz_in, 16)

        def pe_ssm(pe):
            pe.wait_ge(first_in, 48)
            for m in range(2 * MH):
                for c in range(NCH):
                    n = NCH * m + c
                    if n >= 4:
                        pe.wait_ge(xz_out, n - 3)
                    pe.matmul(bank[n % 4][:, :], w_in[:, 128 * m:128 * m + 128], h_t[:, tok(c)],
                              start=True, stop=True).then_inc(xz_ready, 1)
            pe.wait_ge(f_ready, 1)
            for n in range(4):
                pe.matmul(bank[4 + n][0:4, :], const(K_SEL, 4), F1[:, 16 * n:16 * n + 16, 0:Q],
                          start=True, stop=True).then_inc(taps_ready, 1)
            pe.wait_ge(e_ready, 1)
            pe.wait_ge(xz_out, 16)

            def to_states(k):
                m, c0 = k // 4, GC * (k % 4)
                pe.wait_ge(xq_ready, m + 1)
                if k >= 2:
                    pe.wait_ge(uv_used, k - 1)
                for w, b0 in ((EU, 0), (EV, 2)):
                    for c in range(GC):
                        for g in range(4):
                            r = slice(32 * g, 32 * g + 32)
                            ins = pe.matmul(bank[b0 + k % 2][r, 64 * c:64 * c + 64], w[r, 32 * m + c0 + c, :],
                                            xq[r, m, :, c0 + c], start=True, stop=True)
                ins.then_inc(uv_ready, 1)

            def to_outputs(k):
                m, c0 = k // 4, GC * (k % 4)
                pe.wait_ge(state_ready, k + 1)
                if k == 0:
                    pe.wait_ge(toeplitz_in, 16 * Q)
                    pe.wait_ge(taps_copied, 5)
                if k >= 2:
                    pe.wait_ge(y_copied, k - 1)
                for c in range(GC):
                    mc = 32 * m + c0 + c
                    for g in range(4):
                        r = slice(32 * g, 32 * g + 32)
                        o = bank[4 + k % 2][r, 64 * c:64 * c + 64]
                        pe.matmul(o, TP[r, mc, :], xq[r, m, :, c0 + c], start=True, stop=False)
                    for g in range(4):
                        r = slice(32 * g, 32 * g + 32)
                        o = bank[4 + k % 2][r, 64 * c:64 * c + 64].rearrange("p (b j) -> p b j", b=B)[:, :, 1:NJ]
                        pe.matmul(o, F1[r, mc, 1:Q + 1], hc[k % 2][r, c, :, 0:NJ - 1], start=False, stop=False)
                        ins = pe.matmul(o, F2[r, mc, 1:Q + 1], hs[k % 2][r, c, :, 0:NJ - 1], start=False, stop=True)
                ins.then_inc(y_ready, 1)

            to_states(0)
            for k in range(NG):
                if k + 1 < NG:
                    to_states(k + 1)
                to_outputs(k)
            for c in range(NCH):
                pe.wait_ge(gated, NCH * (MH - 1) + c + 1)
                if c == 0:
                    pe.wait_ge(wout_in, 16)
                    pe.wait_ge(y_copied, NG)
                for m in range(MH):
                    ins = pe.matmul(bank[4 + c][:, :], w_out[:, 128 * m:128 * m + 128], sz[:, m, tok(c)],
                                    start=(m == 0), stop=(m == MH - 1))
                ins.then_inc(out_ready, 1)

        def lookup(act, n, dst, src, func, **kw):
            act.wait_ge(tables, n)
            act.activation(dst, src, func, **kw).then_inc(looked_up, 1)

        def act_ssm(act):
            for n in range(2 * MH * NCH):
                m, c = n // NCH, n % NCH
                act.wait_ge(xz_ready, n + 1)
                if m < MH:
                    d = xpad[:, m, c // 2, 3 + c % 2 * CH:3 + (c % 2 + 1) * CH]
                    if n == 0:
                        act.wait_ge(tables, 4)
                    act.activation(d, bank[n % 4][:, :], ACT.Copy).then_inc(xz_out, 1)
                else:
                    act.activation(sz[:, m - MH, tok(c)], bank[n % 4][:, :], ACT.Silu).then_inc(xz_out, 1)

        (dt2, _a, A2, W2, FR2, K2, P2, S2, SN2, SH2, EA, EM1, NR, NI, DBR, DBI, CR, CI, RHO, p1, p2, t1, t2, t3, DT1, LD1) = (
            small[:, i, :] for i in range(26))
        are, aim, cre, cim, ldt = (par_state[:, i, :] for i in range(5))
        mre, mim, q31 = const(K_MRE, 1), const(K_MIM, 1), const(K_Q31, 1)

        def exact_exp(dve, x, ex, em1, tmp, scale_i):
            k, r, p = tmp
            link(dve, dve.tensor_scalar(x, x, -150.0, 88.0, ALU.max, ALU.min))
            link(dve, dve.tensor_scalar(k, x, LOG2E, MAGIC, MUL, ADD))
            link(dve, dve.tensor_scalar(k, k, MAGIC, None, SUB))
            link(dve, dve.scalar_tensor_tensor(r, k, -LN2H, x, MUL, ADD))
            link(dve, dve.scalar_tensor_tensor(r, k, -LN2L, r, MUL, ADD))
            link(dve, dve.tensor_scalar(p, r, 1 / 5040, None, MUL))
            for co in (1 / 720, 1 / 120, 1 / 24, 1 / 6, 0.5, 1.0):
                link(dve, dve.scalar_tensor_tensor(p, p, co, r, ADD, MUL))
            link(dve, dve.tensor_scalar(scale_i, k, -127.0, 127.0, ALU.max, ADD))
            link(dve, dve.tensor_scalar(scale_i, scale_i, 23, None, ALU.logical_shift_left))
            s = scale_i.bitcast(f32)
            link(dve, dve.tensor_tensor(p, p, s, MUL))
            if em1 is not None:
                link(dve, dve.tensor_scalar(r, s, 1.0, None, SUB))
                link(dve, dve.tensor_tensor(em1, p, r, ADD))
            link(dve, dve.tensor_tensor(ex, p, s, ADD))

        def to_turns(dve, f, w, k):
            link(dve, dve.tensor_scalar(k, w, 1 / (2 * np.pi), MAGIC, MUL, ADD))
            link(dve, dve.tensor_scalar(k, k, MAGIC, None, SUB))
            for part in (C1, C2, C3):
                link(dve, dve.scalar_tensor_tensor(w, k, -part, w, MUL, ADD))
            return dve.tensor_scalar(f, w, 1 / (2 * np.pi), None, MUL)

        def wrap(dve, v, k):
            link(dve, dve.tensor_scalar(k, v, MAGIC, MAGIC, ADD, SUB))
            link(dve, dve.tensor_tensor(v, v, k, SUB))

        def dve_tables(dve):
            dve.memset(eps[:, 0:1], EPS_LN).then_inc(eps_set, 1)
            dve.memset(eps[:, 1:2], EPS_RMS).then_inc(eps_set, 1)
            dve.memset(kpad[:, :, :], 0.0).then_inc(taps_copied, 1)
            for side in (slice(0, WIN), slice(WIN + L, LP)):
                dve.memset(xn[:, :, side], 0.0)
            dve.wait_ge(consts_in, 16)
            dve.wait_ge(par_in, 32)
            ei = work[:, 0:64].bitcast(i32)
            tmp = [work[:, 256 + 128 * i:256 + 128 * i + 64] for i in range(3)]
            link(dve, dve.tensor_copy(t1, ldt))
            exact_exp(dve, t1, dt2, None, tmp, ei)
            link(dve, dve.tensor_tensor(A2, dt2, are, MUL))
            link(dve, dve.tensor_tensor(W2, dt2, aim, MUL))
            link(dve, dve.tensor_copy(t1, A2))
            exact_exp(dve, t1, EA, EM1, tmp, ei)
            link(dve, dve.tensor_scalar(t1, A2, float(Q), None, MUL))
            exact_exp(dve, t1, RHO, None, tmp, ei)
            to_turns(dve, FR2, W2, t1).then_inc(tables, 1)
            dve.wait_ge(tables, 1)
            a1, f1, v1, k1 = (w[:, 0:1024].rearrange("p (c n) -> p c n", n=NST) for w in tmpw)
            mag1, s1, h1 = (w[:, 1024:2048].rearrange("p (c n) -> p c n", n=NST) for w in tmpw[:3])
            dtb = spread(dt2, 2, NST)
            link(dve, dve.tensor_tensor(a1, par_step[:, 0], dtb, MUL))
            dve.tensor_tensor(f1, par_step[:, 1], dtb, MUL).then_inc(tables, 1)
            dve.wait_ge(tables, 2)
            link(dve, to_turns(dve, f1, f1, k1))
            link(dve, dve.tensor_scalar(v1, f1, q31, None, MUL))
            link(dve, dve.tensor_scalar(k1, v1, MAGIC, MAGIC, ADD, SUB))
            dve.tensor_tensor(v1, v1, k1, SUB).then_inc(tables, 1)
            dve.memset(xpad[:, :, :, 0:3], 0.0).then_inc(tables, 1)
            dve.wait_ge(tables, 4)
            dve.wait_ge(looked_up, 2)
            link(dve, dve.scalar_tensor_tensor(t1, SH2, -2.0, SH2, MUL, MUL))
            link(dve, dve.tensor_tensor(t1, t1, EA, MUL))
            link(dve, dve.tensor_tensor(NR, t1, EM1, ADD))
            link(dve, dve.tensor_tensor(NI, EA, SN2, MUL))
            link(dve, dve.tensor_tensor(t1, are, are, MUL))
            link(dve, dve.tensor_tensor(t2, aim, aim, MUL))
            link(dve, dve.tensor_tensor(t1, t1, t2, ADD))
            link(dve, dve.reciprocal(t3, t1))

            def cmul(re, im, ar, ai, br, bi, conj):
                link(dve, dve.tensor_tensor(t1, ar, br, MUL))
                link(dve, dve.tensor_tensor(t2, ai, bi, MUL))
                link(dve, dve.tensor_tensor(re, t1, t2, ADD if conj else SUB))
                link(dve, dve.tensor_tensor(t1, ai, br, MUL))
                link(dve, dve.tensor_tensor(t2, ar, bi, MUL))
                link(dve, dve.tensor_tensor(im, t1, t2, SUB if conj else ADD))

            cmul(DBR, DBI, NR, NI, are, aim, True)
            link(dve, dve.tensor_tensor(DBR, DBR, t3, MUL))
            link(dve, dve.tensor_tensor(DBI, DBI, t3, MUL))
            cmul(CR, CI, DBR, DBI, cre, cim, False)
            link(dve, dve.tensor_scalar(t1, CI, mim, -2.0, MUL, MUL))
            link(dve, dve.tensor_scalar(t2, CR, mre, 2.0, MUL, MUL))
            link(dve, dve.tensor_tensor(p1, t1, t2, ADD))
            link(dve, dve.tensor_scalar(t1, CI, mre, -2.0, MUL, MUL))
            link(dve, dve.tensor_scalar(t2, CR, mim, -2.0, MUL, MUL))
            link(dve, dve.tensor_tensor(p2, t1, t2, ADD))
            dve.wait_ge(looked_up, 5)
            link(dve, dve.scalar_tensor_tensor(h1, h1, -2.0, h1, MUL, MUL))
            link(dve, dve.scalar_tensor_tensor(EU[:, :, 0:NST], h1, 1.0, mag1, ADD, MUL))
            link(dve, dve.tensor_tensor(EU[:, :, NST:], s1, mag1, MUL))
            link(dve, dve.tensor_scalar(EV[:, :, NST:], EU[:, :, 0:NST], -1.0, None, MUL))
            dve.tensor_copy(EV[:, :, 0:NST], EU[:, :, NST:]).then_inc(e_ready, 1)
            dve.wait_ge(e_ready, 1)
            v2, m2, s2, h2 = (w.rearrange("p (c l) -> p c l", l=Q + 1) for w in tmpw)
            lrow = spread(const(K_LROW, Q + 1), 1, 64)
            dve.tensor_tensor(m2, spread(A2, 2, Q + 1), lrow, MUL).then_inc(tables, 1)
            link(dve, dve.tensor_tensor(v2, spread(FR2, 2, Q + 1), lrow, MUL))
            link(dve, dve.tensor_scalar(s2, v2, MAGIC, MAGIC, ADD, SUB))
            dve.tensor_tensor(v2, v2, s2, SUB).then_inc(tables, 1)
            jrow = spread(const(K_JROW, NJ), 1, 64)
            link(dve, dve.tensor_tensor(sin_j, spread(FR2, 2, NJ), jrow, MUL))
            link(dve, dve.tensor_scalar(cos_j, sin_j, MAGIC, MAGIC, ADD, SUB))
            dve.tensor_tensor(sin_j, sin_j, cos_j, SUB).then_inc(tables, 1)
            dve.wait_ge(looked_up, 8)
            link(dve, dve.scalar_tensor_tensor(h2, h2, -2.0, h2, MUL, MUL))
            link(dve, dve.scalar_tensor_tensor(h2, h2, 1.0, m2, ADD, MUL))
            link(dve, dve.tensor_tensor(s2, s2, m2, MUL))
            P1, P2b = spread(p1, 2, Q + 1), spread(p2, 2, Q + 1)
            link(dve, dve.tensor_tensor(F1, h2, P1, MUL))
            link(dve, dve.tensor_tensor(m2, s2, P2b, MUL))
            dve.tensor_tensor(F1, F1, m2, ADD).then_inc(f_ready, 1)
            link(dve, dve.tensor_tensor(F2, h2, P2b, MUL))
            dve.wait_ge(f_ready, 1)
            link(dve, dve.tensor_tensor(m2, s2, P1, MUL))
            link(dve, dve.tensor_tensor(F2, F2, m2, SUB))
            for n in range(4):
                dve.wait_ge(taps_ready, n + 1)
                dve.tensor_copy(kpad[:, 16 * n:16 * n + 16, Q - 1:2 * Q - 1],
                                bank[4 + n][0:4, :].rearrange("p (c l) -> p c l", l=Q)).then_inc(taps_copied, 1)
            dve.wait_ge(looked_up, 10)
            link(dve, dve.scalar_tensor_tensor(cos_j, cos_j, -2.0, cos_j, MUL, MUL))
            link(dve, dve.tensor_scalar(cos_j, cos_j, 1.0, None, ADD))

        def act_tables(act):
            a1, f1, v1 = (w[:, 0:1024].rearrange("p (c n) -> p c n", n=NST) for w in tmpw[:3])
            mag1, s1, h1 = (w[:, 1024:2048].rearrange("p (c n) -> p c n", n=NST) for w in tmpw[:3])
            lookup(act, 1, SN2, FR2, ACT.Sin, scale=TWO_PI)
            lookup(act, 1, SH2, FR2, ACT.Sin, scale=TWO_PI / 2)
            lookup(act, 3, s1, v1, ACT.Sin, scale=TWO_PI)
            lookup(act, 3, h1, v1, ACT.Sin, scale=TWO_PI / 2)
            lookup(act, 3, mag1, a1, ACT.Exp, scale=q31)

        def act_tables2(act):
            v2, m2, s2, h2 = (w.rearrange("p (c l) -> p c l", l=Q + 1) for w in tmpw)
            lookup(act, 6, m2, m2, ACT.Exp)
            lookup(act, 6, s2, v2, ACT.Sin, scale=TWO_PI)
            lookup(act, 6, h2, v2, ACT.Sin, scale=TWO_PI / 2)
            act.wait_ge(tables, 7)
            act.activation(cos_j, sin_j, ACT.Sin, scale=TWO_PI / 2).then_inc(looked_up, 1)
            act.wait_ge(looked_up, 9)
            act.activation(sin_j, sin_j, ACT.Sin, scale=TWO_PI).then_inc(looked_up, 1)

        def dve_ssm(dve):
            dve.wait_ge(taps_out, 16)
            for m in range(MH):
                for b in range(B):
                    n = B * m + b
                    dve.wait_ge(xz_out, NCH * m + 2 * b + 2)
                    o = u[:, m, L * b:L * b + L]
                    col = ssm_col[:, 6 * m:6 * m + 6]
                    link(dve, dve.tensor_scalar(o, xpad[:, m, b, 0:L], col[:, 0:1], None, MUL))
                    for k in range(1, 4):
                        ins = dve.scalar_tensor_tensor(o, xpad[:, m, b, k:k + L], col[:, k:k + 1], o, MUL, ADD)
                        if k < 3:
                            link(dve, ins)
                    ins.then_inc(conv_done, 1)
            for m in range(MH):
                dve.wait_ge(u_ready, B * (m + 1))
                dve.transpose(xq[:, m].rearrange("p b c -> p (b c)"), u[:, m, :]).then_inc(xq_ready, 1)
            for k in range(NG):
                m, c0 = k // 4, GC * (k % 4)
                cj = spread(cos_j[:, 32 * m + c0:32 * m + c0 + GC, :], 2, B)
                sj = spread(sin_j[:, 32 * m + c0:32 * m + c0 + GC, :], 2, B)
                g4 = "p (c b j) -> p c b j"
                pa4, pb4 = pa.rearrange(g4, c=GC, b=B), pb_.rearrange(g4, c=GC, b=B)
                rho4 = rho_g.rearrange("p (c b j) -> p c (b j)", c=GC, b=B)
                link(dve, dve.tensor_copy(rho4, spread(RHO[:, 32 * m + c0:32 * m + c0 + GC], 2, B * NJ)))
                dve.wait_ge(uv_ready, k + 1)
                link(dve, dve.tensor_tensor(pa4, bank[k % 2][:, :].rearrange(g4, c=GC, b=B), cj, MUL))
                link(dve, dve.memset(rho_g.rearrange("p (s j) -> p s j", j=NJ)[:, :, 0:1], 0.0))
                dve.tensor_tensor(pb4, bank[2 + k % 2][:, :].rearrange(g4, c=GC, b=B), sj, MUL).then_inc(uv_used, 1)
                dve.wait_ge(uv_used, k + 1)
                link(dve, dve.tensor_tensor(pa, pa, pb_, ADD))
                link(dve, dve.tensor_tensor_scan(pb_, rho_g, pa, 0.0, MUL, ADD))
                if k >= 2:
                    dve.wait_ge(y_ready, k - 1)
                link(dve, dve.tensor_tensor(hc[k % 2], pb4, cj, MUL))
                dve.tensor_tensor(hs[k % 2], pb4, sj, MUL).then_inc(state_ready, 1)
            for m in range(MH):
                dve.wait_ge(y_copied, 4 * (m + 1))
                link(dve, dve.transpose(y_t[:, m].rearrange("p b c -> p (b c)"),
                                        ysb[:, m].rearrange("p b c -> p (b c)")))
                yt = y_t[:, m].rearrange("p b c -> p (b c)")
                for c in range(NCH):
                    link(dve, dve.scalar_tensor_tensor(yt[:, tok(c)], u[:, m, tok(c)], ssm_col[:, 6 * m + 5:6 * m + 6],
                                                       yt[:, tok(c)], MUL, ADD))
                    dve.tensor_tensor(sz[:, m, tok(c)], yt[:, tok(c)], sz[:, m, tok(c)], MUL).then_inc(gated, 1)
            for c in range(NCH):
                dve.wait_ge(out_ready, c + 1)
                dve.tensor_tensor(X[:, tok(c)], h_t[:, tok(c)], bank[4 + c][:, :], ADD).then_inc(resid_ready, 1)

        def act_ssm2(act):
            for n in range(MH * B):
                m, b = n // B, n % B
                act.wait_ge(conv_done, n + 1)
                o = u[:, m, L * b:L * b + L]
                act.activation(o, o, ACT.Silu, bias=ssm_col[:, 6 * m + 4:6 * m + 5]).then_inc(u_ready, 1)
            for k in range(NG):
                m, c0 = k // 4, GC * (k % 4)
                act.wait_ge(y_ready, k + 1)
                act.activation(ysb[:, m, :, c0:c0 + GC],
                               bank[4 + k % 2][:, :].rearrange("p (c t) -> p t c", c=GC), ACT.Copy).then_inc(y_copied, 1)

        logits = place(0, NT, E1)
        kept = place(1024, NT, E1)
        cw2 = place(2048, NT, 2, E1)
        best = place(4096, NT, 8)
        rowv = place(4224, 3, NT)
        cwt = place(4352, T)
        cw_hm = place(6400, T, dt=bf16)
        cw_lo = place(7424, T, dt=bf16)
        cw_rest = place(8448, CH)
        hid = [place(8960 + CH * n, CH) for n in range(3)]
        hidw = [place(10496 + CH * n, CH) for n in range(3)]
        m1_w2 = place(MH * T * 2 + 512 + MH * B * (L + 3), KB1 + KBS, 128)
        sel1_f = place(MH * T * 2 + 512 + MH * B * (L + 3) + 128 * (KB1 + KBS), KB1, 128)
        sel1 = place(25000, KB1, 128, dt=bf16)
        m1_w1, m1_b1 = wts["m1_w1"], wts["m1_b1"]
        NB1 = KB1 + KBS
        order1 = list(range(KB1, NB1)) + list(range(KB1))
        route_ready, cw_ready, cwt_ready, cwt_split = (
            sem(n) for n in ("route_ready", "cw_ready", "cwt_ready", "cwt_split"))
        soft_in, soft_out = sem("soft_in"), sem("soft_out")
        up_ready, silu_done, spread_ready, scaled, m1_out, sel_cast = (
            sem(n) for n in ("up_ready", "silu_done", "spread_ready", "scaled", "m1_out", "sel_cast"))
        late_in = sem("late_in")

        def sp_moe1(sp):
            names = [n for n in wts]
            for n in names:
                sp.dma_start(wts[n][:, :], dram[n]).then_inc(m1_in, 16)
            sp.wait_ge(y_ready, NG)
            sp.dma_start(m1_w2, dram["m1_w2"].rearrange("p (a b) -> p a b", b=128)).then_inc(late_in, 16)
            sp.dma_start(sel1_f, dram["sel1"].rearrange("p (a b) -> p a b", b=128)).then_inc(late_in, 16)

        def pe_moe1(pe):
            pe.wait_ge(m1_in, 16 * len(wts))
            for t in range(NT):
                pe.wait_ge(normed, t // 4 + 1)
                ins = pe.matmul(bank[t // 8][:, 64 * (t % 8):64 * (t % 8) + 64], X[:, 128 * t:128 * t + 128],
                                wts["r1_w"][:, :], start=True, stop=True)
                if t % 8 == 7:
                    ins.then_inc(route_ready, 1)

            def turn(g):
                if g == 0:
                    pe.wait_ge(cw_ready, 1)
                if g >= 2:
                    pe.wait_ge(cwt_split, g - 1)
                for t in range(4 * g, 4 * g + 4):
                    ins = pe.transpose(bank[3 + g % 2][:, 128 * (t % 4):128 * (t % 4) + 128],
                                       cw2[:, t].rearrange("p a e -> p (a e)"), const(K_ID, 128))
                ins.then_inc(cwt_ready, 1)

            def up(n):
                c, kb = n // NB1, order1[n % NB1]
                if n < 3:
                    pe.wait_ge(soft_in, 1)
                if n >= 3:
                    pe.wait_ge(silu_done, n - 2)
                pe.matmul(bank[n % 3][:, :], m1_w1[:, 128 * kb:128 * kb + 128], X[:, tok(c)],
                          start=True, stop=True).then_inc(up_ready, 1)
                if kb < KB1:
                    r = KB1 * c + kb
                    if r == 0:
                        for g in range(NCH):
                            turn(g)
                        pe.wait_ge(cwt_split, NCH)
                        pe.wait_ge(sel_cast, 1)
                    if r >= 3:
                        pe.wait_ge(scaled, r - 2)
                    o = bank[3 + r % 3][:, :]
                    pe.matmul(o, sel1[:, kb, :], cw_hm[:, tok(c)], start=True, stop=False)
                    pe.matmul(o, sel1[:, kb, :], cw_lo[:, tok(c)], start=False, stop=True).then_inc(spread_ready, 1)

            def down(n):
                c, kb = n // NB1, order1[n % NB1]
                if n % NB1 == 0 and c >= 2:
                    pe.wait_ge(resid_ready, NCH + c - 1)
                if n == 0:
                    pe.wait_ge(late_in, 32)
                    pe.wait_ge(normed, NCH)
                if kb < KB1:
                    pe.wait_ge(scaled, KB1 * c + kb + 1)
                else:
                    pe.wait_ge(silu_done, n + 1)
                last = n % NB1 == NB1 - 1
                pe.matmul(bank[6 + c % 2][:, :], m1_w2[:, kb, :], (hidw if kb < KB1 else hid)[n % 3],
                          start=(n % NB1 == 0), stop=False).then_inc(down_done, 1)
                if last:
                    pe.matmul(bank[6 + c % 2][:, :], wts["m1_b2"][:, :], cwt[0:E1 + ES, tok(c)],
                              start=False, stop=True).then_inc(m1_out, 1)

            up(0)
            up(1)
            for n in range(NCH * NB1):
                if n + 2 < NCH * NB1:
                    up(n + 2)
                down(n)

        def act_moe1(act):
            act.wait_ge(soft_in, 2)
            act.activation(logits, logits, ACT.Exp).then_inc(soft_out, 1)
            for n in range(NCH * NB1):
                c, kb = n // NB1, order1[n % NB1]
                act.wait_ge(up_ready, n + 1)
                if n >= 3:
                    pr = order1[(n - 3) % NB1]
                    if pr < KB1:
                        act.wait_ge(scaled, KB1 * ((n - 3) // NB1) + pr + 1)
                    else:
                        act.wait_ge(down_done, n - 2)
                act.activation(hid[n % 3], bank[n % 3][:, :], ACT.Silu, bias=m1_b1[:, kb:kb + 1])\
                    .then_inc(silu_done, 1)

        down_done = sem("down_done")

        def dve_moe1(dve):
            dve.wait_ge(m1_in, 16 * len(wts))
            for h in range(2):
                dve.wait_ge(route_ready, h + 1)
                ins = dve.tensor_tensor(logits[:, 8 * h:8 * h + 8], bank[h][:, :].rearrange("p (t e) -> p t e", e=E1),
                                        spread(wts["r1_b"][:, :], 1, 8), ADD)
                if h == 0:
                    link(dve, ins)
            ins.then_inc(soft_in, 1)
            dve.wait_ge(soft_in, 1)
            link(dve, dve.tensor_reduce(rowv[:, 0], logits, AX.X, ALU.max))
            dve.tensor_tensor(logits, logits, spread(rowv[:, 0], 2, E1), SUB).then_inc(soft_in, 1)
            link(dve, dve.memset(cwt[64:96, :], 1.0))
            link(dve, dve.memset(cw_lo[64:128, :], 0.0))
            dve.wait_ge(late_in, 32)
            dve.tensor_copy(sel1, sel1_f).then_inc(sel_cast, 1)
            dve.wait_ge(soft_out, 1)
            for t in range(NT):
                ins = dve.max(best[:, t], logits[:, t])
            link(dve, ins)
            for t in range(NT):
                ins = dve.match_replace(kept[:, t], best[:, t], logits[:, t], 0.0)
            link(dve, ins)
            link(dve, dve.tensor_tensor(kept, logits, kept, SUB))
            link(dve, dve.tensor_reduce(rowv[:, 1], kept, AX.X, ADD))
            link(dve, dve.reciprocal(rowv[:, 2], rowv[:, 1]))
            link(dve, dve.tensor_tensor(cw2[:, :, 0], kept, spread(rowv[:, 2], 2, E1), MUL))
            dve.tensor_copy(cw2[:, :, 1], cw2[:, :, 0]).then_inc(cw_ready, 1)
            for g in range(NCH):
                dve.wait_ge(cwt_ready, g + 1)
                w = bank[3 + g % 2]
                link(dve, dve.tensor_copy(cw_hm[:, tok(g)], w[:, :]))
                link(dve, dve.tensor_tensor(cw_rest, w[:, :], cw_hm[:, tok(g)], SUB))
                dve.tensor_copy(cwt[0:64, tok(g)], w[0:64, :])
                link(dve, dve.tensor_copy(cw_hm[64:128, tok(g)], cw_rest[64:128, :]))
                link(dve, dve.tensor_copy(cw_lo[0:64, tok(g)], cw_rest[0:64, :]))
                link(dve, dve.tensor_tensor(cw_rest[0:64, :], cw_rest[0:64, :], cw_lo[0:64, tok(g)], SUB))
                dve.tensor_copy(cw_lo[0:64, tok(g)], cw_rest[0:64, :]).then_inc(cwt_split, 1)
            for c in range(NCH):
                for kb in range(KB1):
                    r, n = KB1 * c + kb, NB1 * c + KBS + kb
                    dve.wait_ge(silu_done, n + 1)
                    dve.wait_ge(spread_ready, r + 1)
                    if n >= 3:
                        dve.wait_ge(down_done, n - 2)
                    dve.tensor_tensor(hidw[n % 3], hid[n % 3], bank[3 + r % 3][:, :], MUL).then_inc(scaled, 1)
                dve.wait_ge(m1_out, c + 1)
                dve.tensor_tensor(X[:, tok(c)], X[:, tok(c)], bank[6 + c % 2][:, :], ADD).then_inc(resid_ready, 1)

        q9 = [place(8448 * b, H, NL * QL, dt=bf16) for b in range(B)]
        k9 = [place(16896 + 2176 * b, KVH, LP, dt=bf16) for b in range(B)]
        vt = place(21248, B * NL, KVH, 32)
        rope = place(24064, 2, L + CH)
        parts = [place(27136 + 768 * n, 3, CH, dt=bf16) for n in range(3)]
        rot = [work[:, CH * n:CH * n + CH] for n in range(5)]
        rot2, rtm = work[:, CH * 5:CH * 6], work[:, CH * 6:CH * 7]
        rsq = [work[:, CH * n:CH * n + CH] for n in (7, 8)]
        rgs = [work[:, CH * n:CH * n + CH] for n in (9, 10)]
        lat = work[0:LAT, CH * 12:CH * 16]
        RING = 6
        probs = [work[:, 2 * CH * n:2 * CH * n + 2 * CH] for n in range(RING)]
        osb = [work[:, CH * n:CH * n + CH] for n in (12, 13)]
        onrm = [work[:, CH * n:CH * n + CH] for n in (14, 15)]
        rec, rec2 = place(29440, CH), place(27136, CH)
        q_dram = [nc.dram_tensor(f"q_parts{n}", (3, 128, T), bf16, kind="Internal").ap() for n in range(2)]
        k_dram = [nc.dram_tensor(f"k_parts{n}", (3, 32, T), bf16, kind="Internal").ap() for n in range(2)]
        lat_ready, lat_copied, v_ready, v_copied = (sem(n) for n in ("lat_ready", "lat_copied", "v_ready", "v_copied"))
        rope_in, pr_ready, rot_ready, rsq_ready, ms_ready, gs_ready, parts_ready = (
            sem(n) for n in ("rope_in", "pr_ready", "rot_ready", "rsq_ready", "ms_ready", "gs_ready", "parts_ready"))
        parts_out = [sem(f"parts_out{n}") for n in range(3)]
        in9 = [sem(f"relayout_in{b}") for b in range(B)]
        pads = sem("pads")
        normed9, high_ready, rest_ready, mid_ready = (
            sem(n) for n in ("item_normed", "high_ready", "rest_ready", "mid_ready"))
        x_in = place(30000, T)
        x_kept, x_added = sem("x_kept"), sem("x_added")

        def pool_attn(pool):
            pool.wait_ge(normed, 2 * NCH)
            for b in range(B):
                link(pool, pool.memset(arena[64:128, 8448 * b:8448 * b + 8448], 0.0))
                link(pool, pool.memset(arena[64:128, 16896 + 2176 * b:16896 + 2176 * b + 2176], 0.0))
                pool.memset(k9[b][0:64, :, 0:WIN], 0.0)
                pool.memset(k9[b][0:64, :, WIN + L:LP], 0.0)
                pool.memset(q9[b][0:64, :, L:NL * QL], 0.0).then_inc(pads, 1)
                pool.wait_ge(pads, b + 1)
            for c in range(NCH):
                pool.tensor_copy(x_in[:, tok(c)], X[:, tok(c)]).then_inc(x_kept, 1)
            pool_parts(pool, 0)
            for c in range(NCH):
                pool.wait_ge(x_kept, c + 1)
                pool.wait_ge(normed, NCH * 3 + c + 1)
                pool.tensor_tensor(X[:, tok(c)], X[:, tok(c)], x_in[:, tok(c)], ADD).then_inc(x_added, 1)
            pool_parts(pool, 1)

        def pool_parts(pool, n):
            for i in range(NIT + 1):
                if i < NIT:
                    j = NIT * n + i
                    pool.wait_ge(high_ready, j + 1)
                    pool.tensor_tensor(rot[i], rot[i], parts[slot_of[j]][:, 0], SUB).then_inc(rest_ready, 1)
                if i >= 1:
                    j = NIT * n + i - 1
                    pool.wait_ge(mid_ready, j + 1)
                    pool.tensor_tensor(parts[slot_of[j]][:, 2], rot[i - 1], parts[slot_of[j]][:, 1], SUB)\
                        .then_inc(parts_ready, 1)
        scores_ready, exp_done, masked, pv_done, guessed = (
            sem(n) for n in ("scores_ready", "exp_done", "masked", "pv_done", "den_guessed"))
        osb_ready, den_ready, on_ready, wo_ready, added = (
            sem(n) for n in ("osb_ready", "den_ready", "on_ready", "wo_ready", "added"))
        NIT = 1 + NCH
        sends = [KVH if i == 0 else 1 for i in range(NIT)] * 2
        slot_of = [j % 3 for j in range(2 * NIT)]

        def sent(j):
            return 16 * sum(sends[m] for m in range(j + 1) if slot_of[m] == slot_of[j])

        def item_banks(i):
            return [(4, 5), (2, 3), (0, 1), (2, 3), (0, 1)][i]

        def sp_attn(sp, n):
            if n == 0:
                sp.wait_ge(normed, 2 * NCH)
            else:
                sp.wait_ge(parts_ready, NIT)
            sp.dma_start(rope, dram["rope"][n]).then_inc(rope_in, 16)
            for i in range(NIT):
                j = NIT * n + i
                sp.wait_ge(parts_ready, j + 1)
                p = parts[slot_of[j]]
                if i == 0:
                    for c in range(NCH):
                        sp.dma_start(k_dram[n][:, :, tok(c)].rearrange("a r t -> r a t"), p[32 * c:32 * c + 32])\
                            .then_inc(parts_out[slot_of[j]], 16)
                else:
                    sp.dma_start(q_dram[n][:, :, tok(i - 1)].rearrange("a r t -> r a t"), p)\
                        .then_inc(parts_out[slot_of[j]], 16)
                if i in (2, 4):
                    b = i // 2 - 1
                    for m in range(NIT * n, j + 1):
                        sp.wait_ge(parts_out[slot_of[m]], sent(m))
                    sp.wait_ge(pads, b + 1)
                    if n == 1 and b == 0:
                        sp.wait_ge(pv_done, UG)
                    for a in range(3):
                        for c in range(3):
                            r = slice((3 * a + c) * HD, (3 * a + c) * HD + HD)
                            sp.dma_start(q9[b][r, :, 0:L], q_dram[n][c, :, L * b:L * b + L]
                                         .rearrange("(h d) t -> d h t", d=HD)).then_inc(in9[b], 16)
                            sp.dma_start(k9[b][r, :, WIN:WIN + L], k_dram[n][a, :, L * b:L * b + L]
                                         .rearrange("(h d) t -> d h t", d=HD)).then_inc(in9[b], 16)

        def v_tiles(n):
            return [(b, i) for b in range(B) for i in range(NL if n else NQT)]

        def pe_proj(pe, n):
            kv, q = (wts["g_kv"], wts["g_q"]) if n == 0 else (wts["l_kv"], wts["l_q"])
            for c in range(NCH):
                pe.wait_ge(normed, NCH * (2 + n) + c + 1)
                if n == 0:
                    if c >= 2:
                        pe.wait_ge(lat_copied, c - 1)
                    pe.matmul(bank[c % 2][0:LAT, :], wts["g_down"][:, :], xn_tok(c), start=True, stop=True)\
                        .then_inc(lat_ready, 1)
            if n == 0:
                pe.wait_ge(lat_copied, NCH)
            for t, (b, i) in enumerate(v_tiles(n)):
                l = lat[:, (NQT * b + i) * 128:(NQT * b + i) * 128 + 128] if n == 0 else xn[:, b, QL * i:QL * i + 128]
                ins = pe.matmul(bank[t // 16][:, 32 * (t % 16):32 * (t % 16) + 32], l, kv[:, 64:96],
                                start=True, stop=True)
            ins.then_inc(v_ready, 1)

            def project(i):
                j = NIT * n + i
                b0, b1 = item_banks(i)
                if i == 2:
                    pe.wait_ge(v_copied, n + 1)
                if i >= 3:
                    pe.wait_ge(rot_ready, j - 1)
                if i == 0:
                    for w, bk in ((0, b0), (32, b1)):
                        for c in range(NCH):
                            x = lat[:, tok(c)] if n == 0 else xn_tok(c)
                            ins = pe.matmul(bank[bk][32 * c:32 * c + 32, :], kv[:, w:w + 32], x, start=True, stop=True)
                else:
                    for w, bk in ((0, b0), (128, b1)):
                        ins = pe.matmul(bank[bk][:, :], q[:, w:w + 128], xn_tok(i - 1), start=True, stop=True)
                ins.then_inc(pr_ready, 1)

            def mean_square(i):
                j = NIT * n + i
                pe.wait_ge(rsq_ready, j + 1)
                if i >= 2:
                    pe.wait_ge(normed9, j - 1)
                pe.matmul(bank[6 + i % 2][:, :], const(K_HEAD, 128), rsq[i % 2], start=True, stop=True)\
                    .then_inc(ms_ready, 1)

            project(0)
            project(1)
            project(2)
            for i in range(NIT):
                mean_square(i)
                if i + 3 < NIT:
                    project(i + 3)

        def act_proj(act, n):
            if n == 0:
                for c in range(NCH):
                    act.wait_ge(lat_ready, c + 1)
                    act.activation(lat[:, tok(c)], bank[c % 2][0:LAT, :], ACT.Copy).then_inc(lat_copied, 1)

            def squares(i):
                j = NIT * n + i
                act.wait_ge(rot_ready, j + 1)
                if i >= 2:
                    act.wait_ge(ms_ready, j - 1)
                act.activation(rsq[i % 2], rot[i], ACT.Square).then_inc(rsq_ready, 1)

            def part(i, m):
                j = NIT * n + i
                act.wait_ge((normed9, rest_ready)[m], j + 1)
                if m == 0 and j >= 3:
                    act.wait_ge(parts_out[slot_of[j]], sent(j - 3))
                act.activation(parts[slot_of[j]][:, m], rot[i], ACT.Copy).then_inc((high_ready, mid_ready)[m], 1)

            squares(0)
            squares(1)
            for i in range(NIT + 2):
                if i < NIT:
                    j = NIT * n + i
                    act.wait_ge(ms_ready, j + 1)
                    if i >= 2:
                        act.wait_ge(normed9, j - 1)
                    link(act, act.activation(rgs[i % 2], bank[6 + i % 2][:, :], ACT.Ln, bias=eps[:, 1:2]))
                    act.activation(rgs[i % 2], rgs[i % 2], ACT.Exp, scale=-0.5).then_inc(gs_ready, 1)
                if i + 2 < NIT:
                    squares(i + 2)
                if 1 <= i <= NIT:
                    part(i - 1, 0)
                if i >= 2:
                    part(i - 2, 1)

        def dve_proj(dve, n):
            if n == 1:
                dve.wait_ge(pv_done, UG)
            link(dve, dve.memset(vt, 1.0))
            if n == 1:
                for b in range(B):
                    link(dve, dve.memset(vt[0:WIN, NL * b], 0.0))
            dve.wait_ge(v_ready, n + 1)
            nt = len(v_tiles(n))
            for t0 in range(0, nt, 16):
                m = min(16, nt - t0)
                ins = dve.tensor_copy(vt[:, t0:t0 + m, :, 0:HD], bank[t0 // 16][:, 0:32 * m]
                                      .rearrange("p (t k d) -> p t k d", k=KVH, d=HD))
            ins.then_inc(v_copied, 1)
            dve.wait_ge(rope_in, 16 * (n + 1))

            def rotate(i):
                j = NIT * n + i
                b0, b1 = item_banks(i)
                at = L if i == 0 else (i - 1) % 2 * CH
                dve.wait_ge(pr_ready, j + 1)
                if n:
                    dve.wait_ge(parts_ready, NIT)
                r = rot[i]
                link(dve, dve.tensor_tensor(r, bank[b0][:, :], rope[:, 0, at:at + CH], MUL))
                link(dve, dve.tensor_tensor(rot2, bank[b1][:, :], rope[:, 1, at:at + CH], MUL))
                dve.tensor_tensor(r, r, rot2, ADD).then_inc(rot_ready, 1)

            def finish(i):
                j = NIT * n + i
                r = rot[i]
                dve.wait_ge(gs_ready, j + 1)
                rsqrt_step(dve, rgs[i % 2], bank[6 + i % 2][:, :], rtm, EPS_RMS)
                dve.tensor_tensor(r, r, rgs[i % 2], MUL).then_inc(normed9, 1)

            rotate(0)
            rotate(1)
            for i in range(NIT):
                if i + 2 < NIT:
                    rotate(i + 2)
                finish(i)

        def tiles(n):
            if n == 0:
                return [(b, t, t + 1) for b in range(B) for t in range(NQT)]
            return [(b, t, 1) for b in range(B) for t in range(NL)]

        def units(n):
            return [(o, kt) for o, (b, t, nk) in enumerate(tiles(n)) for kt in range(nk)]

        UG, UL = len(units(0)), len(units(1))
        width = (128, QL)
        base_u, base_o = (0, UG), (0, len(tiles(0)))

        def ends(n):
            return {u: o for u, (o, kt) in enumerate(units(n)) if kt == tiles(n)[o][2] - 1}

        D_COPY, D_DEN, D_GUESS, D_NORM, D_OUT = 2, 3, 4, (3, 4), (6, 6)

        def wo_group(n, o):
            b, t, _ = tiles(n)[o]
            per = 4 if n == 0 else 5
            w = width[n]
            count = NQT if n == 0 else NL
            first = t // per * per
            full = t % per == per - 1 or t == count - 1
            g = sum(1 for m in range(o) if wo_full(n, m))
            return (t % per) * w, full, (L * b + first * w, min(L * b + (t + 1) * w, L * b + L)), g

        def wo_full(n, o):
            b, t, _ = tiles(n)[o]
            per = 4 if n == 0 else 5
            return t % per == per - 1 or t == (NQT if n == 0 else NL) - 1

        def pe_core(pe, n):
            U, E, TL, w = units(n), ends(n), tiles(n), width[n]
            wo = wts["g_o" if n == 0 else "l_o"]

            def scores(u, hp):
                o, kt = U[u]
                b, t, _ = TL[o]
                if hp == 0 and kt == 0 and t == 0:
                    pe.wait_ge(in9[b], 18 * 16 * (n + 1))
                if u == 0:
                    pe.wait_ge(parts_ready, NIT * (n + 1))
                else:
                    pe.wait_ge(exp_done, 2 * (base_u[n] + u) + hp - 1)
                k0 = WIN + 128 * kt if n == 0 else QL * t
                for kv in (2 * hp, 2 * hp + 1):
                    out_ = bank[kv][:, 0:4 * w].rearrange("p (h q) -> p h q", h=4)
                    ins = pe.matmul(out_, k9[b][:, kv, k0:k0 + 128],
                                    q9[b][:, 4 * kv:4 * kv + 4, w * t:w * t + w], start=True, stop=True)
                ins.then_inc(scores_ready, 1)

            def values(u):
                o, kt = U[u]
                b, t, nk = TL[o]
                if kt == nk - 1:
                    pe.wait_ge(masked, 2 * (base_o[n] + o + 1))
                else:
                    pe.wait_ge(exp_done, 2 * (base_u[n] + u + 1))
                if kt == 0 and o >= 2:
                    pe.wait_ge(osb_ready, base_o[n] + o - 1)
                tile = (NQT if n == 0 else NL) * b + (kt if n == 0 else t)
                for kv in range(KVH):
                    p = probs[(2 * u + kv // 2) % RING]
                    ins = pe.matmul(bank[4 + o % 2][32 * kv:32 * kv + 32, 0:4 * w], vt[:, tile, kv, :],
                                    p[:, kv % 2 * CH:kv % 2 * CH + 4 * w], start=(kt == 0), stop=(kt == nk - 1))
                ins.then_inc(pv_done, 1)

            def denominators(o):
                pe.wait_ge(osb_ready, base_o[n] + o + 1)
                if o >= 1:
                    pe.wait_ge(on_ready, base_o[n] + o)
                pe.matmul(bank[6][:, 0:4 * w], const(K_DEN, 128), osb[o % 2][:, 0:4 * w], start=True, stop=True)\
                    .then_inc(den_ready, 1)

            def outputs(o):
                at, full, cols, g = wo_group(n, o)
                pe.wait_ge(on_ready, base_o[n] + o + 1)
                if at == 0 and g >= 1:
                    if n == 0:
                        pe.wait_ge(resid_ready, NCH * 2 + g)
                    elif (g - 1) % 3 == 0:
                        pe.wait_ge(added, (g - 1) // 3 + 1)
                    else:
                        pe.wait_ge(resid_ready, NCH * 3 + (g - 1) // 3 * 2 + (g - 1) % 3)
                for h in range(4):
                    ins = pe.matmul(bank[7][:, at:at + w], wo[:, 128 * h:128 * h + 128],
                                    onrm[o % 2][:, w * h:w * h + w], start=(h == 0), stop=(h == 3))
                ins.then_inc(wo_ready, 1)

            scores(0, 0)
            scores(0, 1)
            for u in range(len(U) + D_OUT[n]):
                if u + 1 < len(U):
                    scores(u + 1, 0)
                if 1 <= u <= len(U):
                    values(u - 1)
                if u + 1 < len(U):
                    scores(u + 1, 1)
                if u - D_OUT[n] in E:
                    outputs(E[u - D_OUT[n]])
                if u - D_DEN in E:
                    denominators(E[u - D_DEN])

        def act_core(act, n):
            U, E, w = units(n), ends(n), width[n]
            for u in range(len(U) + D_GUESS):
                for hp in range(2 if u < len(U) else 0):
                    s = 2 * u + hp
                    act.wait_ge(scores_ready, 2 * base_u[n] + s + 1)
                    if s >= RING:
                        act.wait_ge(pv_done, base_u[n] + (s - RING) // 2 + 1)
                    p = probs[s % RING].rearrange("p (k c) -> p k c", k=2)[:, :, 0:4 * w]
                    act.activation(p, two[hp][:, :, 0:4 * w], ACT.Exp, scale=HD ** -0.5).then_inc(exp_done, 1)
                if n == 1 and u - D_GUESS in E:
                    o = E[u - D_GUESS]
                    act.wait_ge(den_ready, base_o[n] + o + 1)
                    if o >= 1:
                        act.wait_ge(on_ready, base_o[n] + o)
                    link(act, act.activation(rec[:, 0:4 * w], bank[6][:, 0:4 * w], ACT.Ln))
                    act.activation(rec[:, 0:4 * w], rec[:, 0:4 * w], ACT.Exp, scale=-1.0).then_inc(guessed, 1)
                if u - D_COPY in E:
                    o = E[u - D_COPY]
                    act.wait_ge(pv_done, base_u[n] + u - D_COPY + 1)
                    if o >= 2:
                        act.wait_ge(on_ready, base_o[n] + o - 1)
                    act.activation(osb[o % 2][:, 0:4 * w], bank[4 + o % 2][:, 0:4 * w], ACT.Copy)\
                        .then_inc(osb_ready, 1)

        def dve_core(dve, n):
            U, E, TL, w = units(n), ends(n), tiles(n), width[n]
            if n == 1:
                dve.wait_ge(parts_out[0], sent(max(j for j in range(2 * NIT) if slot_of[j] == 0)))
            mask = spread(spread(const(K_CAUS, 128) if n == 0 else const(K_BAND, QL), 1, 4), 1, 2)
            for u in range(len(U) + D_OUT[n]):
                if u < len(U) and u in E:
                    for hp in range(2):
                        s = 2 * u + hp
                        dve.wait_ge(exp_done, 2 * base_u[n] + s + 1)
                        v = probs[s % RING].rearrange("p (k c) -> p k c", k=2)[:, :, 0:4 * w]\
                            .rearrange("p k (h q) -> p k h q", h=4)
                        dve.tensor_tensor(v, v, mask, MUL).then_inc(masked, 1)
                if u - D_NORM[n] in E:
                    o = E[u - D_NORM[n]]
                    d, r, r2 = bank[6][:, 0:4 * w], rec[:, 0:4 * w], rec2[:, 0:4 * w]
                    if n == 0:
                        dve.wait_ge(den_ready, base_o[n] + o + 1)
                        link(dve, dve.reciprocal(r, d))
                    else:
                        dve.wait_ge(guessed, o + 1)
                        link(dve, dve.tensor_tensor(r2, d, r, MUL))
                        link(dve, dve.scalar_tensor_tensor(r2, r2, 2.0, r, SUB, MUL))
                    if o >= 2:
                        dve.wait_ge(wo_ready, base_o[n] + o - 1)
                    dve.scalar_tensor_tensor(onrm[o % 2][:, 0:4 * w], osb[o % 2][:, 0:4 * w],
                                             1.0 if n == 0 else -1.0, r if n == 0 else r2, MUL, MUL)\
                        .then_inc(on_ready, 1)
                if u - D_OUT[n] in E:
                    o = E[u - D_OUT[n]]
                    at, full, (x0, x1), g = wo_group(n, o)
                    if full:
                        dve.wait_ge(wo_ready, base_o[n] + o + 1)
                        dve.wait_ge(x_kept if n == 0 else x_added, NCH)
                        ins = dve.tensor_tensor(X[:, x0:x1], X[:, x0:x1], bank[7][:, 0:x1 - x0], ADD)
                        ins.then_inc(resid_ready if n == 0 or g % 3 > 0 else added, 1)

        r2w, r2b, firstw, sel2f = wts["r2_w"], wts["r2_b"], wts["first"], wts["sel2"]
        m2_w1 = place(0, E2 * FF2)
        m2_w2 = place(E2 * FF2, E2 * 4, 128)
        D0 = 16896
        rt = place(D0, NT, E2)
        mk = place(D0 + 128, NT, E2)
        mk2 = place(D0 + 256, NT, 2 * E2)
        mrow = place(D0 + 512, 2, NT)
        mt = place(D0 + 1024, T)
        mtb = place(D0 + 3072, T, dt=bf16)
        selb = place(D0 + 4096, E2 + 1, 128, dt=bf16)
        pbx = place(D0 + 4864, T)
        xe = [place(D0 + 6912 + CH * n, CH) for n in range(2)]
        ge = [place(D0 + 7936 + CH * n, CH) for n in range(4)]
        route2_ready, sig_in, sig_out, mk_ready, mt_ready, mt_copied = (
            sem(n) for n in ("route2_ready", "sig_in", "sig_out", "mk_ready", "mt_ready", "mt_copied"))
        mb_ready, xe_ready, up2_ready, gelu_done, down2, m2_out, pb_ready, pb_copied = (
            sem(n) for n in ("mb_ready", "xe_ready", "up2_ready", "gelu_done", "down2", "m2_out", "pb_ready", "pb_copied"))
        KBE = FF2 // 128

        def sp_moe2(sp):
            sp.wait_ge(pv_done, UG + NL)
            sp.dma_start(m2_w1, dram["m2_w1"]).then_inc(m2_in, 16)
            sp.dma_start(m2_w2, dram["m2_w2"].rearrange("p (a b) -> p a b", b=128)).then_inc(m2_in, 16)

        def pe_moe2(pe):
            for t in range(NT):
                pe.wait_ge(normed, NCH * 4 + t // 4 + 1)
                ins = pe.matmul(bank[0][:, 8 * t:8 * t + 8], X[:, 128 * t:128 * t + 128], r2w[:, :],
                                start=True, stop=True)
            ins.then_inc(route2_ready, 1)
            pe.wait_ge(mk_ready, 1)
            for g in range(NCH):
                if g >= 2:
                    pe.wait_ge(mt_copied, g - 1)
                for t in range(4 * g, 4 * g + 4):
                    ins = pe.transpose(bank[1 + g % 2][0:16, 128 * (t % 4):128 * (t % 4) + 128], mk2[:, t], const(K_ID, 128))
                ins.then_inc(mt_ready, 1)
            pe.wait_ge(mt_copied, NCH)
            for c in range(NCH):
                if c >= 2:
                    pe.wait_ge(pb_copied, c - 1)
                pe.matmul(bank[1 + c % 2][:, :], sel2f[:, 128 * E2:128 * E2 + 128], mt[0:16, tok(c)],
                          start=True, stop=True).then_inc(pb_ready, 1)
            pe.wait_ge(pb_copied, NCH)
            pe.wait_ge(m2_in, 32)

            def masks(n):
                c, e = n // E2, n % E2
                if n >= 1:
                    pe.wait_ge(xe_ready, n)
                pe.matmul(bank[0][:, :], selb[0:16, e, :], mtb[0:16, tok(c)], start=True, stop=True)\
                    .then_inc(mb_ready, 1)

            def up(m):
                n, k = m // KBE, m % KBE
                e = n % E2
                pe.wait_ge(xe_ready, n + 1)
                if m >= 4:
                    pe.wait_ge(gelu_done, m - 3)
                pe.matmul(bank[1 + m % 4][:, :], m2_w1[:, FF2 * e + 128 * k:FF2 * e + 128 * k + 128], xe[n % 2],
                          start=True, stop=True).then_inc(up2_ready, 1)

            def down(m):
                n, k = m // KBE, m % KBE
                c, e = n // E2, n % E2
                if e == 0 and k == 0 and c >= 2:
                    pe.wait_ge(resid_ready, NCH * 4 + c - 1)
                pe.wait_ge(gelu_done, m + 1)
                ins = pe.matmul(bank[6 + c % 2][:, :], m2_w2[:, KBE * e + k, :], ge[m % 4],
                                start=(e == 0 and k == 0), stop=(e == E2 - 1 and k == KBE - 1))
                ins.then_inc(down2, 1)

            masks(0)
            masks(1)
            M = NCH * E2 * KBE
            up(0)
            up(1)
            up(2)
            for m in range(M):
                if m + 3 < M:
                    up(m + 3)
                if m % KBE == 0 and m // KBE + 2 < NCH * E2:
                    masks(m // KBE + 2)
                down(m)

        def act_moe2(act):
            act.wait_ge(sig_in, 1)
            act.activation(rt, rt, ACT.Sigmoid).then_inc(sig_out, 1)
            for m in range(NCH * E2 * KBE):
                act.wait_ge(up2_ready, m + 1)
                if m >= 4:
                    act.wait_ge(down2, m - 3)
                act.activation(ge[m % 4], bank[1 + m % 4][:, :], ACT.Gelu).then_inc(gelu_done, 1)

        def dve_moe2(dve):
            dve.wait_ge(route2_ready, 1)
            g = "p (t e) -> p t e"
            dve.tensor_tensor(rt, bank[0][:, 0:128].rearrange(g, e=E2), spread(r2b[:, :], 1, NT), ADD)\
                .then_inc(sig_in, 1)
            link(dve, dve.tensor_copy(selb[0:16], sel2f[:, :].rearrange("p (a b) -> p a b", b=128)))
            dve.wait_ge(sig_out, 1)
            link(dve, dve.tensor_reduce(mrow[:, 0], rt, AX.X, ALU.max))
            link(dve, dve.tensor_tensor(mk, rt, spread(mrow[:, 0], 2, E2), ALU.is_equal))
            link(dve, dve.tensor_tensor(mk, mk, firstw[:, :].rearrange(g, e=E2), MUL))
            link(dve, dve.tensor_reduce(mrow[:, 1], mk, AX.X, ALU.max))
            link(dve, dve.tensor_tensor(mk2[:, :, 0:E2], mk, spread(mrow[:, 1], 2, E2), ALU.is_equal))
            dve.tensor_tensor(mk2[:, :, E2:], mk2[:, :, 0:E2], spread(mrow[:, 0], 2, E2), MUL).then_inc(mk_ready, 1)
            for c in range(NCH):
                dve.wait_ge(mt_ready, c + 1)
                link(dve, dve.tensor_copy(mt[0:16, tok(c)], bank[1 + c % 2][0:16, :]))
                dve.tensor_copy(mtb[0:16, tok(c)], mt[0:16, tok(c)]).then_inc(mt_copied, 1)
            for c in range(NCH):
                dve.wait_ge(pb_ready, c + 1)
                dve.tensor_copy(pbx[:, tok(c)], bank[1 + c % 2][:, :]).then_inc(pb_copied, 1)

            def result(c):
                dve.wait_ge(m2_out_at(c)[0], m2_out_at(c)[1])
                t = pbx[:, tok(c)]
                link(dve, dve.tensor_tensor(t, t, bank[6 + c % 2][:, :], MUL))
                dve.tensor_tensor(X[:, tok(c)], X[:, tok(c)], t, ADD).then_inc(resid_ready, 1)

            for n in range(NCH * E2):
                c, e = n // E2, n % E2
                dve.wait_ge(mb_ready, n + 1)
                if n >= 2:
                    dve.wait_ge(up2_ready, KBE * (n - 1))
                dve.tensor_tensor(xe[n % 2], X[:, tok(c)], bank[0][:, :], MUL).then_inc(xe_ready, 1)
                if e == 3 and c >= 1:
                    result(c - 1)
            result(NCH - 1)

        def m2_out_at(c):
            return down2, KBE * E2 * (c + 1)

        block = stack.enter_context(nc.Block())

        @block.sync
        def _(sp):
            sp_ssm(sp)
            n_norms = 1
            if stages >= 2:
                sp_moe1(sp)
                n_norms = 2
            if stages >= 3:
                sp_attn(sp, 0)
                sp_attn(sp, 1)
                sp_moe2(sp)
                n_norms = 5
            if stages >= 4:
                n_norms = 6
            for c in range(NCH):
                sp.wait_ge(normed, NCH * (n_norms - 1) + c + 1)
                sp.dma_start(out[:, tok(c)], X[:, tok(c)]).then_inc(sem_out, 16)
            sp.wait_ge(m2_in, 32) if stages >= 3 else None
            sp.wait_ge(sem_out, 16 * NCH)

        @block.gpsimd
        def _(pool):
            if stages >= 3:
                pool_attn(pool)

        @block.tensor
        def _(pe):
            pe_ssm(pe)
            pe_norm(pe, 0, False)
            if stages >= 2:
                pe_moe1(pe)
                pe_norm(pe, 1, False)
            if stages >= 3:
                for n in range(2):
                    pe_norm(pe, 2 + n, True)
                    pe_proj(pe, n)
                    pe_core(pe, n)
                pe_norm(pe, 4, False)
            if stages >= 4:
                pe_moe2(pe)
                pe_norm(pe, 5, False)

        @block.scalar
        def _(act):
            act_tables(act)
            act_ssm(act)
            act_tables2(act)
            act_ssm2(act)
            act_norm(act, 0, 0)
            if stages >= 2:
                act_moe1(act)
                act_norm(act, 1, 0)
            if stages >= 3:
                for n in range(2):
                    act_norm(act, 2 + n, 1)
                    act_proj(act, n)
                    act_core(act, n)
                act_norm(act, 4, 0)
            if stages >= 4:
                act_moe2(act)
                act_norm(act, 5, 0)

        @block.vector
        def _(dve):
            dve_tables(dve)
            dve_ssm(dve)
            dve_norm(dve, 0, 0)
            if stages >= 2:
                dve_moe1(dve)
                dve_norm(dve, 1, 0)
            if stages >= 3:
                for n in range(2):
                    dve_norm(dve, 2 + n, 1)
                    dve_proj(dve, n)
                    dve_core(dve, n)
                dve_norm(dve, 4, 0)
            if stages >= 4:
                dve_moe2(dve)
                dve_norm(dve, 5, 0)


def kernel(**inputs):
    from concourse import bacc
    from concourse.bass_utils import run_bass_kernel_spmd

    nc = bacc.Bacc("TRN2", target_bir_lowering=False, num_devices=1)
    arrays = {"in_" + k: v for k, v in lay_out({k: np.asarray(v) for k, v in inputs.items()}).items()}
    dram = {k[3:]: nc.dram_tensor(k, v.shape, mybir.dt.from_np(v.dtype), kind="ExternalInput").ap()
            for k, v in arrays.items()}
    out = nc.dram_tensor("out", (DM, T), mybir.dt.float32, kind="ExternalOutput").ap()
    build(nc, dram, out)
    r = run_bass_kernel_spmd(nc, [arrays], core_ids=[0])
    return np.ascontiguousarray(np.asarray(r.results[0]["out"]).T).reshape(B, L, DM)
```

```python
import numpy as np
from contextlib import ExitStack

import concourse.bass as bass
from concourse import mybir

B, L, DM = 2, 1024, 128
T = B * L
CH = 512
NCH = T // CH
DIN, NST = 256, 16
MH = DIN // 128
Q = 32
NJ = L // Q
GC = 8
NG = MH * 32 // GC
E1, H1, ES, HS1 = 64, 32, 2, 256
KB1 = E1 * H1 // 128
KBS = ES * HS1 // 128
E2, FF2 = 8, 512
H, KVH, HD, LAT, WIN = 16, 4, 8, 32, 32
QL = 128 - WIN
NL = -(-L // QL)
LP = WIN + NL * QL
NQT = L // 128
NT = T // 128
AREA = 33000
EPS_LN, EPS_RMS = 1e-5, 1e-6
MAGIC = 12582912.0
TWO_PI = 6.283185
C1, C2 = 6.28125, 0.0019350051879882812
C3 = 2 * np.pi - C1 - C2
LOG_EXP = "natural_log_exp_and_others"
LOG2E, LN2H, LN2L = 1.4426950408889634, 0.693359375, -2.12194440e-4

K_Q31, K_MRE, K_MIM, K_LROW, K_JROW, K_SEL = 0, 1, 2, 3, 36, 68
K_MEAN, K_HEAD, K_DEN, K_ID, K_CAUS, K_BAND, K_N = 72, 200, 328, 456, 584, 712, 808


def constants():
    c = np.zeros((128, K_N), np.float32)
    p = np.arange(128)
    c[:, K_Q31] = Q - 1 - p % 32
    c[:, K_MRE] = p % 32 < NST
    c[:, K_MIM] = p % 32 >= NST
    c[:, K_LROW:K_LROW + Q + 1] = np.arange(Q + 1)
    c[:, K_JROW:K_JROW + NJ] = np.arange(NJ) * Q
    for g in range(4):
        c[32 * g:32 * g + NST, K_SEL + g] = 1.0
    c[:, K_MEAN:K_MEAN + 128] = 1.0 / 128
    c[:, K_HEAD:K_HEAD + 128] = (p[:, None] // HD == p[None] // HD) / HD
    c[:, K_DEN:K_DEN + 128] = p[:, None] == p[None] // 32 * 32 + HD
    c[:, K_ID:K_ID + 128] = np.eye(128)
    c[:, K_CAUS:K_CAUS + 128] = p[:, None] <= p[None]
    diff = np.arange(QL)[None] + WIN - p[:, None]
    c[:, K_BAND:K_BAND + QL] = (diff >= 0) & (diff < WIN)
    rope = np.zeros((2, 2, 128, L), np.float32)
    for n, base in enumerate((1000000.0, 10000.0)):
        inv = 1.0 / np.float32(base) ** (np.arange(0, HD, 2, dtype=np.float32) / HD)
        ang = np.arange(L, dtype=np.float32)[:, None] * inv[None].astype(np.float32)
        cos, sin = np.cos(ang).T, np.sin(ang).T
        d = p % HD
        rope[n, 0] = cos[d // 2]
        rope[n, 1] = sin[d // 2] * np.where(d % 2 == 0, -1.0, 1.0)[:, None]
    sel1 = np.zeros((2, E1, KB1, 128), np.float32)
    for kb in range(KB1):
        sel1[:, 4 * kb + p // 32, kb, p] = 1.0
    sel2 = np.zeros((2 * E2, E2 + 1, 128), np.float32)
    for e in range(E2):
        sel2[e, e, :] = 1.0
    sel2[E2:, E2, :] = 1.0
    first = np.tile(np.arange(E2, 0, -1, dtype=np.float32), (128, NT))
    kept = rope[:, :, :32].reshape(2, 2, 32, 2, CH)
    kept = np.concatenate([kept[:, :, :, n % 2] for n in range(NCH)], 2)
    rope = np.concatenate([rope, kept], 3).transpose(0, 2, 1, 3)
    return {"consts": c, "rope": rope, "sel1": sel1.reshape(128, -1),
            "sel2": sel2.reshape(2 * E2, -1), "first": first}


def lay_out(x):
    a = {}
    a["h_t"] = x["L0_attn_hidden_states"].reshape(T, DM).T
    a["w_in"] = x["L0_attn_in_proj_w"].T
    cw = x["L0_attn_conv_w"].reshape(MH, 128, 4)
    cb = x["L0_attn_conv_b"].reshape(MH, 128, 1)
    ds = x["L0_attn_D_skip"].reshape(MH, 128, 1)
    a["ssm_col"] = np.concatenate([cw, cb, ds], 2).transpose(1, 0, 2).reshape(128, -1)
    a["w_out"] = x["L0_attn_out_proj_w"].T.reshape(MH, 128, DM).transpose(1, 0, 2).reshape(128, -1)
    names = ("L0_attn_A_re", "L0_attn_A_im", "L0_attn_C_re", "L0_attn_C_im")
    by_state = []
    for n in names:
        v = x[n].reshape(MH, 4, 32, NST).transpose(1, 3, 0, 2)
        by_state.append(np.broadcast_to(v[:, None], (4, 2, NST, MH, 32)).reshape(128, 64))
    ld = x["L0_attn_log_dt"].reshape(MH, 4, 32).transpose(1, 0, 2)
    ld = np.broadcast_to(ld[:, None], (4, 32, MH, 32)).reshape(128, 64)
    a["par_state"] = np.concatenate(by_state + [ld], 1)
    by_step = []
    for n in names[:2]:
        v = x[n].reshape(MH, 4, 32, NST).transpose(1, 0, 2, 3)
        by_step.append(np.broadcast_to(v[:, None], (4, 32, MH, 32, NST)).reshape(128, -1))
    a["par_step"] = np.concatenate(by_step, 1)
    a["r1_w"] = x["L0_ffn_router_w"]
    a["r1_b"] = np.broadcast_to(x["L0_ffn_router_b"], (128, E1))
    a["m1_w1"] = np.concatenate([x["L0_ffn_w1"].transpose(1, 0, 2).reshape(DM, -1),
                                 x["L0_ffn_sw1"].transpose(1, 0, 2).reshape(DM, -1)], 1)
    a["m1_b1"] = np.concatenate([x["L0_ffn_b1"].reshape(KB1, 128), x["L0_ffn_sb1"].reshape(KBS, 128)]).T
    w2 = np.concatenate([x["L0_ffn_w2"].reshape(KB1, 128, DM), x["L0_ffn_sw2"].reshape(KBS, 128, DM)])
    a["m1_w2"] = w2.transpose(1, 0, 2).reshape(128, -1)
    a["m1_b2"] = np.concatenate([x["L0_ffn_b2"], x["L0_ffn_sb2"]])
    swap = np.arange(128) ^ 1
    a["norm_w"] = np.stack([x["L1_attn_norm1_w"], x["L1_attn_norm2_w"]], 1)
    for n in "gl":
        wq = x[f"L1_attn_{n}_wq"]
        a[f"{n}_q"] = np.concatenate([wq, wq[:, swap]], 1)
        wo = np.zeros((4, 32, 4, DM), np.float32)
        wo[:, :HD] = x[f"L1_attn_{n}_wo"].reshape(KVH, 4, HD, DM).transpose(0, 2, 1, 3)
        a[f"{n}_o"] = wo.reshape(128, -1)
    up, wk = x["L1_attn_g_k_up"], x["L1_attn_l_wk"]
    a["g_down"] = x["L1_attn_g_kv_down"]
    a["g_kv"] = np.concatenate([up, up[:, swap[:32]], x["L1_attn_g_v_up"]], 1)
    a["l_kv"] = np.concatenate([wk, wk[:, swap[:32]], x["L1_attn_l_wv"]], 1)
    a["r2_w"] = x["L1_ffn_Wr"]
    a["r2_b"] = np.tile(x["L1_ffn_br"], (128, 1))
    a["m2_w1"] = x["L1_ffn_W1"].transpose(1, 0, 2).reshape(DM, -1)
    a["m2_w2"] = x["L1_ffn_W2"].reshape(E2 * 4, 128, DM).transpose(1, 0, 2).reshape(128, -1)
    a.update(constants())
    return {k: np.ascontiguousarray(v) for k, v in a.items()}


def spread(ap, axis, n):
    dims = [list(d) for d in ap.ap]
    return bass.AP(tensor=ap.tensor, offset=ap.offset, ap=dims[:axis] + [[0, n]] + dims[axis:])


def build(nc, dram, out, stages=99):
    f32, f32r, bf16, i32 = (mybir.dt.float32, mybir.dt.float32r, mybir.dt.bfloat16, mybir.dt.int32)
    ALU, ACT, AX = mybir.AluOpType, mybir.ActivationFunctionType, mybir.AxisListType
    ADD, SUB, MUL = ALU.add, ALU.subtract, ALU.mult
    stack = ExitStack()

    def sem(name):
        return stack.enter_context(nc.semaphore(name))

    def sb(name, shape, dt=f32):
        return stack.enter_context(nc.sbuf_tensor(name, shape, dt))

    with stack:
        cst = sb("cst", [128, K_N])
        X = sb("X", [128, T])
        xn = sb("xn", [128, B, LP])
        work = sb("work", [128, 4 * T + 256])
        dev, sq, y0 = (work[:, n * T:(n + 1) * T] for n in range(3))
        wts = {name: sb("w_" + name, list(dram[name].shape)) for name in dram
               if name.split("_")[0] in ("r1", "m1", "norm", "g", "l", "r2", "sel2", "first")
               and name != "m1_w2"}
        two = [stack.enter_context(nc.psum_tensor(f"banks{i}", [128, 2, CH], f32)) for i in range(4)]
        bank = [two[i // 2][:, i % 2, :] for i in range(8)]
        eps = sb("eps", [128, 2])
        ssm_col = sb("ssm_col", [128, MH * 6])
        w_out = sb("w_out", [128, MH * 128])
        with nc.sbuf_tensor("arena", [128, AREA], f32) as arena:
            pass

        def place(at, *shape, dt=f32):
            n = int(np.prod(shape))
            words = n // (2 if dt == bf16 else 1)
            assert at + words <= AREA, (at, shape)
            v = arena[:, at:at + words]
            if dt != f32:
                v = v.bitcast(dt)
            names = "abcd"[:len(shape)]
            return v.rearrange(f"p ({' '.join(names)}) -> p {' '.join(names)}",
                               **{k: s for k, s in zip(names, shape)})

        def place_half(at, *shape):
            names = "abcd"[:len(shape)]
            n = int(np.prod(shape))
            assert at + n <= AREA and at % 8 == 0, (at, shape)
            with ExitStack() as here:
                if at:
                    here.enter_context(nc.sbuf_tensor(f"below_{len(halves)}", [128, at], f32))
                v = here.enter_context(nc.sbuf_tensor(f"half_{len(halves)}", [128, n], f32r))
                halves.append(v)
            return v[:, :].rearrange(f"p ({' '.join(names)}) -> p {' '.join(names)}",
                                     **{k: s for k, s in zip(names, shape)})

        halves = []

        def halve(eng, high, low, value, done):
            link(eng, eng.tensor_copy(high, value))
            eng.tensor_tensor(low, value, high.bitcast(f32), SUB).then_inc(done, 1)

        def product(pe, o, w, x, start, stop):
            (wh, wl), (xh, xl) = w, x
            pe.matmul(o, wh, xh, start=start, stop=False)
            pe.matmul(o, wh, xl, start=False, stop=False)
            return pe.matmul(o, wl, xh, start=False, stop=stop)

        def const(at, n, rows=128):
            return cst[0:rows, at:at + n]

        chain = {}

        def link(eng, ins):
            s = chain[eng.engine]
            s[1] += 1
            ins.then_inc(s[0], 1)
            eng.wait_ge(s[0], s[1])

        for e, n in ((nc.vector, "vector_step"), (nc.scalar, "scalar_step"), (nc.gpsimd, "pool_step")):
            chain[e.engine] = [sem(n), 0]

        consts_in, first_in, par_in, wout_in = sem("consts_in"), sem("first_in"), sem("par_in"), sem("wout_in")
        m1_in, attn_in, m2_in = sem("m1_in"), sem("attn_in"), sem("m2_in")

        resid_ready = sem("resid_ready")
        mean_ready = sem("mean_ready")
        dev_ready = sem("dev_ready")
        square_ready = sem("square_ready")
        var_ready = sem("var_ready")
        guess_ready = sem("guess_ready")
        normed = sem("normed")

        def tok(c):
            return slice(c * CH, (c + 1) * CH)

        def xn_tok(c):
            return xn[:, c // 2, WIN + c % 2 * CH:WIN + (c % 2 + 1) * CH]

        def pe_norm(pe, k, rms):
            if not rms:
                for c in range(NCH):
                    pe.wait_ge(resid_ready, NCH * resid_index[k] + c + 1)
                    pe.matmul(bank[c][:, :], const(K_MEAN, 128), X[:, tok(c)], start=True, stop=True)\
                        .then_inc(mean_ready, 1)
            for c in range(NCH):
                pe.wait_ge(square_ready, NCH * k + c + 1)
                pe.matmul(bank[4 + c][:, :], const(K_MEAN, 128), sq[:, tok(c)], start=True, stop=True)\
                    .then_inc(var_ready, 1)

        def act_norm(act, k, rms):
            for c in range(NCH):
                if rms:
                    if k == 2:
                        act.wait_ge(normed, NCH * k - NCH + c + 1)
                    else:
                        act.wait_ge(resid_ready, NCH * resid_index[k] + c + 1)
                else:
                    act.wait_ge(dev_ready, ln_index[k] * NCH + c + 1)
                act.activation(sq[:, tok(c)], X[:, tok(c)] if rms else dev[:, tok(c)], ACT.Square)\
                    .then_inc(square_ready, 1)
            act.preload_act_table_set(LOG_EXP)
            for c in range(NCH):
                act.wait_ge(var_ready, NCH * k + c + 1)
                link(act, act.activation(y0[:, tok(c)], bank[4 + c][:, :], ACT.Ln,
                                         bias=eps[:, rms:rms + 1]))
                act.activation(y0[:, tok(c)], y0[:, tok(c)], ACT.Exp, scale=-0.5).then_inc(guess_ready, 1)

        def rsqrt_step(dve, guess, square, tmp, eps_value):
            link(dve, dve.scalar_tensor_tensor(tmp, guess, -0.5, guess, MUL, MUL))
            link(dve, dve.scalar_tensor_tensor(tmp, square, eps_value, tmp, ADD, MUL))
            link(dve, dve.scalar_tensor_tensor(guess, tmp, 1.5, guess, ADD, MUL))

        def dve_norm(dve, k, rms):
            if not rms:
                for c in range(NCH):
                    dve.wait_ge(mean_ready, ln_index[k] * NCH + c + 1)
                    dve.tensor_tensor(dev[:, tok(c)], X[:, tok(c)], bank[c][:, :], SUB).then_inc(dev_ready, 1)
            for c in range(NCH):
                dve.wait_ge(guess_ready, NCH * k + c + 1)
                y = y0[:, tok(c)]
                rsqrt_step(dve, y, bank[4 + c][:, :], sq[:, tok(c)], EPS_RMS if rms else EPS_LN)
                if rms:
                    dve.scalar_tensor_tensor(xn_tok(c), X[:, tok(c)], wts["norm_w"][:, k - 2:k - 1], y, MUL, MUL)\
                        .then_inc(normed, 1)
                else:
                    dve.tensor_tensor(X[:, tok(c)], dev[:, tok(c)], y, MUL).then_inc(normed, 1)

        ln_index = {0: 0, 1: 1, 4: 2, 5: 3}
        resid_index = {0: 0, 1: 1, 3: 2, 4: 3, 5: 4}
        eps_set = sem("eps_set")
        sem_out = sem("sem_out")

        h_t = X
        w_in = place(0, 512)
        u = place(0, MH, T)
        at = MH * T
        w_in = place(at, 512); at += 512
        sz = place(at, MH, T); at += MH * T
        xpad = place(at, MH, B, L + 3)
        y_t = place(at, MH, B * NJ, Q); at += MH * B * (L + 3)
        EU = place(at, 64, 32); at += 2048
        EV = place(at, 64, 32); at += 2048
        F1 = place(at, 64, Q + 1); at += 64 * (Q + 1)
        F2 = place(at, 64, Q + 1); at += 64 * (Q + 1)
        TP = place(at, 64, Q); at += 2048
        cos_j = place(at, 64, NJ); at += 2048
        sin_j = place(at, 64, NJ); at += 2048
        rho_g = place(at, GC * B * NJ); at += 512
        pa = place(at, GC * B * NJ); at += 512
        pb_ = place(at, GC * B * NJ); at += 512
        hc = [place(at + 512 * n, GC, B, NJ) for n in range(2)]; at += 1024
        hs = [place(at + 512 * n, GC, B, NJ) for n in range(2)]; at += 1024
        par_state = place(at, 5, 64); at += 320
        small = place(at, 26, 64); at += 26 * 64
        tmpw = [work[:, n * 2112:(n + 1) * 2112] for n in range(4)]
        xq = work[:, 0:MH * T].rearrange("p (m b c) -> p m b c", m=MH, c=32)
        ysb = work[:, MH * T:2 * MH * T].rearrange("p (m b c) -> p m b c", m=MH, c=32)
        par_step = sz
        par_step = place(MH * T + 512 + MH * T, 2, 64, NST)
        kpad = place(0, 64, 64)[0:4]
        kd = nc.dram_tensor("taps", (4, 64, 64), f32, kind="Internal").ap()

        xz_ready, xz_out = sem("xz_ready"), sem("xz_out")
        conv_done, u_ready, xq_ready = sem("conv_done"), sem("u_ready"), sem("xq_ready")
        tables = sem("tables")
        looked_up = sem("looked_up")
        f_ready, e_ready, taps_ready, taps_copied = sem("f_ready"), sem("e_ready"), sem("taps_ready"), sem("taps_copied")
        taps_out, toeplitz_in = sem("taps_out"), sem("toeplitz_in")
        uv_ready, uv_used, state_ready, y_ready, y_copied = (
            sem(n) for n in ("uv_ready", "uv_used", "state_ready", "y_ready", "y_copied"))
        gated, out_ready = sem("gated"), sem("out_ready")
        coef_ready = sem("coef_ready")

        def sp_ssm(sp):
            sp.dma_start(cst[:, :], dram["consts"]).then_inc(consts_in, 16)
            sp.dma_start(par_state, dram["par_state"].rearrange("p (a b) -> p a b", a=5)).then_inc(par_in, 16)
            sp.dma_start(par_step, dram["par_step"].rearrange("p (a b c) -> p a b c", a=2, c=NST)).then_inc(par_in, 16)
            sp.dma_start(h_t[:, :], dram["h_t"]).then_inc(first_in, 16)
            sp.dma_start(w_in, dram["w_in"]).then_inc(first_in, 16)
            sp.dma_start(ssm_col[:, :], dram["ssm_col"]).then_inc(first_in, 16)
            sp.dma_start(w_out[:, :], dram["w_out"]).then_inc(wout_in, 16)
            sp.wait_ge(taps_copied, 5)
            sp.dma_start(kd, kpad[:, :, :]).then_inc(taps_out, 16)
            sp.wait_ge(taps_out, 16)
            for q in range(Q):
                sp.dma_start(TP[q::Q], kd[:, :, Q - 1 - q:2 * Q - 1 - q]).then_inc(toeplitz_in, 16)

        def pe_ssm(pe):
            pe.wait_ge(first_in, 48)
            for m in range(2 * MH):
                for c in range(NCH):
                    n = NCH * m + c
                    if n >= 4:
                        pe.wait_ge(xz_out, n - 3)
                    pe.matmul(bank[n % 4][:, :], w_in[:, 128 * m:128 * m + 128], h_t[:, tok(c)],
                              start=True, stop=True).then_inc(xz_ready, 1)
            pe.wait_ge(f_ready, 1)
            for n in range(4):
                pe.matmul(bank[4 + n][0:4, :], const(K_SEL, 4), F1[:, 16 * n:16 * n + 16, 0:Q],
                          start=True, stop=True).then_inc(taps_ready, 1)
            pe.wait_ge(e_ready, 1)
            pe.wait_ge(xz_out, 16)

            def to_states(k):
                m, c0 = k // 4, GC * (k % 4)
                pe.wait_ge(xq_ready, m + 1)
                if k >= 2:
                    pe.wait_ge(uv_used, k - 1)
                for w, b0 in ((EU, 0), (EV, 2)):
                    for c in range(GC):
                        for g in range(4):
                            r = slice(32 * g, 32 * g + 32)
                            ins = pe.matmul(bank[b0 + k % 2][r, 64 * c:64 * c + 64], w[r, 32 * m + c0 + c, :],
                                            xq[r, m, :, c0 + c], start=True, stop=True)
                ins.then_inc(uv_ready, 1)

            def to_outputs(k):
                m, c0 = k // 4, GC * (k % 4)
                pe.wait_ge(state_ready, k + 1)
                if k == 0:
                    pe.wait_ge(toeplitz_in, 16 * Q)
                    pe.wait_ge(taps_copied, 5)
                if k >= 2:
                    pe.wait_ge(y_copied, k - 1)
                for c in range(GC):
                    mc = 32 * m + c0 + c
                    for g in range(4):
                        r = slice(32 * g, 32 * g + 32)
                        o = bank[4 + k % 2][r, 64 * c:64 * c + 64]
                        pe.matmul(o, TP[r, mc, :], xq[r, m, :, c0 + c], start=True, stop=False)
                    for g in range(4):
                        r = slice(32 * g, 32 * g + 32)
                        o = bank[4 + k % 2][r, 64 * c:64 * c + 64].rearrange("p (b j) -> p b j", b=B)[:, :, 1:NJ]
                        pe.matmul(o, F1[r, mc, 1:Q + 1], hc[k % 2][r, c, :, 0:NJ - 1], start=False, stop=False)
                        ins = pe.matmul(o, F2[r, mc, 1:Q + 1], hs[k % 2][r, c, :, 0:NJ - 1], start=False, stop=True)
                ins.then_inc(y_ready, 1)

            to_states(0)
            for k in range(NG):
                if k + 1 < NG:
                    to_states(k + 1)
                to_outputs(k)
            for c in range(NCH):
                pe.wait_ge(gated, NCH * (MH - 1) + c + 1)
                if c == 0:
                    pe.wait_ge(wout_in, 16)
                    pe.wait_ge(y_copied, NG)
                for m in range(MH):
                    ins = pe.matmul(bank[4 + c][:, :], w_out[:, 128 * m:128 * m + 128], sz[:, m, tok(c)],
                                    start=(m == 0), stop=(m == MH - 1))
                ins.then_inc(out_ready, 1)

        def lookup(act, n, dst, src, func, **kw):
            act.wait_ge(tables, n)
            act.activation(dst, src, func, **kw).then_inc(looked_up, 1)

        def act_ssm(act):
            for n in range(2 * MH * NCH):
                m, c = n // NCH, n % NCH
                act.wait_ge(xz_ready, n + 1)
                if m < MH:
                    d = xpad[:, m, c // 2, 3 + c % 2 * CH:3 + (c % 2 + 1) * CH]
                    if n == 0:
                        act.wait_ge(tables, 4)
                    act.activation(d, bank[n % 4][:, :], ACT.Copy).then_inc(xz_out, 1)
                else:
                    act.activation(sz[:, m - MH, tok(c)], bank[n % 4][:, :], ACT.Silu).then_inc(xz_out, 1)

        (dt2, _a, A2, W2, FR2, K2, P2, S2, SN2, SH2, EA, EM1, NR, NI, DBR, DBI, CR, CI, RHO, p1, p2, t1, t2, t3, DT1, LD1) = (
            small[:, i, :] for i in range(26))
        are, aim, cre, cim, ldt = (par_state[:, i, :] for i in range(5))
        mre, mim, q31 = const(K_MRE, 1), const(K_MIM, 1), const(K_Q31, 1)

        def exact_exp(dve, x, ex, em1, tmp, scale_i):
            k, r, p = tmp
            link(dve, dve.tensor_scalar(x, x, -150.0, 88.0, ALU.max, ALU.min))
            link(dve, dve.tensor_scalar(k, x, LOG2E, MAGIC, MUL, ADD))
            link(dve, dve.tensor_scalar(k, k, MAGIC, None, SUB))
            link(dve, dve.scalar_tensor_tensor(r, k, -LN2H, x, MUL, ADD))
            link(dve, dve.scalar_tensor_tensor(r, k, -LN2L, r, MUL, ADD))
            link(dve, dve.tensor_scalar(p, r, 1 / 5040, None, MUL))
            for co in (1 / 720, 1 / 120, 1 / 24, 1 / 6, 0.5, 1.0):
                link(dve, dve.scalar_tensor_tensor(p, p, co, r, ADD, MUL))
            link(dve, dve.tensor_scalar(scale_i, k, -127.0, 127.0, ALU.max, ADD))
            link(dve, dve.tensor_scalar(scale_i, scale_i, 23, None, ALU.logical_shift_left))
            s = scale_i.bitcast(f32)
            link(dve, dve.tensor_tensor(p, p, s, MUL))
            if em1 is not None:
                link(dve, dve.tensor_scalar(r, s, 1.0, None, SUB))
                link(dve, dve.tensor_tensor(em1, p, r, ADD))
            link(dve, dve.tensor_tensor(ex, p, s, ADD))

        def to_turns(dve, f, w, k):
            link(dve, dve.tensor_scalar(k, w, 1 / (2 * np.pi), MAGIC, MUL, ADD))
            link(dve, dve.tensor_scalar(k, k, MAGIC, None, SUB))
            for part in (C1, C2, C3):
                link(dve, dve.scalar_tensor_tensor(w, k, -part, w, MUL, ADD))
            return dve.tensor_scalar(f, w, 1 / (2 * np.pi), None, MUL)

        def wrap(dve, v, k):
            link(dve, dve.tensor_scalar(k, v, MAGIC, MAGIC, ADD, SUB))
            link(dve, dve.tensor_tensor(v, v, k, SUB))

        def dve_tables(dve):
            dve.memset(eps[:, 0:1], EPS_LN).then_inc(eps_set, 1)
            dve.memset(eps[:, 1:2], EPS_RMS).then_inc(eps_set, 1)
            dve.memset(kpad[:, :, :], 0.0).then_inc(taps_copied, 1)
            for side in (slice(0, WIN), slice(WIN + L, LP)):
                dve.memset(xn[:, :, side], 0.0)
            dve.wait_ge(consts_in, 16)
            dve.wait_ge(par_in, 32)
            ei = work[:, 0:64].bitcast(i32)
            tmp = [work[:, 256 + 128 * i:256 + 128 * i + 64] for i in range(3)]
            link(dve, dve.tensor_copy(t1, ldt))
            exact_exp(dve, t1, dt2, None, tmp, ei)
            link(dve, dve.tensor_tensor(A2, dt2, are, MUL))
            link(dve, dve.tensor_tensor(W2, dt2, aim, MUL))
            link(dve, dve.tensor_copy(t1, A2))
            exact_exp(dve, t1, EA, EM1, tmp, ei)
            link(dve, dve.tensor_scalar(t1, A2, float(Q), None, MUL))
            exact_exp(dve, t1, RHO, None, tmp, ei)
            to_turns(dve, FR2, W2, t1).then_inc(tables, 1)
            dve.wait_ge(tables, 1)
            a1, f1, v1, k1 = (w[:, 0:1024].rearrange("p (c n) -> p c n", n=NST) for w in tmpw)
            mag1, s1, h1 = (w[:, 1024:2048].rearrange("p (c n) -> p c n", n=NST) for w in tmpw[:3])
            dtb = spread(dt2, 2, NST)
            link(dve, dve.tensor_tensor(a1, par_step[:, 0], dtb, MUL))
            dve.tensor_tensor(f1, par_step[:, 1], dtb, MUL).then_inc(tables, 1)
            dve.wait_ge(tables, 2)
            link(dve, to_turns(dve, f1, f1, k1))
            link(dve, dve.tensor_scalar(v1, f1, q31, None, MUL))
            link(dve, dve.tensor_scalar(k1, v1, MAGIC, MAGIC, ADD, SUB))
            dve.tensor_tensor(v1, v1, k1, SUB).then_inc(tables, 1)
            dve.memset(xpad[:, :, :, 0:3], 0.0).then_inc(tables, 1)
            dve.wait_ge(tables, 4)
            dve.wait_ge(looked_up, 2)
            link(dve, dve.scalar_tensor_tensor(t1, SH2, -2.0, SH2, MUL, MUL))
            link(dve, dve.tensor_tensor(t1, t1, EA, MUL))
            link(dve, dve.tensor_tensor(NR, t1, EM1, ADD))
            link(dve, dve.tensor_tensor(NI, EA, SN2, MUL))
            link(dve, dve.tensor_tensor(t1, are, are, MUL))
            link(dve, dve.tensor_tensor(t2, aim, aim, MUL))
            link(dve, dve.tensor_tensor(t1, t1, t2, ADD))
            link(dve, dve.reciprocal(t3, t1))

            def cmul(re, im, ar, ai, br, bi, conj):
                link(dve, dve.tensor_tensor(t1, ar, br, MUL))
                link(dve, dve.tensor_tensor(t2, ai, bi, MUL))
                link(dve, dve.tensor_tensor(re, t1, t2, ADD if conj else SUB))
                link(dve, dve.tensor_tensor(t1, ai, br, MUL))
                link(dve, dve.tensor_tensor(t2, ar, bi, MUL))
                link(dve, dve.tensor_tensor(im, t1, t2, SUB if conj else ADD))

            cmul(DBR, DBI, NR, NI, are, aim, True)
            link(dve, dve.tensor_tensor(DBR, DBR, t3, MUL))
            link(dve, dve.tensor_tensor(DBI, DBI, t3, MUL))
            cmul(CR, CI, DBR, DBI, cre, cim, False)
            link(dve, dve.tensor_scalar(t1, CI, mim, -2.0, MUL, MUL))
            link(dve, dve.tensor_scalar(t2, CR, mre, 2.0, MUL, MUL))
            link(dve, dve.tensor_tensor(p1, t1, t2, ADD))
            link(dve, dve.tensor_scalar(t1, CI, mre, -2.0, MUL, MUL))
            link(dve, dve.tensor_scalar(t2, CR, mim, -2.0, MUL, MUL))
            link(dve, dve.tensor_tensor(p2, t1, t2, ADD))
            dve.wait_ge(looked_up, 5)
            link(dve, dve.scalar_tensor_tensor(h1, h1, -2.0, h1, MUL, MUL))
            link(dve, dve.scalar_tensor_tensor(EU[:, :, 0:NST], h1, 1.0, mag1, ADD, MUL))
            link(dve, dve.tensor_tensor(EU[:, :, NST:], s1, mag1, MUL))
            link(dve, dve.tensor_scalar(EV[:, :, NST:], EU[:, :, 0:NST], -1.0, None, MUL))
            dve.tensor_copy(EV[:, :, 0:NST], EU[:, :, NST:]).then_inc(e_ready, 1)
            dve.wait_ge(e_ready, 1)
            v2, m2, s2, h2 = (w.rearrange("p (c l) -> p c l", l=Q + 1) for w in tmpw)
            lrow = spread(const(K_LROW, Q + 1), 1, 64)
            dve.tensor_tensor(m2, spread(A2, 2, Q + 1), lrow, MUL).then_inc(tables, 1)
            link(dve, dve.tensor_tensor(v2, spread(FR2, 2, Q + 1), lrow, MUL))
            link(dve, dve.tensor_scalar(s2, v2, MAGIC, MAGIC, ADD, SUB))
            dve.tensor_tensor(v2, v2, s2, SUB).then_inc(tables, 1)
            jrow = spread(const(K_JROW, NJ), 1, 64)
            link(dve, dve.tensor_tensor(sin_j, spread(FR2, 2, NJ), jrow, MUL))
            link(dve, dve.tensor_scalar(cos_j, sin_j, MAGIC, MAGIC, ADD, SUB))
            dve.tensor_tensor(sin_j, sin_j, cos_j, SUB).then_inc(tables, 1)
            dve.wait_ge(looked_up, 8)
            link(dve, dve.scalar_tensor_tensor(h2, h2, -2.0, h2, MUL, MUL))
            link(dve, dve.scalar_tensor_tensor(h2, h2, 1.0, m2, ADD, MUL))
            link(dve, dve.tensor_tensor(s2, s2, m2, MUL))
            P1, P2b = spread(p1, 2, Q + 1), spread(p2, 2, Q + 1)
            link(dve, dve.tensor_tensor(F1, h2, P1, MUL))
            link(dve, dve.tensor_tensor(m2, s2, P2b, MUL))
            dve.tensor_tensor(F1, F1, m2, ADD).then_inc(f_ready, 1)
            link(dve, dve.tensor_tensor(F2, h2, P2b, MUL))
            dve.wait_ge(f_ready, 1)
            link(dve, dve.tensor_tensor(m2, s2, P1, MUL))
            link(dve, dve.tensor_tensor(F2, F2, m2, SUB))
            for n in range(4):
                dve.wait_ge(taps_ready, n + 1)
                dve.tensor_copy(kpad[:, 16 * n:16 * n + 16, Q - 1:2 * Q - 1],
                                bank[4 + n][0:4, :].rearrange("p (c l) -> p c l", l=Q)).then_inc(taps_copied, 1)
            dve.wait_ge(looked_up, 10)
            link(dve, dve.scalar_tensor_tensor(cos_j, cos_j, -2.0, cos_j, MUL, MUL))
            link(dve, dve.tensor_scalar(cos_j, cos_j, 1.0, None, ADD))

        def act_tables(act):
            a1, f1, v1 = (w[:, 0:1024].rearrange("p (c n) -> p c n", n=NST) for w in tmpw[:3])
            mag1, s1, h1 = (w[:, 1024:2048].rearrange("p (c n) -> p c n", n=NST) for w in tmpw[:3])
            lookup(act, 1, SN2, FR2, ACT.Sin, scale=TWO_PI)
            lookup(act, 1, SH2, FR2, ACT.Sin, scale=TWO_PI / 2)
            lookup(act, 3, s1, v1, ACT.Sin, scale=TWO_PI)
            lookup(act, 3, h1, v1, ACT.Sin, scale=TWO_PI / 2)
            lookup(act, 3, mag1, a1, ACT.Exp, scale=q31)

        def act_tables2(act):
            v2, m2, s2, h2 = (w.rearrange("p (c l) -> p c l", l=Q + 1) for w in tmpw)
            lookup(act, 6, m2, m2, ACT.Exp)
            lookup(act, 6, s2, v2, ACT.Sin, scale=TWO_PI)
            lookup(act, 6, h2, v2, ACT.Sin, scale=TWO_PI / 2)
            act.wait_ge(tables, 7)
            act.activation(cos_j, sin_j, ACT.Sin, scale=TWO_PI / 2).then_inc(looked_up, 1)
            act.wait_ge(looked_up, 9)
            act.activation(sin_j, sin_j, ACT.Sin, scale=TWO_PI).then_inc(looked_up, 1)

        def dve_ssm(dve):
            dve.wait_ge(taps_out, 16)
            for m in range(MH):
                for b in range(B):
                    n = B * m + b
                    dve.wait_ge(xz_out, NCH * m + 2 * b + 2)
                    o = u[:, m, L * b:L * b + L]
                    col = ssm_col[:, 6 * m:6 * m + 6]
                    link(dve, dve.tensor_scalar(o, xpad[:, m, b, 0:L], col[:, 0:1], None, MUL))
                    for k in range(1, 4):
                        ins = dve.scalar_tensor_tensor(o, xpad[:, m, b, k:k + L], col[:, k:k + 1], o, MUL, ADD)
                        if k < 3:
                            link(dve, ins)
                    ins.then_inc(conv_done, 1)
            for m in range(MH):
                dve.wait_ge(u_ready, B * (m + 1))
                dve.transpose(xq[:, m].rearrange("p b c -> p (b c)"), u[:, m, :]).then_inc(xq_ready, 1)
            for k in range(NG):
                m, c0 = k // 4, GC * (k % 4)
                cj = spread(cos_j[:, 32 * m + c0:32 * m + c0 + GC, :], 2, B)
                sj = spread(sin_j[:, 32 * m + c0:32 * m + c0 + GC, :], 2, B)
                g4 = "p (c b j) -> p c b j"
                pa4, pb4 = pa.rearrange(g4, c=GC, b=B), pb_.rearrange(g4, c=GC, b=B)
                rho4 = rho_g.rearrange("p (c b j) -> p c (b j)", c=GC, b=B)
                link(dve, dve.tensor_copy(rho4, spread(RHO[:, 32 * m + c0:32 * m + c0 + GC], 2, B * NJ)))
                dve.wait_ge(uv_ready, k + 1)
                link(dve, dve.tensor_tensor(pa4, bank[k % 2][:, :].rearrange(g4, c=GC, b=B), cj, MUL))
                link(dve, dve.memset(rho_g.rearrange("p (s j) -> p s j", j=NJ)[:, :, 0:1], 0.0))
                dve.tensor_tensor(pb4, bank[2 + k % 2][:, :].rearrange(g4, c=GC, b=B), sj, MUL).then_inc(uv_used, 1)
                dve.wait_ge(uv_used, k + 1)
                link(dve, dve.tensor_tensor(pa, pa, pb_, ADD))
                link(dve, dve.tensor_tensor_scan(pb_, rho_g, pa, 0.0, MUL, ADD))
                if k >= 2:
                    dve.wait_ge(y_ready, k - 1)
                link(dve, dve.tensor_tensor(hc[k % 2], pb4, cj, MUL))
                dve.tensor_tensor(hs[k % 2], pb4, sj, MUL).then_inc(state_ready, 1)
            for m in range(MH):
                dve.wait_ge(y_copied, 4 * (m + 1))
                link(dve, dve.transpose(y_t[:, m].rearrange("p b c -> p (b c)"),
                                        ysb[:, m].rearrange("p b c -> p (b c)")))
                yt = y_t[:, m].rearrange("p b c -> p (b c)")
                for c in range(NCH):
                    link(dve, dve.scalar_tensor_tensor(yt[:, tok(c)], u[:, m, tok(c)], ssm_col[:, 6 * m + 5:6 * m + 6],
                                                       yt[:, tok(c)], MUL, ADD))
                    dve.tensor_tensor(sz[:, m, tok(c)], yt[:, tok(c)], sz[:, m, tok(c)], MUL).then_inc(gated, 1)
            for c in range(NCH):
                dve.wait_ge(out_ready, c + 1)
                dve.tensor_tensor(X[:, tok(c)], h_t[:, tok(c)], bank[4 + c][:, :], ADD).then_inc(resid_ready, 1)

        def act_ssm2(act):
            for n in range(MH * B):
                m, b = n // B, n % B
                act.wait_ge(conv_done, n + 1)
                o = u[:, m, L * b:L * b + L]
                act.activation(o, o, ACT.Silu, bias=ssm_col[:, 6 * m + 4:6 * m + 5]).then_inc(u_ready, 1)
            for k in range(NG):
                m, c0 = k // 4, GC * (k % 4)
                act.wait_ge(y_ready, k + 1)
                act.activation(ysb[:, m, :, c0:c0 + GC],
                               bank[4 + k % 2][:, :].rearrange("p (c t) -> p t c", c=GC), ACT.Copy).then_inc(y_copied, 1)

        logits = place(0, NT, E1)
        kept = place(1024, NT, E1)
        cw2 = place(2048, NT, 2, E1)
        best = place(4096, NT, 8)
        rowv = place(4224, 3, NT)
        cwt = place(4352, T)
        cw_halves = place_half(6400, T)
        hid = [place(8448 + CH * n, CH) for n in range(3)]
        hidw = [place(9984 + CH * n, CH) for n in range(3)]
        W0 = -(-(MH * T * 2 + 512 + MH * B * (L + 3)) // 8) * 8
        NB1 = KB1 + KBS
        m1_w2 = place(W0, NB1, 128)
        sel1_f = place(W0 + 128 * NB1, KB1, 128)
        W0 += 128 * (NB1 + KB1)
        sel1 = place_half(W0, KB1, 128)
        W0 += 128 * KB1
        w1_halves = [place_half(W0 + 128 * NB1 * n, NB1, 128) for n in range(2)]
        W0 += 128 * NB1 * 2
        w2_halves = [place_half(W0, NB1, 128), place_half(W0 - 128 * (NB1 * 3 + KB1 * 2), NB1, 128)]
        W0 += 128 * NB1
        x_halves = [[place_half(W0 + CH * (2 * n + a), CH) for a in range(2)] for n in range(2)]
        h_halves = [[place_half(W0 + 2048 + CH * (2 * n + a), CH) for a in range(2)] for n in range(3)]
        m1_w1, m1_b1 = wts["m1_w1"], wts["m1_b1"]
        shared, routed = list(range(KB1, NB1)), list(range(KB1))
        steps1 = [(c, kb) for c in (0, 1) for kb in shared] + [(c, kb) for c in (0, 1) for kb in routed]
        steps1 += [(c, kb) for c in (2, 3) for kb in shared + routed]
        before = [sum(kb < KB1 for c, kb in steps1[:n]) for n in range(len(steps1) + 1)]
        FIRST1 = 2 * KBS
        first_of = [steps1.index((c, KB1)) for c in range(NCH)]
        last_of = [max(n for n, s in enumerate(steps1) if s[0] == c) for c in range(NCH)]
        w_groups = [KB1] + list(range(0, KB1, 4))
        w_split, x_split, high_done, split_done = (
            sem(n) for n in ("w_split", "x_split", "hidden_high", "hidden_split"))
        route_ready, cw_ready, cwt_ready, cwt_split = (
            sem(n) for n in ("route_ready", "cw_ready", "cwt_ready", "cwt_split"))
        soft_in, soft_out = sem("soft_in"), sem("soft_out")
        up_ready, silu_done, spread_ready, scaled, m1_out, sel_cast = (
            sem(n) for n in ("up_ready", "silu_done", "spread_ready", "scaled", "m1_out", "sel_cast"))
        late_in = sem("late_in")

        def sp_moe1(sp):
            names = [n for n in wts]
            for n in names:
                sp.dma_start(wts[n][:, :], dram[n]).then_inc(m1_in, 16)
            sp.wait_ge(y_ready, NG)
            sp.dma_start(m1_w2, dram["m1_w2"].rearrange("p (a b) -> p a b", b=128)).then_inc(late_in, 16)
            sp.dma_start(sel1_f, dram["sel1"].rearrange("p (a b) -> p a b", b=128)).then_inc(late_in, 16)

        def pe_moe1(pe):
            pe.wait_ge(m1_in, 16 * len(wts))
            for t in range(NT):
                pe.wait_ge(normed, t // 4 + 1)
                ins = pe.matmul(bank[t // 8][:, 64 * (t % 8):64 * (t % 8) + 64], X[:, 128 * t:128 * t + 128],
                                wts["r1_w"][:, :], start=True, stop=True)
                if t % 8 == 7:
                    ins.then_inc(route_ready, 1)

            def turn(g):
                if g == 0:
                    pe.wait_ge(cw_ready, 1)
                if g >= 2:
                    pe.wait_ge(cwt_split, g - 1)
                for t in range(4 * g, 4 * g + 4):
                    ins = pe.transpose(bank[3 + g % 2][:, 128 * (t % 4):128 * (t % 4) + 128],
                                       cw2[:, t].rearrange("p a e -> p (a e)"), const(K_ID, 128))
                ins.then_inc(cwt_ready, 1)

            def up(n):
                c, kb = steps1[n]
                if n < 3:
                    pe.wait_ge(soft_in, 1)
                if n >= 3:
                    pe.wait_ge(silu_done, n - 2)
                pe.wait_ge(x_split, c + 1)
                pe.wait_ge(w_split, 2 * w_groups.index(kb // 4 * 4) + 1)
                product(pe, bank[n % 3][:, :], [w[:, kb] for w in w1_halves], x_halves[c % 2], True, True)\
                    .then_inc(up_ready, 1)
                if kb < KB1:
                    r = before[n]
                    if r == 0:
                        for g in range(NCH):
                            turn(g)
                        pe.wait_ge(cwt_split, NCH)
                        pe.wait_ge(sel_cast, 1)
                    if r >= 3:
                        pe.wait_ge(scaled, r - 2)
                    pe.matmul(bank[3 + r % 3][:, :], sel1[:, kb, :], cw_halves[:, tok(c)], start=True, stop=True)\
                        .then_inc(spread_ready, 1)

            def down(n):
                c, kb = steps1[n]
                if n == first_of[c] and c >= 2:
                    pe.wait_ge(resid_ready, NCH + c - 1)
                if n == 0:
                    pe.wait_ge(normed, NCH)
                pe.wait_ge(w_split, 2 * w_groups.index(kb // 4 * 4) + 2)
                pe.wait_ge(split_done, n + 1)
                product(pe, bank[6 + c % 2][:, :], [w[:, kb] for w in w2_halves], h_halves[n % 3],
                        n == first_of[c], False).then_inc(down_done, 1)
                if n == last_of[c]:
                    pe.matmul(bank[6 + c % 2][:, :], wts["m1_b2"][:, :], cwt[0:E1 + ES, tok(c)],
                              start=False, stop=True).then_inc(m1_out, 1)

            for n in range(3):
                up(n)
            for n in range(len(steps1)):
                if n + 3 < len(steps1):
                    up(n + 3)
                down(n)

        def pool_moe1(pool):
            pool.wait_ge(m1_in, 16 * len(wts))
            pool.wait_ge(late_in, 32)
            w1 = m1_w1[:, :].rearrange("p (a b) -> p a b", b=128)
            for n, g in enumerate(w_groups):
                r = slice(g, g + 4)
                halve(pool, w1_halves[0][:, r], w1_halves[1][:, r], w1[:, r], w_split)
                halve(pool, w2_halves[0][:, r], w2_halves[1][:, r], m1_w2[:, r], w_split)
            pool.tensor_copy(sel1, sel1_f).then_inc(sel_cast, 1)
            for c in range(NCH):
                pool.wait_ge(normed, c + 1)
                if c >= 2:
                    pool.wait_ge(up_ready, last_of[c - 2] + 1)
                halve(pool, x_halves[c % 2][0], x_halves[c % 2][1], X[:, tok(c)], x_split)
                if c == 1:
                    for n in range(FIRST1):
                        low_half(pool, n)

        def low_half(eng, n):
            kb = steps1[n][1]
            if kb < KB1:
                eng.wait_ge(high_done, before[n] + 1)
            else:
                eng.wait_ge(silu_done, n + 1)
            if n >= 3:
                eng.wait_ge(down_done, n - 2)
            high, low = h_halves[n % 3]
            eng.tensor_tensor(low, (hidw if kb < KB1 else hid)[n % 3], high.bitcast(f32), SUB)\
                .then_inc(split_done, 1)

        def act_moe1(act):
            act.wait_ge(soft_in, 2)
            act.activation(logits, logits, ACT.Exp).then_inc(soft_out, 1)
            for n in range(len(steps1) + 1):
                if n < len(steps1):
                    c, kb = steps1[n]
                    act.wait_ge(up_ready, n + 1)
                    b1 = m1_b1[:, kb:kb + 1]
                    if n >= 3:
                        if steps1[n - 3][1] < KB1:
                            act.wait_ge(scaled, before[n - 2])
                        else:
                            act.wait_ge(split_done, n - 2)
                    ins = act.activation(hid[n % 3], bank[n % 3][:, :], ACT.Silu, bias=b1)
                    if kb >= KB1:
                        if n >= 3:
                            act.wait_ge(down_done, n - 2)
                        ins = act.activation(h_halves[n % 3][0], bank[n % 3][:, :], ACT.Silu, bias=b1)
                    ins.then_inc(silu_done, 1)
                if n >= 1 and steps1[n - 1][1] < KB1:
                    m = n - 1
                    act.wait_ge(scaled, before[m] + 1)
                    act.wait_ge(down_done, m - 2)
                    act.activation(h_halves[m % 3][0], hidw[m % 3], ACT.Copy).then_inc(high_done, 1)

        down_done = sem("down_done")

        def dve_moe1(dve):
            dve.wait_ge(m1_in, 16 * len(wts))
            for h in range(2):
                dve.wait_ge(route_ready, h + 1)
                ins = dve.tensor_tensor(logits[:, 8 * h:8 * h + 8], bank[h][:, :].rearrange("p (t e) -> p t e", e=E1),
                                        spread(wts["r1_b"][:, :], 1, 8), ADD)
                if h == 0:
                    link(dve, ins)
            ins.then_inc(soft_in, 1)
            dve.wait_ge(soft_in, 1)
            link(dve, dve.tensor_reduce(rowv[:, 0], logits, AX.X, ALU.max))
            dve.tensor_tensor(logits, logits, spread(rowv[:, 0], 2, E1), SUB).then_inc(soft_in, 1)
            link(dve, dve.memset(cwt[64:96, :], 1.0))
            dve.wait_ge(soft_out, 1)
            for t in range(NT):
                ins = dve.max(best[:, t], logits[:, t])
            link(dve, ins)
            for t in range(NT):
                ins = dve.match_replace(kept[:, t], best[:, t], logits[:, t], 0.0)
            link(dve, ins)
            link(dve, dve.tensor_tensor(kept, logits, kept, SUB))
            link(dve, dve.tensor_reduce(rowv[:, 1], kept, AX.X, ADD))
            link(dve, dve.reciprocal(rowv[:, 2], rowv[:, 1]))
            link(dve, dve.tensor_tensor(cw2[:, :, 0], kept, spread(rowv[:, 2], 2, E1), MUL))
            dve.tensor_copy(cw2[:, :, 1], cw2[:, :, 0]).then_inc(cw_ready, 1)
            for g in range(NCH):
                dve.wait_ge(cwt_ready, g + 1)
                w, o = bank[3 + g % 2], cw_halves[:, tok(g)]
                dve.tensor_copy(cwt[0:64, tok(g)], w[0:64, :])
                link(dve, dve.tensor_copy(o, w[:, :]))
                dve.tensor_tensor(o[64:128], w[64:128, :], o[64:128].bitcast(f32), SUB).then_inc(cwt_split, 1)

            def result(c):
                dve.wait_ge(m1_out, c + 1)
                dve.tensor_tensor(X[:, tok(c)], X[:, tok(c)], bank[6 + c % 2][:, :], ADD).then_inc(resid_ready, 1)

            N = len(steps1)
            for n in range(N + 5):
                if n < N and steps1[n][1] < KB1:
                    dve.wait_ge(silu_done, n + 1)
                    dve.wait_ge(spread_ready, before[n] + 1)
                    dve.wait_ge(split_done, n - 2)
                    dve.tensor_tensor(hidw[n % 3], hid[n % 3], bank[3 + before[n] % 3][:, :], MUL).then_inc(scaled, 1)
                if n == FIRST1:
                    dve.wait_ge(split_done, FIRST1)
                if FIRST1 < n <= N:
                    low_half(dve, n - 1)
                if n - 5 in last_of:
                    result(last_of.index(n - 5))

        q9 = [place(8448 * b, H, NL * QL, dt=bf16) for b in range(B)]
        k9 = [place(16896 + 2176 * b, KVH, LP, dt=bf16) for b in range(B)]
        vt = place(21248, B * NL, KVH, 32)
        rope = place(24064, 2, L + CH)
        parts = [place(27136 + 768 * n, 3, CH, dt=bf16) for n in range(3)]
        rot = [work[:, CH * n:CH * n + CH] for n in range(5)]
        rot2, rtm = work[:, CH * 5:CH * 6], work[:, CH * 6:CH * 7]
        rsq = [work[:, CH * n:CH * n + CH] for n in (7, 8)]
        rgs = [work[:, CH * n:CH * n + CH] for n in (9, 10)]
        lat = work[0:LAT, CH * 12:CH * 16]
        RING = 6
        probs = [work[:, 2 * CH * n:2 * CH * n + 2 * CH] for n in range(RING)]
        osb = [work[:, CH * n:CH * n + CH] for n in (12, 13)]
        onrm = [work[:, CH * n:CH * n + CH] for n in (14, 15)]
        rec, rec2 = [place(29440, CH), place(27136 + CH, CH)], place(27136, CH)
        q_dram = [nc.dram_tensor(f"q_parts{n}", (3, 128, T), bf16, kind="Internal").ap() for n in range(2)]
        k_dram = [nc.dram_tensor(f"k_parts{n}", (3, 32, T), bf16, kind="Internal").ap() for n in range(2)]
        lat_ready, lat_copied, v_ready, v_copied = (sem(n) for n in ("lat_ready", "lat_copied", "v_ready", "v_copied"))
        rope_in, pr_ready, rot_ready, rsq_ready, ms_ready, gs_ready, parts_ready = (
            sem(n) for n in ("rope_in", "pr_ready", "rot_ready", "rsq_ready", "ms_ready", "gs_ready", "parts_ready"))
        parts_out = [sem(f"parts_out{n}") for n in range(3)]
        in9 = [sem(f"relayout_in{b}") for b in range(B)]
        pads = sem("pads")
        normed9, high_ready, rest_ready, mid_ready = (
            sem(n) for n in ("item_normed", "high_ready", "rest_ready", "mid_ready"))
        x_in = place(30000, T)
        x_kept, x_added = sem("x_kept"), sem("x_added")

        def pool_attn(pool):
            pool.wait_ge(x_split, NCH)
            pool.wait_ge(normed, 2 * NCH)
            for b in range(B):
                link(pool, pool.memset(arena[64:128, 8448 * b:8448 * b + 8448], 0.0))
                link(pool, pool.memset(arena[64:128, 16896 + 2176 * b:16896 + 2176 * b + 2176], 0.0))
                pool.memset(k9[b][0:64, :, 0:WIN], 0.0)
                pool.memset(k9[b][0:64, :, WIN + L:LP], 0.0)
                pool.memset(q9[b][0:64, :, L:NL * QL], 0.0).then_inc(pads, 1)
                pool.wait_ge(pads, b + 1)
            for c in range(NCH):
                pool.tensor_copy(x_in[:, tok(c)], X[:, tok(c)]).then_inc(x_kept, 1)
            pool_parts(pool, 0)
            for c in range(NCH):
                pool.wait_ge(x_kept, c + 1)
                pool.wait_ge(normed, NCH * 3 + c + 1)
                pool.tensor_tensor(X[:, tok(c)], X[:, tok(c)], x_in[:, tok(c)], ADD).then_inc(x_added, 1)
            pool_parts(pool, 1)
            pool_core(pool)

        def pool_parts(pool, n):
            for i in range(NIT + 1):
                if i < NIT:
                    j = NIT * n + i
                    pool.wait_ge(high_ready, j + 1)
                    pool.tensor_tensor(rot[i], rot[i], parts[slot_of[j]][:, 0], SUB).then_inc(rest_ready, 1)
                if i >= 1:
                    j = NIT * n + i - 1
                    pool.wait_ge(mid_ready, j + 1)
                    pool.tensor_tensor(parts[slot_of[j]][:, 2], rot[i - 1], parts[slot_of[j]][:, 1], SUB)\
                        .then_inc(parts_ready, 1)
        scores_ready, exp_done, masked, pv_done, guessed = (
            sem(n) for n in ("scores_ready", "exp_done", "masked", "pv_done", "den_guessed"))
        masked_by_pool, den_read = sem("masked_by_pool"), sem("den_read")
        osb_ready, den_ready, on_ready, wo_ready, added = (
            sem(n) for n in ("osb_ready", "den_ready", "on_ready", "wo_ready", "added"))
        NIT = 1 + NCH
        sends = [KVH if i == 0 else 1 for i in range(NIT)] * 2
        slot_of = [j % 3 for j in range(2 * NIT)]

        def sent(j):
            return 16 * sum(sends[m] for m in range(j + 1) if slot_of[m] == slot_of[j])

        def item_banks(i):
            return [(4, 5), (2, 3), (0, 1), (2, 3), (0, 1)][i]

        def sp_attn(sp, n):
            if n == 0:
                sp.wait_ge(normed, 2 * NCH)
            else:
                sp.wait_ge(parts_ready, NIT)
            sp.dma_start(rope, dram["rope"][n]).then_inc(rope_in, 16)
            for i in range(NIT):
                j = NIT * n + i
                sp.wait_ge(parts_ready, j + 1)
                p = parts[slot_of[j]]
                if i == 0:
                    for c in range(NCH):
                        sp.dma_start(k_dram[n][:, :, tok(c)].rearrange("a r t -> r a t"), p[32 * c:32 * c + 32])\
                            .then_inc(parts_out[slot_of[j]], 16)
                else:
                    sp.dma_start(q_dram[n][:, :, tok(i - 1)].rearrange("a r t -> r a t"), p)\
                        .then_inc(parts_out[slot_of[j]], 16)
                if i in (2, 4):
                    b = i // 2 - 1
                    for m in range(NIT * n, j + 1):
                        sp.wait_ge(parts_out[slot_of[m]], sent(m))
                    sp.wait_ge(pads, b + 1)
                    if n == 1 and b == 0:
                        sp.wait_ge(pv_done, UG)
                    for a in range(3):
                        for c in range(3):
                            r = slice((3 * a + c) * HD, (3 * a + c) * HD + HD)
                            sp.dma_start(q9[b][r, :, 0:L], q_dram[n][c, :, L * b:L * b + L]
                                         .rearrange("(h d) t -> d h t", d=HD)).then_inc(in9[b], 16)
                            sp.dma_start(k9[b][r, :, WIN:WIN + L], k_dram[n][a, :, L * b:L * b + L]
                                         .rearrange("(h d) t -> d h t", d=HD)).then_inc(in9[b], 16)

        def v_tiles(n):
            return [(b, i) for b in range(B) for i in range(NL if n else NQT)]

        def pe_proj(pe, n):
            kv, q = (wts["g_kv"], wts["g_q"]) if n == 0 else (wts["l_kv"], wts["l_q"])
            for c in range(NCH):
                pe.wait_ge(normed, NCH * (2 + n) + c + 1)
                if n == 0:
                    if c >= 2:
                        pe.wait_ge(lat_copied, c - 1)
                    pe.matmul(bank[c % 2][0:LAT, :], wts["g_down"][:, :], xn_tok(c), start=True, stop=True)\
                        .then_inc(lat_ready, 1)
            if n == 0:
                pe.wait_ge(lat_copied, NCH)
            for t, (b, i) in enumerate(v_tiles(n)):
                l = lat[:, (NQT * b + i) * 128:(NQT * b + i) * 128 + 128] if n == 0 else xn[:, b, QL * i:QL * i + 128]
                ins = pe.matmul(bank[t // 16][:, 32 * (t % 16):32 * (t % 16) + 32], l, kv[:, 64:96],
                                start=True, stop=True)
            ins.then_inc(v_ready, 1)

            def project(i):
                j = NIT * n + i
                b0, b1 = item_banks(i)
                if i == 2:
                    pe.wait_ge(v_copied, n + 1)
                if i >= 3:
                    pe.wait_ge(rot_ready, j - 1)
                if i == 0:
                    for w, bk in ((0, b0), (32, b1)):
                        for c in range(NCH):
                            x = lat[:, tok(c)] if n == 0 else xn_tok(c)
                            ins = pe.matmul(bank[bk][32 * c:32 * c + 32, :], kv[:, w:w + 32], x, start=True, stop=True)
                else:
                    for w, bk in ((0, b0), (128, b1)):
                        ins = pe.matmul(bank[bk][:, :], q[:, w:w + 128], xn_tok(i - 1), start=True, stop=True)
                ins.then_inc(pr_ready, 1)

            def mean_square(i):
                j = NIT * n + i
                pe.wait_ge(rsq_ready, j + 1)
                if i >= 2:
                    pe.wait_ge(normed9, j - 1)
                pe.matmul(bank[6 + i % 2][:, :], const(K_HEAD, 128), rsq[i % 2], start=True, stop=True)\
                    .then_inc(ms_ready, 1)

            project(0)
            project(1)
            project(2)
            for i in range(NIT):
                mean_square(i)
                if i + 3 < NIT:
                    project(i + 3)

        def act_proj(act, n):
            if n == 0:
                for c in range(NCH):
                    act.wait_ge(lat_ready, c + 1)
                    act.activation(lat[:, tok(c)], bank[c % 2][0:LAT, :], ACT.Copy).then_inc(lat_copied, 1)

            def squares(i):
                j = NIT * n + i
                act.wait_ge(rot_ready, j + 1)
                if i >= 2:
                    act.wait_ge(ms_ready, j - 1)
                act.activation(rsq[i % 2], rot[i], ACT.Square).then_inc(rsq_ready, 1)

            def part(i, m):
                j = NIT * n + i
                act.wait_ge((normed9, rest_ready)[m], j + 1)
                if m == 0 and j >= 3:
                    act.wait_ge(parts_out[slot_of[j]], sent(j - 3))
                act.activation(parts[slot_of[j]][:, m], rot[i], ACT.Copy).then_inc((high_ready, mid_ready)[m], 1)

            squares(0)
            squares(1)
            for i in range(NIT + 2):
                if i < NIT:
                    j = NIT * n + i
                    act.wait_ge(ms_ready, j + 1)
                    if i >= 2:
                        act.wait_ge(normed9, j - 1)
                    link(act, act.activation(rgs[i % 2], bank[6 + i % 2][:, :], ACT.Ln, bias=eps[:, 1:2]))
                    act.activation(rgs[i % 2], rgs[i % 2], ACT.Exp, scale=-0.5).then_inc(gs_ready, 1)
                if i + 2 < NIT:
                    squares(i + 2)
                if 1 <= i <= NIT:
                    part(i - 1, 0)
                if i >= 2:
                    part(i - 2, 1)

        def dve_proj(dve, n):
            if n == 1:
                dve.wait_ge(pv_done, UG)
            link(dve, dve.memset(vt, 1.0))
            if n == 1:
                for b in range(B):
                    link(dve, dve.memset(vt[0:WIN, NL * b], 0.0))
            dve.wait_ge(v_ready, n + 1)
            nt = len(v_tiles(n))
            for t0 in range(0, nt, 16):
                m = min(16, nt - t0)
                ins = dve.tensor_copy(vt[:, t0:t0 + m, :, 0:HD], bank[t0 // 16][:, 0:32 * m]
                                      .rearrange("p (t k d) -> p t k d", k=KVH, d=HD))
            ins.then_inc(v_copied, 1)
            dve.wait_ge(rope_in, 16 * (n + 1))

            def rotate(i):
                j = NIT * n + i
                b0, b1 = item_banks(i)
                at = L if i == 0 else (i - 1) % 2 * CH
                dve.wait_ge(pr_ready, j + 1)
                if n:
                    dve.wait_ge(parts_ready, NIT)
                r = rot[i]
                link(dve, dve.tensor_tensor(r, bank[b0][:, :], rope[:, 0, at:at + CH], MUL))
                link(dve, dve.tensor_tensor(rot2, bank[b1][:, :], rope[:, 1, at:at + CH], MUL))
                dve.tensor_tensor(r, r, rot2, ADD).then_inc(rot_ready, 1)

            def finish(i):
                j = NIT * n + i
                r = rot[i]
                dve.wait_ge(gs_ready, j + 1)
                rsqrt_step(dve, rgs[i % 2], bank[6 + i % 2][:, :], rtm, EPS_RMS)
                dve.tensor_tensor(r, r, rgs[i % 2], MUL).then_inc(normed9, 1)

            rotate(0)
            rotate(1)
            for i in range(NIT):
                if i + 2 < NIT:
                    rotate(i + 2)
                finish(i)

        def tiles(n):
            if n == 0:
                return [(b, t, t + 1) for b in range(B) for t in range(NQT)]
            return [(b, t, 1) for b in range(B) for t in range(NL)]

        def units(n):
            return [(o, kt) for o, (b, t, nk) in enumerate(tiles(n)) for kt in range(nk)]

        UG, UL = len(units(0)), len(units(1))
        width = (128, QL)
        base_u, base_o = (0, UG), (0, len(tiles(0)))

        def ends(n):
            return {u: o for u, (o, kt) in enumerate(units(n)) if kt == tiles(n)[o][2] - 1}

        D_VALUES, D_COPY, D_DEN, D_NORM, D_OUT = (1, 2), (2, 3), (3, 4), (4, 5), (7, 7)
        D_GUESS = 5

        def wo_group(n, o):
            b, t, _ = tiles(n)[o]
            per = 4 if n == 0 else 5
            w = width[n]
            count = NQT if n == 0 else NL
            first = t // per * per
            full = t % per == per - 1 or t == count - 1
            g = sum(1 for m in range(o) if wo_full(n, m))
            return (t % per) * w, full, (L * b + first * w, min(L * b + (t + 1) * w, L * b + L)), g

        def wo_full(n, o):
            b, t, _ = tiles(n)[o]
            per = 4 if n == 0 else 5
            return t % per == per - 1 or t == (NQT if n == 0 else NL) - 1

        def pe_core(pe, n):
            U, E, TL, w = units(n), ends(n), tiles(n), width[n]
            wo = wts["g_o" if n == 0 else "l_o"]

            def scores(u, hp):
                o, kt = U[u]
                b, t, _ = TL[o]
                if hp == 0 and kt == 0 and t == 0:
                    pe.wait_ge(in9[b], 18 * 16 * (n + 1))
                if u == 0:
                    pe.wait_ge(parts_ready, NIT * (n + 1))
                else:
                    pe.wait_ge(exp_done, 2 * (base_u[n] + u) + hp - 1)
                k0 = WIN + 128 * kt if n == 0 else QL * t
                for kv in (2 * hp, 2 * hp + 1):
                    out_ = bank[kv][:, 0:4 * w].rearrange("p (h q) -> p h q", h=4)
                    ins = pe.matmul(out_, k9[b][:, kv, k0:k0 + 128],
                                    q9[b][:, 4 * kv:4 * kv + 4, w * t:w * t + w], start=True, stop=True)
                ins.then_inc(scores_ready, 1)

            def values(u):
                o, kt = U[u]
                b, t, nk = TL[o]
                if kt == nk - 1:
                    if n == 0:
                        pe.wait_ge(masked, 2 * (o + 1))
                    else:
                        pe.wait_ge(masked, 2 * base_o[n] + o + 1)
                        pe.wait_ge(masked_by_pool, o + 1)
                else:
                    pe.wait_ge(exp_done, 2 * (base_u[n] + u + 1))
                if kt == 0 and o >= 2:
                    pe.wait_ge(osb_ready, base_o[n] + o - 1)
                tile = (NQT if n == 0 else NL) * b + (kt if n == 0 else t)
                for kv in range(KVH):
                    p = probs[(2 * u + kv // 2) % RING]
                    ins = pe.matmul(bank[4 + o % 2][32 * kv:32 * kv + 32, 0:4 * w], vt[:, tile, kv, :],
                                    p[:, kv % 2 * CH:kv % 2 * CH + 4 * w], start=(kt == 0), stop=(kt == nk - 1))
                ins.then_inc(pv_done, 1)

            def denominators(o):
                pe.wait_ge(osb_ready, base_o[n] + o + 1)
                if o >= 1:
                    pe.wait_ge(den_read, base_o[n] + o)
                pe.matmul(bank[6][:, 0:4 * w], const(K_DEN, 128), osb[o % 2][:, 0:4 * w], start=True, stop=True)\
                    .then_inc(den_ready, 1)

            def outputs(o):
                at, full, cols, g = wo_group(n, o)
                pe.wait_ge(on_ready, base_o[n] + o + 1)
                if at == 0 and g >= 1:
                    if n == 0:
                        pe.wait_ge(resid_ready, NCH * 2 + g)
                    elif (g - 1) % 3 == 0:
                        pe.wait_ge(added, (g - 1) // 3 + 1)
                    else:
                        pe.wait_ge(resid_ready, NCH * 3 + (g - 1) // 3 * 2 + (g - 1) % 3)
                for h in range(4):
                    ins = pe.matmul(bank[7][:, at:at + w], wo[:, 128 * h:128 * h + 128],
                                    onrm[o % 2][:, w * h:w * h + w], start=(h == 0), stop=(h == 3))
                ins.then_inc(wo_ready, 1)

            scores(0, 0)
            scores(0, 1)
            for u in range(len(U) + D_OUT[n]):
                if u + 1 < len(U):
                    scores(u + 1, 0)
                if D_VALUES[n] <= u < len(U) + D_VALUES[n]:
                    values(u - D_VALUES[n])
                if u + 1 < len(U):
                    scores(u + 1, 1)
                if u - D_OUT[n] in E:
                    outputs(E[u - D_OUT[n]])
                if u - D_DEN[n] in E:
                    denominators(E[u - D_DEN[n]])

        def act_core(act, n):
            U, E, w = units(n), ends(n), width[n]
            for u in range(len(U) + D_GUESS):
                for hp in range(2 if u < len(U) else 0):
                    s = 2 * u + hp
                    act.wait_ge(scores_ready, 2 * base_u[n] + s + 1)
                    if s >= RING:
                        act.wait_ge(pv_done, base_u[n] + (s - RING) // 2 + 1)
                    p = probs[s % RING].rearrange("p (k c) -> p k c", k=2)[:, :, 0:4 * w]
                    act.activation(p, two[hp][:, :, 0:4 * w], ACT.Exp, scale=HD ** -0.5).then_inc(exp_done, 1)
                if n == 1 and u - D_GUESS in E:
                    o = E[u - D_GUESS]
                    r = rec[o % 2][:, 0:4 * w]
                    act.wait_ge(den_ready, base_o[n] + o + 1)
                    if o >= 2:
                        act.wait_ge(on_ready, base_o[n] + o - 1)
                    link(act, act.activation(r, bank[6][:, 0:4 * w], ACT.Ln))
                    act.activation(r, r, ACT.Exp, scale=-1.0).then_inc(guessed, 1)
                if u - D_COPY[n] in E:
                    o = E[u - D_COPY[n]]
                    act.wait_ge(pv_done, base_u[n] + u - D_COPY[n] + 1)
                    if o >= 2:
                        act.wait_ge(on_ready, base_o[n] + o - 1)
                    act.activation(osb[o % 2][:, 0:4 * w], bank[4 + o % 2][:, 0:4 * w], ACT.Copy)\
                        .then_inc(osb_ready, 1)

        def core_mask(n):
            return spread(spread(const(K_CAUS, 128) if n == 0 else const(K_BAND, QL), 1, 4), 1, 2)

        def masked_part(s, w):
            return probs[s % RING].rearrange("p (k c) -> p k c", k=2)[:, :, 0:4 * w]\
                .rearrange("p k (h q) -> p k h q", h=4)

        def pool_core(pool):
            for u in range(UL):
                pool.wait_ge(exp_done, 2 * (UG + u) + 2)
                v = masked_part(2 * u + 1, width[1])
                pool.tensor_tensor(v, v, core_mask(1), MUL).then_inc(masked_by_pool, 1)

        def dve_core(dve, n):
            U, E, TL, w = units(n), ends(n), tiles(n), width[n]
            if n == 1:
                dve.wait_ge(parts_out[0], sent(max(j for j in range(2 * NIT) if slot_of[j] == 0)))
            mask, r2 = core_mask(n), rec2[:, 0:4 * w]

            def weigh(o, sign, r):
                if o >= 2:
                    dve.wait_ge(wo_ready, base_o[n] + o - 1)
                dve.scalar_tensor_tensor(onrm[o % 2][:, 0:4 * w], osb[o % 2][:, 0:4 * w], sign, r, MUL, MUL)\
                    .then_inc(on_ready, 1)

            for u in range(len(U) + D_OUT[n]):
                if u < len(U) and u in E:
                    s = 2 * u
                    for hp in range(2 if n == 0 else 1):
                        dve.wait_ge(exp_done, 2 * base_u[n] + s + hp + 1)
                        v = masked_part(s + hp, w)
                        dve.tensor_tensor(v, v, mask, MUL).then_inc(masked, 1)
                if n == 1 and u - D_NORM[n] in E:
                    o = E[u - D_NORM[n]]
                    r = rec[o % 2][:, 0:4 * w]
                    dve.wait_ge(guessed, o + 1)
                    if o >= 1:
                        dve.wait_ge(on_ready, base_o[n] + o)
                    dve.tensor_tensor(r2, bank[6][:, 0:4 * w], r, MUL).then_inc(den_read, 1)
                    dve.wait_ge(den_read, base_o[n] + o + 1)
                    link(dve, dve.scalar_tensor_tensor(r2, r2, 2.0, r, SUB, MUL))
                    weigh(o, -1.0, r2)
                if n == 0 and u - D_NORM[n] in E:
                    o = E[u - D_NORM[n]]
                    dve.wait_ge(den_ready, base_o[n] + o + 1)
                    if o >= 1:
                        dve.wait_ge(on_ready, base_o[n] + o)
                    dve.reciprocal(rec[0], bank[6][:, 0:4 * w]).then_inc(den_read, 1)
                    dve.wait_ge(den_read, base_o[n] + o + 1)
                    weigh(o, 1.0, rec[0])
                if u - D_OUT[n] in E:
                    o = E[u - D_OUT[n]]
                    at, full, (x0, x1), g = wo_group(n, o)
                    if full:
                        dve.wait_ge(wo_ready, base_o[n] + o + 1)
                        dve.wait_ge(x_kept if n == 0 else x_added, NCH)
                        ins = dve.tensor_tensor(X[:, x0:x1], X[:, x0:x1], bank[7][:, 0:x1 - x0], ADD)
                        ins.then_inc(resid_ready if n == 0 or g % 3 > 0 else added, 1)

        r2w, r2b, firstw, sel2f = wts["r2_w"], wts["r2_b"], wts["first"], wts["sel2"]
        m2_w1 = place(0, E2 * FF2)
        m2_w2 = place(E2 * FF2, E2 * 4, 128)
        D0 = 16896
        rt = place(D0, NT, E2)
        mk = place(D0 + 128, NT, E2)
        mk2 = place(D0 + 256, NT, 2 * E2)
        mrow = place(D0 + 512, 2, NT)
        mt = place(D0 + 1024, T)
        mtb = place(D0 + 3072, T, dt=bf16)
        selb = place(D0 + 4096, E2 + 1, 128, dt=bf16)
        pbx = place(D0 + 4864, T)
        ge = [work[:, 3 * T + CH * n:3 * T + CH * n + CH] for n in range(4)]
        up_halves = [place_half(D, E2 * FF2) for D in (2 * E2 * FF2, 0)]
        down_halves = [place_half(D, E2 * 4, 128) for D in (3 * E2 * FF2, E2 * FF2)]
        x2_halves = [[place_half(D0 + 6912 + CH * (2 * n + a), CH) for a in range(2)] for n in range(2)]
        xe = [[place_half(D0 + 8960 + CH * (2 * n + a), CH) for a in range(2)] for n in range(2)]
        g_halves = [[place_half(D0 + 11008 + CH * (2 * n + a), CH) for a in range(2)] for n in range(4)]
        w2_split, x2_split, gelu_split = (sem(n) for n in ("w_split_2", "x_split_2", "gelu_split"))
        route2_ready, sig_in, sig_out, mk_ready, mt_ready, mt_copied = (
            sem(n) for n in ("route2_ready", "sig_in", "sig_out", "mk_ready", "mt_ready", "mt_copied"))
        mb_ready, xe_ready, up2_ready, gelu_done, down2, m2_out, pb_ready, pb_copied = (
            sem(n) for n in ("mb_ready", "xe_ready", "up2_ready", "gelu_done", "down2", "m2_out", "pb_ready", "pb_copied"))
        KBE = FF2 // 128
        XFIRST = 5

        def sp_moe2(sp):
            sp.wait_ge(pv_done, UG + NL)
            sp.dma_start(m2_w1, dram["m2_w1"]).then_inc(m2_in, 16)
            sp.dma_start(m2_w2, dram["m2_w2"].rearrange("p (a b) -> p a b", b=128)).then_inc(m2_in, 16)

        def pe_moe2(pe):
            for t in range(NT):
                pe.wait_ge(normed, NCH * 4 + t // 4 + 1)
                ins = pe.matmul(bank[0][:, 8 * t:8 * t + 8], X[:, 128 * t:128 * t + 128], r2w[:, :],
                                start=True, stop=True)
            ins.then_inc(route2_ready, 1)
            pe.wait_ge(mk_ready, 1)
            for g in range(NCH):
                if g >= 2:
                    pe.wait_ge(mt_copied, g - 1)
                for t in range(4 * g, 4 * g + 4):
                    ins = pe.transpose(bank[1 + g % 2][0:16, 128 * (t % 4):128 * (t % 4) + 128], mk2[:, t], const(K_ID, 128))
                ins.then_inc(mt_ready, 1)
            pe.wait_ge(mt_copied, NCH)
            for c in range(NCH):
                if c >= 2:
                    pe.wait_ge(pb_copied, c - 1)
                pe.matmul(bank[1 + c % 2][:, :], sel2f[:, 128 * E2:128 * E2 + 128], mt[0:16, tok(c)],
                          start=True, stop=True).then_inc(pb_ready, 1)
            pe.wait_ge(pb_copied, NCH)
            pe.wait_ge(m2_in, 32)

            def masks(n):
                c, e = n // E2, n % E2
                if n >= 1:
                    pe.wait_ge(xe_ready, n)
                pe.matmul(bank[0][:, :], selb[0:16, e, :], mtb[0:16, tok(c)], start=True, stop=True)\
                    .then_inc(mb_ready, 1)

            def up(m):
                n, k = m // KBE, m % KBE
                e = n % E2
                pe.wait_ge(xe_ready, n + 1)
                if m >= 4:
                    pe.wait_ge(gelu_done, m - 3)
                pe.wait_ge(w2_split, 2 * e + 1)
                at = FF2 * e + 128 * k
                product(pe, bank[1 + m % 4][:, :], [w[:, at:at + 128] for w in up_halves], xe[n % 2],
                        True, True).then_inc(up2_ready, 1)

            def down(m):
                n, k = m // KBE, m % KBE
                c, e = n // E2, n % E2
                if e == 0 and k == 0 and c >= 2:
                    pe.wait_ge(resid_ready, NCH * 4 + c - 1)
                pe.wait_ge(gelu_split, m + 1)
                pe.wait_ge(w2_split, 2 * e + 2)
                product(pe, bank[6 + c % 2][:, :], [w[:, KBE * e + k, :] for w in down_halves], g_halves[m % 4],
                        e == 0 and k == 0, e == E2 - 1 and k == KBE - 1).then_inc(down2, 1)

            masks(0)
            masks(1)
            M = NCH * E2 * KBE
            for m in range(4):
                up(m)
            for m in range(M):
                if m + 4 < M:
                    up(m + 4)
                if m % KBE == 0 and m // KBE + 2 < NCH * E2:
                    masks(m // KBE + 2)
                down(m)

        def act_moe2(act):
            act.wait_ge(sig_in, 1)
            act.activation(rt, rt, ACT.Sigmoid).then_inc(sig_out, 1)
            for m in range(NCH * E2 * KBE):
                act.wait_ge(up2_ready, m + 1)
                if m >= 4:
                    act.wait_ge(down2, m - 3)
                act.activation(g_halves[m % 4][0], bank[1 + m % 4][:, :], ACT.Gelu)
                act.activation(ge[m % 4], bank[1 + m % 4][:, :], ACT.Gelu).then_inc(gelu_done, 1)

        def pool_moe2(pool):
            pool.wait_ge(m2_in, 32)
            pool.wait_ge(pv_done, UG + UL)

            def chunk(c):
                pool.wait_ge(normed, NCH * 4 + c + 1)
                if c >= 2:
                    pool.wait_ge(xe_ready, E2 * (c - 1))
                halve(pool, x2_halves[c % 2][0], x2_halves[c % 2][1], X[:, tok(c)], x2_split)

            for e in range(E2):
                w = slice(FF2 * e, FF2 * e + FF2)
                halve(pool, up_halves[0][:, w], up_halves[1][:, w], m2_w1[:, w], w2_split)
                w = slice(KBE * e, KBE * e + KBE)
                halve(pool, down_halves[0][:, w], down_halves[1][:, w], m2_w2[:, w], w2_split)
                if e >= XFIRST:
                    chunk(e - XFIRST)
            for c in range(E2 - XFIRST, NCH):
                chunk(c)

        def dve_moe2(dve):
            dve.wait_ge(route2_ready, 1)
            g = "p (t e) -> p t e"
            dve.tensor_tensor(rt, bank[0][:, 0:128].rearrange(g, e=E2), spread(r2b[:, :], 1, NT), ADD)\
                .then_inc(sig_in, 1)
            link(dve, dve.tensor_copy(selb[0:16], sel2f[:, :].rearrange("p (a b) -> p a b", b=128)))
            dve.wait_ge(sig_out, 1)
            link(dve, dve.tensor_reduce(mrow[:, 0], rt, AX.X, ALU.max))
            link(dve, dve.tensor_tensor(mk, rt, spread(mrow[:, 0], 2, E2), ALU.is_equal))
            link(dve, dve.tensor_tensor(mk, mk, firstw[:, :].rearrange(g, e=E2), MUL))
            link(dve, dve.tensor_reduce(mrow[:, 1], mk, AX.X, ALU.max))
            link(dve, dve.tensor_tensor(mk2[:, :, 0:E2], mk, spread(mrow[:, 1], 2, E2), ALU.is_equal))
            dve.tensor_tensor(mk2[:, :, E2:], mk2[:, :, 0:E2], spread(mrow[:, 0], 2, E2), MUL).then_inc(mk_ready, 1)
            for c in range(NCH):
                dve.wait_ge(mt_ready, c + 1)
                link(dve, dve.tensor_copy(mt[0:16, tok(c)], bank[1 + c % 2][0:16, :]))
                dve.tensor_copy(mtb[0:16, tok(c)], mt[0:16, tok(c)]).then_inc(mt_copied, 1)
            for c in range(NCH):
                dve.wait_ge(pb_ready, c + 1)
                dve.tensor_copy(pbx[:, tok(c)], bank[1 + c % 2][:, :]).then_inc(pb_copied, 1)

            def result(c):
                dve.wait_ge(m2_out_at(c)[0], m2_out_at(c)[1])
                t = pbx[:, tok(c)]
                link(dve, dve.tensor_tensor(t, t, bank[6 + c % 2][:, :], MUL))
                dve.tensor_tensor(X[:, tok(c)], X[:, tok(c)], t, ADD).then_inc(resid_ready, 1)

            def masked_tokens(n):
                c = n // E2
                dve.wait_ge(mb_ready, n + 1)
                dve.wait_ge(x2_split, c + 1)
                if n >= 2:
                    dve.wait_ge(up2_ready, KBE * (n - 1))
                for a in range(2):
                    ins = dve.tensor_tensor(xe[n % 2][a], x2_halves[c % 2][a].bitcast(f32), bank[0][:, :], MUL)
                ins.then_inc(xe_ready, 1)

            masked_tokens(0)
            masked_tokens(1)
            for m in range(NCH * E2 * KBE):
                dve.wait_ge(gelu_done, m + 1)
                if m >= 4:
                    dve.wait_ge(down2, m - 3)
                high, low = g_halves[m % 4]
                dve.tensor_tensor(low, ge[m % 4], high.bitcast(f32), SUB).then_inc(gelu_split, 1)
                n = m // KBE + 2
                if m % KBE == 1 and n < NCH * E2:
                    masked_tokens(n)
                if m % (KBE * E2) == KBE * 2 and m > KBE * E2:
                    result(m // (KBE * E2) - 1)
            result(NCH - 1)

        def m2_out_at(c):
            return down2, KBE * E2 * (c + 1)

        block = stack.enter_context(nc.Block())

        @block.sync
        def _(sp):
            sp_ssm(sp)
            n_norms = 1
            if stages >= 2:
                sp_moe1(sp)
                n_norms = 2
            if stages >= 3:
                sp_attn(sp, 0)
                sp_attn(sp, 1)
                sp_moe2(sp)
                n_norms = 5
            if stages >= 4:
                n_norms = 6
            for c in range(NCH):
                sp.wait_ge(normed, NCH * (n_norms - 1) + c + 1)
                sp.dma_start(out[:, tok(c)], X[:, tok(c)]).then_inc(sem_out, 16)
            sp.wait_ge(m2_in, 32) if stages >= 3 else None
            sp.wait_ge(sem_out, 16 * NCH)

        @block.gpsimd
        def _(pool):
            if stages >= 2:
                pool_moe1(pool)
            if stages >= 3:
                pool_attn(pool)
            if stages >= 4:
                pool_moe2(pool)

        @block.tensor
        def _(pe):
            pe_ssm(pe)
            pe_norm(pe, 0, False)
            if stages >= 2:
                pe_moe1(pe)
                pe_norm(pe, 1, False)
            if stages >= 3:
                for n in range(2):
                    pe_norm(pe, 2 + n, True)
                    pe_proj(pe, n)
                    pe_core(pe, n)
                pe_norm(pe, 4, False)
            if stages >= 4:
                pe_moe2(pe)
                pe_norm(pe, 5, False)

        @block.scalar
        def _(act):
            act_tables(act)
            act_ssm(act)
            act_tables2(act)
            act_ssm2(act)
            act_norm(act, 0, 0)
            if stages >= 2:
                act_moe1(act)
                act_norm(act, 1, 0)
            if stages >= 3:
                for n in range(2):
                    act_norm(act, 2 + n, 1)
                    act_proj(act, n)
                    act_core(act, n)
                act_norm(act, 4, 0)
            if stages >= 4:
                act_moe2(act)
                act_norm(act, 5, 0)

        @block.vector
        def _(dve):
            dve_tables(dve)
            dve_ssm(dve)
            dve_norm(dve, 0, 0)
            if stages >= 2:
                dve_moe1(dve)
                dve_norm(dve, 1, 0)
            if stages >= 3:
                for n in range(2):
                    dve_norm(dve, 2 + n, 1)
                    dve_proj(dve, n)
                    dve_core(dve, n)
                dve_norm(dve, 4, 0)
            if stages >= 4:
                dve_moe2(dve)
                dve_norm(dve, 5, 0)


def kernel(**inputs):
    from concourse import bacc
    from concourse.bass_utils import run_bass_kernel_spmd

    nc = bacc.Bacc("TRN2", target_bir_lowering=False, num_devices=1)
    arrays = {"in_" + k: v for k, v in lay_out({k: np.asarray(v) for k, v in inputs.items()}).items()}
    dram = {k[3:]: nc.dram_tensor(k, v.shape, mybir.dt.from_np(v.dtype), kind="ExternalInput").ap()
            for k, v in arrays.items()}
    out = nc.dram_tensor("out", (DM, T), mybir.dt.float32, kind="ExternalOutput").ap()
    build(nc, dram, out)
    r = run_bass_kernel_spmd(nc, [arrays], core_ids=[0])
    return np.ascontiguousarray(np.asarray(r.results[0]["out"]).T).reshape(B, L, DM)
```

```python
import numpy as np
from contextlib import ExitStack

import concourse.bass as bass
from concourse import mybir

B, L, DM = 2, 1024, 128
T = B * L
CH = 512
NCH = T // CH
DIN, NST = 256, 16
MH = DIN // 128
Q = 32
NJ = L // Q
GC = 8
NG = MH * 32 // GC
E1, H1, ES, HS1 = 64, 32, 2, 256
KB1 = E1 * H1 // 128
KBS = ES * HS1 // 128
E2, FF2 = 8, 512
H, KVH, HD, LAT, WIN = 16, 4, 8, 32, 32
QL = 128 - WIN
NL = -(-L // QL)
LP = WIN + NL * QL
NQT = L // 128
NT = T // 128
AREA = 33000
EPS_LN, EPS_RMS = 1e-5, 1e-6
MAGIC = 12582912.0
TWO_PI = 6.283185
C1, C2 = 6.28125, 0.0019350051879882812
C3 = 2 * np.pi - C1 - C2
LOG_EXP = "natural_log_exp_and_others"
LOG2E, LN2H, LN2L = 1.4426950408889634, 0.693359375, -2.12194440e-4

K_Q31, K_MRE, K_MIM, K_LROW, K_JROW, K_SEL = 0, 1, 2, 3, 36, 68
K_MEAN, K_HEAD, K_DEN, K_ID, K_CAUS, K_BAND, K_N = 72, 200, 328, 456, 584, 712, 808


def constants():
    c = np.zeros((128, K_N), np.float32)
    p = np.arange(128)
    c[:, K_Q31] = Q - 1 - p % 32
    c[:, K_MRE] = p % 32 < NST
    c[:, K_MIM] = p % 32 >= NST
    c[:, K_LROW:K_LROW + Q + 1] = np.arange(Q + 1)
    c[:, K_JROW:K_JROW + NJ] = np.arange(NJ) * Q
    for g in range(4):
        c[32 * g:32 * g + NST, K_SEL + g] = 1.0
    c[:, K_MEAN:K_MEAN + 128] = 1.0 / 128
    c[:, K_HEAD:K_HEAD + 128] = (p[:, None] // HD == p[None] // HD) / HD
    c[:, K_DEN:K_DEN + 128] = p[:, None] == p[None] // 32 * 32 + HD
    c[:, K_ID:K_ID + 128] = np.eye(128)
    c[:, K_CAUS:K_CAUS + 128] = p[:, None] <= p[None]
    diff = np.arange(QL)[None] + WIN - p[:, None]
    c[:, K_BAND:K_BAND + QL] = (diff >= 0) & (diff < WIN)
    rope = np.zeros((2, 2, 128, L), np.float32)
    for n, base in enumerate((1000000.0, 10000.0)):
        inv = 1.0 / np.float32(base) ** (np.arange(0, HD, 2, dtype=np.float32) / HD)
        ang = np.arange(L, dtype=np.float32)[:, None] * inv[None].astype(np.float32)
        cos, sin = np.cos(ang).T, np.sin(ang).T
        d = p % HD
        rope[n, 0] = cos[d // 2]
        rope[n, 1] = sin[d // 2] * np.where(d % 2 == 0, -1.0, 1.0)[:, None]
    sel1 = np.zeros((2, E1, KB1, 128), np.float32)
    for kb in range(KB1):
        sel1[:, 4 * kb + p // 32, kb, p] = 1.0
    sel2 = np.zeros((2 * E2, E2 + 1, 128), np.float32)
    for e in range(E2):
        sel2[e, e, :] = 1.0
    sel2[E2:, E2, :] = 1.0
    first = np.tile(np.arange(E2, 0, -1, dtype=np.float32), (128, NT))
    kept = rope[:, :, :32].reshape(2, 2, 32, 2, CH)
    kept = np.concatenate([kept[:, :, :, n % 2] for n in range(NCH)], 2)
    rope = np.concatenate([rope, kept], 3).transpose(0, 2, 1, 3)
    return {"consts": c, "rope": rope, "sel1": sel1.reshape(128, -1),
            "sel2": sel2.reshape(2 * E2, -1), "first": first}


def lay_out(x):
    a = {}
    a["h_t"] = x["L0_attn_hidden_states"].reshape(T, DM).T
    a["w_in"] = x["L0_attn_in_proj_w"].T
    taps = x["L0_attn_conv_w"].T.reshape(1, -1)
    a["conv_row"] = np.broadcast_to(taps, (128, 4 * DIN))
    a["ssm_bias"] = x["L0_attn_conv_b"].reshape(MH, 128).T
    a["d_skip"] = x["L0_attn_D_skip"].reshape(MH, 4, 32).transpose(1, 0, 2).reshape(4, 64)
    a["w_out"] = x["L0_attn_out_proj_w"].T.reshape(MH, 128, DM).transpose(1, 0, 2).reshape(128, -1)
    names = ("L0_attn_A_re", "L0_attn_A_im", "L0_attn_C_re", "L0_attn_C_im")
    by_state = []
    for n in names:
        v = x[n].reshape(MH, 4, 32, NST).transpose(1, 3, 0, 2)
        by_state.append(np.broadcast_to(v[:, None], (4, 2, NST, MH, 32)).reshape(128, 64))
    ld = x["L0_attn_log_dt"].reshape(MH, 4, 32).transpose(1, 0, 2)
    ld = np.broadcast_to(ld[:, None], (4, 32, MH, 32)).reshape(128, 64)
    a["par_state"] = np.concatenate(by_state + [ld], 1)
    a["r1_w"] = x["L0_ffn_router_w"]
    a["r1_b"] = np.broadcast_to(x["L0_ffn_router_b"], (128, E1))
    a["m1_w1"] = np.concatenate([x["L0_ffn_w1"].transpose(1, 0, 2).reshape(DM, -1),
                                 x["L0_ffn_sw1"].transpose(1, 0, 2).reshape(DM, -1)], 1)
    a["m1_b1"] = np.concatenate([x["L0_ffn_b1"].reshape(KB1, 128), x["L0_ffn_sb1"].reshape(KBS, 128)]).T
    w2 = np.concatenate([x["L0_ffn_w2"].reshape(KB1, 128, DM), x["L0_ffn_sw2"].reshape(KBS, 128, DM)])
    a["m1_w2"] = w2.transpose(1, 0, 2).reshape(128, -1)
    a["m1_b2"] = np.concatenate([x["L0_ffn_b2"], x["L0_ffn_sb2"]])
    swap = np.arange(128) ^ 1
    a["norm_w"] = np.stack([x["L1_attn_norm1_w"], x["L1_attn_norm2_w"]], 1)
    for n in "gl":
        wq = x[f"L1_attn_{n}_wq"]
        a[f"{n}_q"] = np.concatenate([wq, wq[:, swap]], 1)
        wo = np.zeros((4, 32, 4, DM), np.float32)
        wo[:, :HD] = x[f"L1_attn_{n}_wo"].reshape(KVH, 4, HD, DM).transpose(0, 2, 1, 3)
        a[f"{n}_o"] = wo.reshape(128, -1)
    up, wk = x["L1_attn_g_k_up"], x["L1_attn_l_wk"]
    a["g_down"] = x["L1_attn_g_kv_down"]
    a["g_kv"] = np.concatenate([up, up[:, swap[:32]], x["L1_attn_g_v_up"]], 1)
    a["l_kv"] = np.concatenate([wk, wk[:, swap[:32]], x["L1_attn_l_wv"]], 1)
    a["r2_w"] = x["L1_ffn_Wr"]
    a["r2_b"] = np.tile(x["L1_ffn_br"], (128, 1))
    a["m2_w1"] = x["L1_ffn_W1"].transpose(1, 0, 2).reshape(DM, -1)
    a["m2_w2"] = x["L1_ffn_W2"].reshape(E2 * 4, 128, DM).transpose(1, 0, 2).reshape(128, -1)
    a.update(constants())
    return {k: np.ascontiguousarray(v) for k, v in a.items()}


def spread(ap, axis, n):
    dims = [list(d) for d in ap.ap]
    return bass.AP(tensor=ap.tensor, offset=ap.offset, ap=dims[:axis] + [[0, n]] + dims[axis:])


def build(nc, dram, out, stages=99):
    f32, f32r, bf16, i32 = (mybir.dt.float32, mybir.dt.float32r, mybir.dt.bfloat16, mybir.dt.int32)
    ALU, ACT, AX = mybir.AluOpType, mybir.ActivationFunctionType, mybir.AxisListType
    ADD, SUB, MUL = ALU.add, ALU.subtract, ALU.mult
    stack = ExitStack()

    def sem(name):
        return stack.enter_context(nc.semaphore(name))

    def sb(name, shape, dt=f32):
        return stack.enter_context(nc.sbuf_tensor(name, shape, dt))

    with stack:
        cst = sb("cst", [128, K_N])
        X = sb("X", [128, T])
        xn = sb("xn", [128, B, LP])
        work = sb("work", [128, 4 * T + 256])
        dev, sq, y0 = (work[:, n * T:(n + 1) * T] for n in range(3))
        wts = {name: sb("w_" + name, list(dram[name].shape)) for name in dram
               if name.split("_")[0] in ("r1", "m1", "norm", "g", "l", "r2", "sel2", "first")
               and name != "m1_w2"}
        two = [stack.enter_context(nc.psum_tensor(f"banks{i}", [128, 2, CH], f32)) for i in range(4)]
        bank = [two[i // 2][:, i % 2, :] for i in range(8)]
        eps = sb("eps", [128, 3])
        ssm_bias = sb("ssm_bias", [128, MH])
        norm_w = sb("half_norm_w", [128, 2])[:, :]
        w_out = sb("w_out", [128, MH * 128])
        with nc.sbuf_tensor("arena", [128, AREA], f32) as arena:
            pass

        def place(at, *shape, dt=f32):
            n = int(np.prod(shape))
            words = n // (2 if dt == bf16 else 1)
            assert at + words <= AREA, (at, shape)
            v = arena[:, at:at + words]
            if dt != f32:
                v = v.bitcast(dt)
            names = "abcd"[:len(shape)]
            return v.rearrange(f"p ({' '.join(names)}) -> p {' '.join(names)}",
                               **{k: s for k, s in zip(names, shape)})

        def place_half(at, *shape):
            names = "abcd"[:len(shape)]
            n = int(np.prod(shape))
            assert at + n <= AREA and at % 8 == 0, (at, shape)
            with ExitStack() as here:
                if at:
                    here.enter_context(nc.sbuf_tensor(f"below_{len(halves)}", [128, at], f32))
                v = here.enter_context(nc.sbuf_tensor(f"half_{len(halves)}", [128, n], f32r))
                halves.append(v)
            return v[:, :].rearrange(f"p ({' '.join(names)}) -> p {' '.join(names)}",
                                     **{k: s for k, s in zip(names, shape)})

        halves = []

        def halve(eng, high, low, value, done):
            link(eng, eng.tensor_copy(high, value))
            eng.tensor_tensor(low, value, high.bitcast(f32), SUB).then_inc(done, 1)

        def product(pe, o, w, x, start, stop):
            (wh, wl), (xh, xl) = w, x
            pe.matmul(o, wh, xh, start=start, stop=False)
            pe.matmul(o, wh, xl, start=False, stop=False)
            return pe.matmul(o, wl, xh, start=False, stop=stop)

        def const(at, n, rows=128):
            return cst[0:rows, at:at + n]

        chain = {}

        def link(eng, ins):
            s = chain[eng.engine]
            s[1] += 1
            ins.then_inc(s[0], 1)
            eng.wait_ge(s[0], s[1])

        for e, n in ((nc.vector, "vector_step"), (nc.scalar, "scalar_step"), (nc.gpsimd, "pool_step")):
            chain[e.engine] = [sem(n), 0]

        consts_in, first_in, par_in, wout_in = sem("consts_in"), sem("first_in"), sem("par_in"), sem("wout_in")
        m1_in, attn_in, m2_in = sem("m1_in"), sem("attn_in"), sem("m2_in")

        resid_ready = sem("resid_ready")
        mean_ready = sem("mean_ready")
        dev_ready = sem("dev_ready")
        square_ready = sem("square_ready")
        var_ready = sem("var_ready")
        guess_ready = sem("guess_ready")
        normed = sem("normed")

        def tok(c):
            return slice(c * CH, (c + 1) * CH)

        def xn_tok(c):
            return xn[:, c // 2, WIN + c % 2 * CH:WIN + (c % 2 + 1) * CH]

        def pe_norm(pe, k, rms):
            if not rms:
                for c in range(NCH):
                    pe.wait_ge(resid_ready, NCH * resid_index[k] + c + 1)
                    pe.matmul(bank[c][:, :], const(K_MEAN, 128), X[:, tok(c)], start=True, stop=True)\
                        .then_inc(mean_ready, 1)
            for c in range(NCH):
                pe.wait_ge(square_ready, NCH * k + c + 1)
                pe.matmul(bank[4 + c][:, :], const(K_MEAN, 128), sq[:, tok(c)], start=True, stop=True)\
                    .then_inc(var_ready, 1)

        def act_norm(act, k, rms):
            for c in range(NCH):
                if rms:
                    if k == 2:
                        act.wait_ge(normed, NCH * k - NCH + c + 1)
                    else:
                        act.wait_ge(resid_ready, NCH * resid_index[k] + c + 1)
                else:
                    act.wait_ge(dev_ready, ln_index[k] * NCH + c + 1)
                act.activation(sq[:, tok(c)], X[:, tok(c)] if rms else dev[:, tok(c)], ACT.Square)\
                    .then_inc(square_ready, 1)
            act.preload_act_table_set(LOG_EXP)
            for c in range(NCH):
                act.wait_ge(var_ready, NCH * k + c + 1)
                link(act, act.activation(y0[:, tok(c)], bank[4 + c][:, :], ACT.Ln,
                                         bias=eps[:, rms:rms + 1]))
                link(act, act.activation(y0[:, tok(c)], y0[:, tok(c)], ACT.Exp, scale=-0.5))
                act.activation(sq[:, tok(c)], y0[:, tok(c)], ACT.Square).then_inc(guess_ready, 1)

        def rsqrt_step(dve, guess, guess_sq, square, eps_value):
            link(dve, dve.scalar_tensor_tensor(guess_sq, square, eps_value, guess_sq, ADD, MUL))
            link(dve, dve.scalar_tensor_tensor(guess, guess_sq, 3.0, guess, SUB, MUL))

        def dve_norm(dve, k, rms):
            if k == 2:
                link(dve, dve.tensor_scalar(norm_w, wts["norm_w"][:, :], -0.5, None, MUL))
            if not rms:
                for c in range(NCH):
                    dve.wait_ge(mean_ready, ln_index[k] * NCH + c + 1)
                    dve.tensor_tensor(dev[:, tok(c)], X[:, tok(c)], bank[c][:, :], SUB).then_inc(dev_ready, 1)
            for c in range(NCH):
                dve.wait_ge(guess_ready, NCH * k + c + 1)
                y = y0[:, tok(c)]
                rsqrt_step(dve, y, sq[:, tok(c)], bank[4 + c][:, :], EPS_RMS if rms else EPS_LN)
                if rms:
                    dve.scalar_tensor_tensor(xn_tok(c), X[:, tok(c)], norm_w[:, k - 2:k - 1], y, MUL, MUL)\
                        .then_inc(normed, 1)
                else:
                    dve.scalar_tensor_tensor(X[:, tok(c)], dev[:, tok(c)], -0.5, y, MUL, MUL).then_inc(normed, 1)

        ln_index = {0: 0, 1: 1, 4: 2, 5: 3}
        resid_index = {0: 0, 1: 1, 3: 2, 4: 3, 5: 4}
        sem_out = sem("sem_out")

        u = place(0, MH, T)
        at = MH * T
        w_in = place(at, 2 * DIN); at += 2 * DIN
        sz = place(at, MH, T)
        conv_row = place(at, 4, DIN)
        w_conv = place(at + 4 * DIN, 4, DIN); at += MH * T
        kpad = place(at, 64, 64)[0:4]
        y_t = place(at, MH, B * NJ, Q); at += MH * T
        EU = place(at, 64, 32); at += 2048
        EV = place(at, 64, 32); at += 2048
        F1 = place(at, 64, Q + 1); at += 64 * (Q + 1)
        TP = place(at, 64, Q); at += 2048
        cos_j = place(at, 64, NJ); at += 2048
        sin_j = place(at, 64, NJ); at += 2048
        rho_g = [place(at + 512 * n, GC * B * NJ) for n in range(2)]; at += 1024
        pa, pb_, pc, pd = (place(at + 512 * n, GC * B * NJ) for n in range(4)); at += 2048
        hc = [place(at + 512 * n, GC, B, NJ) for n in range(2)]; at += 1024
        par_state = place(at, 5, 64); at += 320
        d_skip = place(at, 64)[0:4]; at += 64
        small = place(at, 28, 64); at += 28 * 64
        tmpw = [work[:, n * 2112:(n + 1) * 2112] for n in range(4)]
        v2, m2, s2, h2 = (w.rearrange("p (c l) -> p c l", l=Q + 1) for w in tmpw)
        xq = work[:, 0:MH * T].rearrange("p (m b c) -> p m b c", m=MH, c=32)
        ysb = work[:, MH * T:2 * MH * T].rearrange("p (m b c) -> p m b c", m=MH, c=32)
        kd = nc.dram_tensor("taps", (4, 64, 64), f32, kind="Internal").ap()

        h_in, weights_in, d_in, w_conv_ready = (sem(n) for n in ("h_in", "w_in_in", "d_skip_in", "w_conv_ready"))
        xz_ready, xz_out, xq_ready = sem("xz_ready"), sem("xz_out"), sem("xq_ready")
        rates_ready = sem("rates_ready")
        turns_ready = sem("turns_ready")
        mag_arg, block_turns = sem("mag_arg"), sem("block_turns")
        kpad_clear, rho_ready = sem("kpad_clear"), sem("rho_ready")
        looked_up = sem("looked_up")
        blocks_looked_up = sem("blocks_looked_up")
        f_ready, e_ready, taps_ready, taps_copied = sem("f_ready"), sem("e_ready"), sem("taps_ready"), sem("taps_copied")
        taps_out, toeplitz_in = sem("taps_out"), sem("toeplitz_in")
        uv_ready, uv_used, state_ready, y_ready, y_copied = (
            sem(n) for n in ("uv_ready", "uv_used", "state_ready", "y_ready", "y_copied"))
        gated, out_ready = sem("gated"), sem("out_ready")

        def sp_ssm(sp):
            sp.dma_start(par_state, dram["par_state"].rearrange("p (a b) -> p a b", a=5)).then_inc(par_in, 16)
            sp.dma_start(cst[:, :], dram["consts"]).then_inc(consts_in, 16)
            sp.dma_start(w_in, dram["w_in"]).then_inc(weights_in, 16)
            sp.dma_start(conv_row, dram["conv_row"].rearrange("p (k c) -> p k c", k=4)).then_inc(weights_in, 16)
            for b in range(B):
                sp.dma_start(xn[:, b, WIN:WIN + L], dram["h_t"][:, L * b:L * b + L]).then_inc(h_in, 16)
            sp.dma_start(ssm_bias[:, :], dram["ssm_bias"]).then_inc(h_in, 16)
            sp.dma_start(X[:, :], dram["h_t"]).then_inc(first_in, 16)
            sp.dma_start(d_skip, dram["d_skip"]).then_inc(d_in, 16)
            sp.dma_start(w_out[:, :], dram["w_out"]).then_inc(wout_in, 16)
            sp.wait_ge(taps_copied, 1)
            sp.dma_start(kd, kpad[:, :, :]).then_inc(taps_out, 16)
            sp.wait_ge(taps_out, 16)
            for g in range(4):
                rows = bass.AP(tensor=kd.tensor, offset=kd.offset + g * 64 * 64, ap=[[1, Q], [64, 64], [1, Q]])
                sp.dma_start(TP[Q * g:Q * g + Q], rows).then_inc(toeplitz_in, 16)

        def pe_ssm(pe):
            pe.wait_ge(h_in, 48)
            pe.wait_ge(w_conv_ready, 3)
            for n in range(2 * MH * NCH):
                m, c = n // NCH, n % NCH
                if n >= 8:
                    pe.wait_ge(xz_out, n - 7)
                if m < MH:
                    at = WIN + c % 2 * CH
                    for k in range(4):
                        ins = pe.matmul(bank[n % 8][:, :], w_conv[:, k, 128 * m:128 * m + 128],
                                        xn[:, c // 2, at + k - 3:at + k - 3 + CH], start=(k == 0), stop=(k == 3))
                else:
                    ins = pe.matmul(bank[n % 8][:, :], w_in[:, 128 * m:128 * m + 128], xn_tok(c), start=True, stop=True)
                ins.then_inc(xz_ready, 1)
            pe.wait_ge(f_ready, 1)
            pe.wait_ge(xz_out, 12)
            for n in range(4):
                pe.matmul(bank[n][0:4, :], const(K_SEL, 4), F1[:, 16 * n:16 * n + 16, 0:Q],
                          start=True, stop=True).then_inc(taps_ready, 1)
            pe.wait_ge(e_ready, 1)
            pe.wait_ge(taps_copied, 1)
            pe.wait_ge(xz_out, 16)

            def to_states(k):
                m, c0 = k // 4, GC * (k % 4)
                pe.wait_ge(xq_ready, m + 1)
                if k >= 2:
                    pe.wait_ge(uv_used, k - 1)
                for w, b0 in ((EU, 0), (EV, 2)):
                    for c in range(GC):
                        for g in range(4):
                            r = slice(32 * g, 32 * g + 32)
                            ins = pe.matmul(bank[b0 + k % 2][r, 64 * c:64 * c + 64], w[r, 32 * m + c0 + c, :],
                                            xq[r, m, :, c0 + c], start=True, stop=True)
                ins.then_inc(uv_ready, 1)

            def to_outputs(k):
                m, c0 = k // 4, GC * (k % 4)
                pe.wait_ge(state_ready, k + 1)
                if k == 0:
                    pe.wait_ge(toeplitz_in, 16 * 4)
                if k >= 2:
                    pe.wait_ge(y_copied, k - 1)
                for c in range(GC):
                    mc = 32 * m + c0 + c
                    for g in range(4):
                        r = slice(32 * g, 32 * g + 32)
                        o = bank[4 + k % 2][r, 64 * c:64 * c + 64]
                        pe.matmul(o, TP[r, mc, :], xq[r, m, :, c0 + c], start=True, stop=False)
                    for g in range(4):
                        r = slice(32 * g, 32 * g + 32)
                        o = bank[4 + k % 2][r, 64 * c:64 * c + 64].rearrange("p (b j) -> p b j", b=B)[:, :, 1:NJ]
                        ins = pe.matmul(o, F1[r, mc, 1:Q + 1], hc[k % 2][r, c, :, 0:NJ - 1], start=False, stop=True)
                ins.then_inc(y_ready, 1)

            to_states(0)
            for k in range(NG):
                if k + 1 < NG:
                    to_states(k + 1)
                to_outputs(k)
            for c in range(NCH):
                pe.wait_ge(gated, NCH * (MH - 1) + c + 1)
                if c == 0:
                    pe.wait_ge(wout_in, 16)
                    pe.wait_ge(y_copied, NG)
                for m in range(MH):
                    ins = pe.matmul(bank[4 + c][:, :], w_out[:, 128 * m:128 * m + 128], sz[:, m, tok(c)],
                                    start=(m == 0), stop=(m == MH - 1))
                ins.then_inc(out_ready, 1)

        def pool_ssm(pool):
            pool.memset(kpad, 0.0).then_inc(kpad_clear, 1)
            pool.wait_ge(kpad_clear, 1)
            pool.wait_ge(consts_in, 16)
            pool.wait_ge(rates_ready, 1)
            pool.tensor_tensor(m2, spread(A2, 2, Q + 1), spread(const(K_LROW, Q + 1), 1, 64), MUL).then_inc(mag_arg, 1)
            pool.wait_ge(turns_ready, 1)
            link(pool, pool.tensor_tensor(sin_j, spread(FR2, 2, NJ), spread(const(K_JROW, NJ), 1, 64), MUL))
            link(pool, pool.tensor_scalar(cos_j, sin_j, MAGIC, MAGIC, ADD, SUB))
            pool.tensor_tensor(sin_j, sin_j, cos_j, SUB).then_inc(block_turns, 1)
            pool.wait_ge(f_ready, 1)
            for k in range(NG):
                if k >= 2:
                    pool.wait_ge(state_ready, k - 1)
                at = 32 * (k // 4) + GC * (k % 4)
                r = rho_g[k % 2]
                link(pool, pool.tensor_copy(r.rearrange("p (c n) -> p c n", c=GC),
                                            spread(RHO[:, at:at + GC], 2, B * NJ)))
                pool.memset(r.rearrange("p (s j) -> p s j", j=NJ)[:, :, 0:1], 0.0).then_inc(rho_ready, 1)

        def act_ssm(act):
            def silu_x(n):
                act.wait_ge(xz_ready, n + 1)
                m, c = n // NCH, n % NCH
                o = u[:, m, tok(c)].rearrange("p (j q) -> p j q", q=Q)
                o = bass.AP(tensor=o.tensor, offset=o.offset + Q - 1, ap=[list(d) for d in o.ap][:2] + [[-1, Q]])
                act.activation(o, bank[n][:, :].rearrange("p (j q) -> p j q", q=Q), ACT.Silu,
                               bias=ssm_bias[:, m:m + 1]).then_inc(xz_out, 1)

            for n in range(NCH):
                silu_x(n)
            act.wait_ge(mag_arg, 1)
            act.activation(m2, m2, ACT.Exp).then_inc(looked_up, 1)
            act.preload_act_table_set("silu_and_others")
            act.wait_ge(turns_ready, 1)
            act.activation(SN2, FR2, ACT.Sin, scale=TWO_PI).then_inc(looked_up, 1)
            act.activation(SH2, FR2, ACT.Sin, scale=TWO_PI / 2).then_inc(looked_up, 1)
            act.wait_ge(turns_ready, 2)
            link(act, act.activation(h2, v2, ACT.Sin, scale=TWO_PI / 2))
            act.activation(s2, v2, ACT.Sin, scale=TWO_PI).then_inc(looked_up, 1)
            link(act, act.activation(h2, h2, ACT.Square, scale=2 ** 0.5))
            act.activation(h2, h2, ACT.Identity, scale=-1.0, bias=eps[:, 2:3]).then_inc(looked_up, 1)
            act.wait_ge(block_turns, 1)
            link(act, act.activation(cos_j, sin_j, ACT.Sin, scale=TWO_PI / 2))
            act.activation(sin_j, sin_j, ACT.Sin, scale=TWO_PI).then_inc(blocks_looked_up, 1)
            link(act, act.activation(cos_j, cos_j, ACT.Square, scale=2 ** 0.5))
            act.activation(cos_j, cos_j, ACT.Identity, scale=-1.0, bias=eps[:, 2:3]).then_inc(blocks_looked_up, 1)
            for n in range(NCH, MH * NCH):
                silu_x(n)
            for n in range(MH * NCH, 2 * MH * NCH):
                act.wait_ge(xz_ready, n + 1)
                m, c = n // NCH, n % NCH
                act.activation(sz[:, m - MH, tok(c)], bank[n % 8][:, :], ACT.Silu).then_inc(xz_out, 1)
            for k in range(NG):
                m, c0 = k // 4, GC * (k % 4)
                act.wait_ge(y_ready, k + 1)
                act.activation(ysb[:, m, :, c0:c0 + GC],
                               bank[4 + k % 2][:, :].rearrange("p (c t) -> p t c", c=GC), ACT.Copy).then_inc(y_copied, 1)

        (dt2, W2, FR2, SN2, SH2, NR, NI, DBR, DBI, CR, CI, p1, p2, t1, t2, t3) = (small[:, i, :] for i in range(16))
        rates, ex2, em2 = small[:, 16:18], small[:, 18:20], small[:, 20:22]
        scaled_rates, exp_tmp, exp_scale = small[:, 22:24], [small[:, n:n + 2] for n in (24, 26)], small[:, 14:16]
        A2, EA, EM1, RHO = rates[:, 0], ex2[:, 0], em2[:, 0], ex2[:, 1]
        are, aim, cre, cim, ldt = (par_state[:, i, :] for i in range(5))
        mre, mim, q31 = const(K_MRE, 1), const(K_MIM, 1), const(K_Q31, 1)

        def exact_exp(dve, x, ex, em1, tmp, scale_i):
            k, r, p = tmp
            link(dve, dve.tensor_scalar(x, x, -150.0, 88.0, ALU.max, ALU.min))
            link(dve, dve.tensor_scalar(k, x, LOG2E, MAGIC, MUL, ADD))
            link(dve, dve.tensor_scalar(k, k, MAGIC, None, SUB))
            link(dve, dve.scalar_tensor_tensor(r, k, -LN2H, x, MUL, ADD))
            link(dve, dve.scalar_tensor_tensor(r, k, -LN2L, r, MUL, ADD))
            link(dve, dve.tensor_scalar(p, r, 1 / 5040, None, MUL))
            for co in (1 / 720, 1 / 120, 1 / 24, 1 / 6, 0.5, 1.0):
                link(dve, dve.scalar_tensor_tensor(p, p, co, r, ADD, MUL))
            link(dve, dve.tensor_scalar(scale_i, k, -127.0, 127.0, ALU.max, ADD))
            link(dve, dve.tensor_scalar(scale_i, scale_i, 23, None, ALU.logical_shift_left))
            s = scale_i.bitcast(f32)
            link(dve, dve.tensor_tensor(p, p, s, MUL))
            if em1 is not None:
                link(dve, dve.tensor_scalar(r, s, 1.0, None, SUB))
                link(dve, dve.tensor_tensor(em1, p, r, ADD))
            link(dve, dve.tensor_tensor(ex, p, s, ADD))

        def to_turns(dve, f, w, k):
            link(dve, dve.tensor_scalar(k, w, 1 / (2 * np.pi), MAGIC, MUL, ADD))
            link(dve, dve.tensor_scalar(k, k, MAGIC, None, SUB))
            for part in (C1, C2, C3):
                link(dve, dve.scalar_tensor_tensor(w, k, -part, w, MUL, ADD))
            return dve.tensor_scalar(f, w, 1 / (2 * np.pi), None, MUL)

        def wrap(dve, v, k):
            link(dve, dve.tensor_scalar(k, v, MAGIC, MAGIC, ADD, SUB))
            link(dve, dve.tensor_tensor(v, v, k, SUB))

        def dve_tables(dve):
            for n, v in enumerate((EPS_LN, EPS_RMS, 1.0)):
                dve.memset(eps[:, n:n + 1], v)
            for side in (slice(0, WIN), slice(WIN + L, LP)):
                dve.memset(xn[:, :, side], 0.0).then_inc(w_conv_ready, 1)
            dve.wait_ge(par_in, 16)
            link(dve, dve.tensor_copy(t1, ldt))
            exact_exp(dve, t1, dt2, None, (small[:, 24], small[:, 26], small[:, 27]), small[:, 25].bitcast(i32))
            link(dve, dve.tensor_tensor(W2, dt2, aim, MUL))
            dve.tensor_tensor(A2, dt2, are, MUL).then_inc(rates_ready, 1)
            dve.wait_ge(rates_ready, 1)
            dve.wait_ge(weights_in, 32)
            dve.tensor_tensor(w_conv, conv_row, spread(w_in[:, 0:DIN], 1, 4), MUL).then_inc(w_conv_ready, 1)
            to_turns(dve, FR2, W2, t1).then_inc(turns_ready, 1)
            dve.wait_ge(turns_ready, 1)
            dve.wait_ge(consts_in, 16)
            lrow = spread(const(K_LROW, Q + 1), 1, 64)
            link(dve, dve.tensor_tensor(v2, spread(FR2, 2, Q + 1), lrow, MUL))
            link(dve, dve.tensor_scalar(s2, v2, MAGIC, MAGIC, ADD, SUB))
            dve.tensor_tensor(v2, v2, s2, SUB).then_inc(turns_ready, 1)
            link(dve, dve.tensor_copy(scaled_rates[:, 0], A2))
            link(dve, dve.tensor_scalar(scaled_rates[:, 1], A2, float(Q), None, MUL))
            exact_exp(dve, scaled_rates, ex2, em2, (exp_tmp[0], exp_tmp[1], small[:, 12:14]), exp_scale.bitcast(i32))
            dve.wait_ge(looked_up, 3)
            link(dve, dve.scalar_tensor_tensor(t1, SH2, -2.0, SH2, MUL, MUL))
            link(dve, dve.tensor_tensor(t1, t1, EA, MUL))
            link(dve, dve.tensor_tensor(NR, t1, EM1, ADD))
            link(dve, dve.tensor_tensor(NI, EA, SN2, MUL))
            link(dve, dve.tensor_tensor(t1, are, are, MUL))
            link(dve, dve.tensor_tensor(t2, aim, aim, MUL))
            link(dve, dve.tensor_tensor(t1, t1, t2, ADD))
            link(dve, dve.reciprocal(t3, t1))

            def cmul(re, im, ar, ai, br, bi, conj):
                link(dve, dve.tensor_tensor(t1, ar, br, MUL))
                link(dve, dve.tensor_tensor(t2, ai, bi, MUL))
                link(dve, dve.tensor_tensor(re, t1, t2, ADD if conj else SUB))
                link(dve, dve.tensor_tensor(t1, ai, br, MUL))
                link(dve, dve.tensor_tensor(t2, ar, bi, MUL))
                link(dve, dve.tensor_tensor(im, t1, t2, SUB if conj else ADD))

            cmul(DBR, DBI, NR, NI, are, aim, True)
            link(dve, dve.tensor_tensor(DBR, DBR, t3, MUL))
            link(dve, dve.tensor_tensor(DBI, DBI, t3, MUL))
            cmul(CR, CI, DBR, DBI, cre, cim, False)
            link(dve, dve.tensor_scalar(t1, CI, mim, -2.0, MUL, MUL))
            link(dve, dve.tensor_scalar(t2, CR, mre, 2.0, MUL, MUL))
            link(dve, dve.tensor_tensor(p1, t1, t2, ADD))
            link(dve, dve.tensor_scalar(t1, CI, mre, -2.0, MUL, MUL))
            link(dve, dve.tensor_scalar(t2, CR, mim, -2.0, MUL, MUL))
            link(dve, dve.tensor_tensor(p2, t1, t2, ADD))
            dve.wait_ge(looked_up, 5)
            link(dve, dve.tensor_tensor(h2, h2, m2, MUL))
            link(dve, dve.tensor_tensor(s2, s2, m2, MUL))
            dve.tensor_tensor(F1, h2, spread(p1, 2, Q + 1), MUL)
            link(dve, dve.tensor_tensor(m2, s2, spread(p2, 2, Q + 1), MUL))
            dve.tensor_tensor(F1, F1, m2, ADD).then_inc(f_ready, 1)
            dve.wait_ge(f_ready, 1)
            xr, yr = h2[:, :, 0:Q], s2[:, :, 0:Q]
            eu, ev = (w[:, 0:2048].rearrange("p (c l) -> p c l", l=Q) for w in tmpw[:2])
            link(dve, dve.tensor_scalar(eu, xr, mre, None, MUL))
            dve.scalar_tensor_tensor(eu, yr, mim, eu, MUL, ADD)
            link(dve, dve.tensor_scalar(ev, xr, mim, -1.0, MUL, MUL))
            link(dve, dve.scalar_tensor_tensor(ev, yr, mre, ev, MUL, ADD))
            flat = "p c l -> p (c l)"
            dve.transpose(EU.rearrange(flat), eu.rearrange(flat))
            dve.transpose(EV.rearrange(flat), ev.rearrange(flat)).then_inc(e_ready, 1)
            dve.wait_ge(e_ready, 1)
            dve.wait_ge(xz_out, NCH)
            dve.transpose(xq[:, 0].rearrange("p b c -> p (b c)"), u[:, 0, :]).then_inc(xq_ready, 1)
            dve.wait_ge(kpad_clear, 1)
            dve.wait_ge(d_in, 16)
            for n in range(4):
                dve.wait_ge(taps_ready, n + 1)
                ins = dve.tensor_copy(kpad[:, 16 * n:16 * n + 16, Q - 1:2 * Q - 1],
                                      bank[n][0:4, :].rearrange("p (c l) -> p c l", l=Q))
            link(dve, ins)
            dve.tensor_tensor(kpad[:, :, Q - 1], kpad[:, :, Q - 1], d_skip, ADD).then_inc(taps_copied, 1)
            dve.wait_ge(xz_out, MH * NCH)
            dve.transpose(xq[:, 1].rearrange("p b c -> p (b c)"), u[:, 1, :]).then_inc(xq_ready, 1)
            dve.wait_ge(blocks_looked_up, 2)

        def dve_ssm(dve):
            def turn_back(m):
                dve.wait_ge(y_copied, 4 * (m + 1))
                dve.wait_ge(taps_out, 16)
                link(dve, dve.transpose(y_t[:, m].rearrange("p b c -> p (b c)"),
                                        ysb[:, m].rearrange("p b c -> p (b c)")))

            def gate(m):
                yt = y_t[:, m].rearrange("p b c -> p (b c)")
                dve.wait_ge(xz_out, NCH * (MH + m + 1))
                for c in range(NCH):
                    dve.tensor_tensor(sz[:, m, tok(c)], yt[:, tok(c)], sz[:, m, tok(c)], MUL).then_inc(gated, 1)

            for k in range(NG):
                m, c0 = k // 4, GC * (k % 4)
                cj = spread(cos_j[:, 32 * m + c0:32 * m + c0 + GC, :], 2, B)
                sj = spread(sin_j[:, 32 * m + c0:32 * m + c0 + GC, :], 2, B)
                g4 = "p (c b j) -> p c b j"
                pa4, pb4, pc4, pd4 = (v.rearrange(g4, c=GC, b=B) for v in (pa, pb_, pc, pd))
                uk, vk = (bank[b0 + k % 2][:, :].rearrange(g4, c=GC, b=B) for b0 in (0, 2))
                if k >= 1:
                    dve.wait_ge(state_ready, k)
                dve.wait_ge(uv_ready, k + 1)
                dve.tensor_tensor(pa4, uk, cj, MUL)
                dve.tensor_tensor(pb4, vk, sj, MUL)
                dve.tensor_tensor(pc4, vk, cj, MUL)
                dve.tensor_tensor(pd4, uk, sj, MUL).then_inc(uv_used, 1)
                dve.wait_ge(uv_used, k + 1)
                dve.tensor_tensor(pa, pa, pb_, ADD)
                link(dve, dve.tensor_tensor(pc, pc, pd, SUB))
                dve.wait_ge(rho_ready, k + 1)
                dve.tensor_tensor_scan(pb_, rho_g[k % 2], pa, 0.0, MUL, ADD)
                link(dve, dve.tensor_tensor_scan(pd, rho_g[k % 2], pc, 0.0, MUL, ADD))
                dve.tensor_tensor(pa4, pb4, cj, MUL)
                link(dve, dve.tensor_tensor(pc4, pd4, sj, MUL))
                if k >= 2:
                    dve.wait_ge(y_ready, k - 1)
                dve.tensor_tensor(hc[k % 2], pa4, pc4, SUB).then_inc(state_ready, 1)
                if k == 5:
                    turn_back(0)
                if k == 6:
                    gate(0)
            turn_back(1)
            gate(1)
            dve.wait_ge(first_in, 16)
            for c in range(NCH):
                dve.wait_ge(out_ready, c + 1)
                dve.tensor_tensor(X[:, tok(c)], X[:, tok(c)], bank[4 + c][:, :], ADD).then_inc(resid_ready, 1)

        logits = place(0, NT, E1)
        kept = place(1024, NT, E1)
        cw2 = place(2048, NT, 2, E1)
        best = place(4096, NT, 8)
        rowv = place(4224, 3, NT)
        cwt = place(4352, T)
        cw_halves = place_half(6400, T)
        hid = [place(8448 + CH * n, CH) for n in range(3)]
        hidw = [place(9984 + CH * n, CH) for n in range(3)]
        W0 = MH * T * 3 + 512
        NB1 = KB1 + KBS
        m1_w2 = place(W0, NB1, 128)
        sel1_f = place(W0 + 128 * NB1, KB1, 128)
        W0 += 128 * (NB1 + KB1)
        sel1 = place_half(W0, KB1, 128)
        W0 += 128 * KB1
        w1_halves = [place_half(W0 + 128 * NB1 * n, NB1, 128) for n in range(2)]
        W0 += 128 * NB1 * 2
        w2_halves = [place_half(W0, NB1, 128), place_half(W0 - 128 * (NB1 * 3 + KB1 * 2), NB1, 128)]
        W0 += 128 * NB1
        x_halves = [[place_half(W0 + CH * (2 * n + a), CH) for a in range(2)] for n in range(2)]
        h_halves = [[place_half(W0 + 2048 + CH * (2 * n + a), CH) for a in range(2)] for n in range(3)]
        m1_w1, m1_b1 = wts["m1_w1"], wts["m1_b1"]
        shared, routed = list(range(KB1, NB1)), list(range(KB1))
        steps1 = [(c, kb) for c in (0, 1) for kb in shared] + [(c, kb) for c in (0, 1) for kb in routed]
        steps1 += [(c, kb) for c in (2, 3) for kb in shared + routed]
        before = [sum(kb < KB1 for c, kb in steps1[:n]) for n in range(len(steps1) + 1)]
        FIRST1, POOL1 = 2 * KBS, 5
        first_of = [steps1.index((c, KB1)) for c in range(NCH)]
        last_of = [max(n for n, s in enumerate(steps1) if s[0] == c) for c in range(NCH)]
        w_groups = [KB1] + list(range(0, KB1, 4))
        w_split, x_split, high_done, split_done = (
            sem(n) for n in ("w_split", "x_split", "hidden_high", "hidden_split"))
        route_ready, cw_ready, cwt_ready, cwt_split = (
            sem(n) for n in ("route_ready", "cw_ready", "cwt_ready", "cwt_split"))
        soft_in, soft_out = sem("soft_in"), sem("soft_out")
        up_ready, silu_done, spread_ready, scaled, m1_out, sel_cast = (
            sem(n) for n in ("up_ready", "silu_done", "spread_ready", "scaled", "m1_out", "sel_cast"))
        late_in = sem("late_in")

        def sp_moe1(sp):
            names = [n for n in wts]
            for n in names:
                sp.dma_start(wts[n][:, :], dram[n]).then_inc(m1_in, 16)
            sp.wait_ge(y_ready, NG)
            sp.dma_start(m1_w2, dram["m1_w2"].rearrange("p (a b) -> p a b", b=128)).then_inc(late_in, 16)
            sp.dma_start(sel1_f, dram["sel1"].rearrange("p (a b) -> p a b", b=128)).then_inc(late_in, 16)

        def pe_moe1(pe):
            pe.wait_ge(m1_in, 16 * len(wts))
            for t in range(NT):
                pe.wait_ge(normed, t // 4 + 1)
                ins = pe.matmul(bank[t // 8][:, 64 * (t % 8):64 * (t % 8) + 64], X[:, 128 * t:128 * t + 128],
                                wts["r1_w"][:, :], start=True, stop=True)
                if t % 8 == 7:
                    ins.then_inc(route_ready, 1)

            def turn(g):
                if g == 0:
                    pe.wait_ge(cw_ready, 1)
                if g >= 2:
                    pe.wait_ge(cwt_split, g - 1)
                for t in range(4 * g, 4 * g + 4):
                    ins = pe.transpose(bank[3 + g % 2][:, 128 * (t % 4):128 * (t % 4) + 128],
                                       cw2[:, t].rearrange("p a e -> p (a e)"), const(K_ID, 128))
                ins.then_inc(cwt_ready, 1)

            def up(n):
                c, kb = steps1[n]
                if n == POOL1 + 1:
                    turn(0)
                    turn(1)
                if n < 3:
                    pe.wait_ge(soft_in, 1)
                if n >= 3:
                    pe.wait_ge(silu_done, n - 2)
                pe.wait_ge(x_split, c + 1)
                pe.wait_ge(w_split, 2 * w_groups.index(kb // 4 * 4) + 1)
                product(pe, bank[n % 3][:, :], [w[:, kb] for w in w1_halves], x_halves[c % 2], True, True)\
                    .then_inc(up_ready, 1)
                if kb < KB1:
                    r = before[n]
                    if r == 0:
                        turn(2)
                        turn(3)
                        pe.wait_ge(cwt_split, NCH)
                        pe.wait_ge(sel_cast, 1)
                    if r >= 3:
                        pe.wait_ge(scaled, r - 2)
                    pe.matmul(bank[3 + r % 3][:, :], sel1[:, kb, :], cw_halves[:, tok(c)], start=True, stop=True)\
                        .then_inc(spread_ready, 1)

            def down(n):
                c, kb = steps1[n]
                if n == first_of[c] and c >= 2:
                    pe.wait_ge(resid_ready, NCH + c - 1)
                if n == 0:
                    pe.wait_ge(normed, NCH)
                pe.wait_ge(w_split, 2 * w_groups.index(kb // 4 * 4) + 2)
                pe.wait_ge(split_done, n + 1)
                product(pe, bank[6 + c % 2][:, :], [w[:, kb] for w in w2_halves], h_halves[n % 3],
                        n == first_of[c], False).then_inc(down_done, 1)
                if n == last_of[c]:
                    pe.matmul(bank[6 + c % 2][:, :], wts["m1_b2"][:, :], cwt[0:E1 + ES, tok(c)],
                              start=False, stop=True).then_inc(m1_out, 1)

            for n in range(3):
                up(n)
            for n in range(len(steps1)):
                if n + 3 < len(steps1):
                    up(n + 3)
                down(n)

        def pool_moe1(pool):
            pool.wait_ge(m1_in, 16 * len(wts))
            pool.wait_ge(late_in, 32)
            w1 = m1_w1[:, :].rearrange("p (a b) -> p a b", b=128)
            def weights(g):
                r = slice(w_groups[g], w_groups[g] + 4)
                halve(pool, w1_halves[0][:, r], w1_halves[1][:, r], w1[:, r], w_split)
                halve(pool, w2_halves[0][:, r], w2_halves[1][:, r], m1_w2[:, r], w_split)

            def chunk(c):
                pool.wait_ge(normed, c + 1)
                if c >= 2:
                    pool.wait_ge(up_ready, last_of[c - 2] + 1)
                halve(pool, x_halves[c % 2][0], x_halves[c % 2][1], X[:, tok(c)], x_split)

            weights(0)
            weights(1)
            chunk(0)
            chunk(1)
            for n in range(POOL1):
                low_half(pool, n)
            pool.tensor_copy(sel1, sel1_f).then_inc(sel_cast, 1)
            for g in range(2, len(w_groups)):
                weights(g)
            chunk(2)
            chunk(3)

        def low_half(eng, n):
            kb = steps1[n][1]
            if kb < KB1:
                eng.wait_ge(high_done, before[n] + 1)
            else:
                eng.wait_ge(silu_done, n + 1)
            if n >= 3:
                eng.wait_ge(down_done, n - 2)
            high, low = h_halves[n % 3]
            eng.tensor_tensor(low, (hidw if kb < KB1 else hid)[n % 3], high.bitcast(f32), SUB)\
                .then_inc(split_done, 1)

        def act_moe1(act):
            act.wait_ge(soft_in, 2)
            act.activation(logits, logits, ACT.Exp).then_inc(soft_out, 1)
            for n in range(len(steps1) + 1):
                if n < len(steps1):
                    c, kb = steps1[n]
                    act.wait_ge(up_ready, n + 1)
                    b1 = m1_b1[:, kb:kb + 1]
                    if n >= 3:
                        if steps1[n - 3][1] < KB1:
                            act.wait_ge(scaled, before[n - 2])
                        else:
                            act.wait_ge(split_done, n - 2)
                    ins = act.activation(hid[n % 3], bank[n % 3][:, :], ACT.Silu, bias=b1)
                    if kb >= KB1:
                        if n >= 3:
                            act.wait_ge(down_done, n - 2)
                        ins = act.activation(h_halves[n % 3][0], bank[n % 3][:, :], ACT.Silu, bias=b1)
                    ins.then_inc(silu_done, 1)
                if n >= 1 and steps1[n - 1][1] < KB1:
                    m = n - 1
                    act.wait_ge(scaled, before[m] + 1)
                    act.wait_ge(down_done, m - 2)
                    act.activation(h_halves[m % 3][0], hidw[m % 3], ACT.Copy).then_inc(high_done, 1)

        down_done = sem("down_done")

        def dve_moe1(dve):
            dve.wait_ge(m1_in, 16 * len(wts))
            for h in range(2):
                dve.wait_ge(route_ready, h + 1)
                ins = dve.tensor_tensor(logits[:, 8 * h:8 * h + 8], bank[h][:, :].rearrange("p (t e) -> p t e", e=E1),
                                        spread(wts["r1_b"][:, :], 1, 8), ADD)
                if h == 0:
                    link(dve, ins)
            ins.then_inc(soft_in, 1)
            dve.wait_ge(soft_in, 1)
            link(dve, dve.tensor_reduce(rowv[:, 0], logits, AX.X, ALU.max))
            dve.tensor_tensor(logits, logits, spread(rowv[:, 0], 2, E1), SUB).then_inc(soft_in, 1)
            link(dve, dve.memset(cwt[64:96, :], 1.0))
            dve.wait_ge(soft_out, 1)
            for t in range(NT):
                ins = dve.max(best[:, t], logits[:, t])
            link(dve, ins)
            for t in range(NT):
                ins = dve.match_replace(kept[:, t], best[:, t], logits[:, t], 0.0)
            link(dve, ins)
            link(dve, dve.tensor_tensor(kept, logits, kept, SUB))
            link(dve, dve.tensor_reduce(rowv[:, 1], kept, AX.X, ADD))
            link(dve, dve.reciprocal(rowv[:, 2], rowv[:, 1]))
            link(dve, dve.tensor_tensor(cw2[:, :, 0], kept, spread(rowv[:, 2], 2, E1), MUL))
            dve.tensor_copy(cw2[:, :, 1], cw2[:, :, 0]).then_inc(cw_ready, 1)
            for g in range(NCH):
                dve.wait_ge(cwt_ready, g + 1)
                w, o = bank[3 + g % 2], cw_halves[:, tok(g)]
                dve.tensor_copy(cwt[0:64, tok(g)], w[0:64, :])
                link(dve, dve.tensor_copy(o, w[:, :]))
                dve.tensor_tensor(o[64:128], w[64:128, :], o[64:128].bitcast(f32), SUB).then_inc(cwt_split, 1)
                if g == 1:
                    dve.wait_ge(split_done, POOL1)
                    for n in range(POOL1, FIRST1):
                        low_half(dve, n)

            def result(c):
                dve.wait_ge(m1_out, c + 1)
                dve.tensor_tensor(X[:, tok(c)], X[:, tok(c)], bank[6 + c % 2][:, :], ADD).then_inc(resid_ready, 1)

            N = len(steps1)
            for n in range(N + 5):
                if n < N and steps1[n][1] < KB1:
                    dve.wait_ge(silu_done, n + 1)
                    dve.wait_ge(spread_ready, before[n] + 1)
                    dve.wait_ge(split_done, n - 2)
                    dve.tensor_tensor(hidw[n % 3], hid[n % 3], bank[3 + before[n] % 3][:, :], MUL).then_inc(scaled, 1)
                if FIRST1 < n <= N:
                    low_half(dve, n - 1)
                if n - 5 in last_of:
                    result(last_of.index(n - 5))

        q9 = [place(8448 * b, H, NL * QL, dt=bf16) for b in range(B)]
        k9 = [place(16896 + 2176 * b, KVH, LP, dt=bf16) for b in range(B)]
        vt = place(21248, B * NL, KVH, 32)
        rope = place(24064, 2, L + CH)
        parts = [place(27136 + 768 * n, 3, CH, dt=bf16) for n in range(3)]
        rot = [work[:, CH * n:CH * n + CH] for n in range(5)]
        rot2 = work[:, CH * 5:CH * 6]
        rtm = [work[:, CH * n:CH * n + CH] for n in (6, 11)]
        rsq = [work[:, CH * n:CH * n + CH] for n in (7, 8)]
        rgs = [work[:, CH * n:CH * n + CH] for n in (9, 10)]
        lat = work[0:LAT, CH * 12:CH * 16]
        RING = 6
        probs = [work[:, 2 * CH * n:2 * CH * n + 2 * CH] for n in range(RING)]
        osb = [work[:, CH * n:CH * n + CH] for n in (12, 13)] + [place(30000 + T, CH)]
        onrm = [work[:, CH * n:CH * n + CH] for n in (14, 15)]
        rec, rec2 = [place(29440, CH), place(27136 + CH, CH)], place(27136, CH)
        q_dram = [nc.dram_tensor(f"q_parts{n}", (3, 128, T), bf16, kind="Internal").ap() for n in range(2)]
        k_dram = [nc.dram_tensor(f"k_parts{n}", (3, 32, T), bf16, kind="Internal").ap() for n in range(2)]
        lat_ready, lat_copied, v_ready, v_copied = (sem(n) for n in ("lat_ready", "lat_copied", "v_ready", "v_copied"))
        rope_in, pr_ready, rot_ready, rsq_ready, ms_ready, gs_ready, parts_ready = (
            sem(n) for n in ("rope_in", "pr_ready", "rot_ready", "rsq_ready", "ms_ready", "gs_ready", "parts_ready"))
        parts_out = [sem(f"parts_out{n}") for n in range(3)]
        k_in = [sem(f"k_in{b}") for b in range(B)]
        q_in = [sem(f"q_in{c}") for c in range(NCH)]
        pads = sem("pads")
        normed9, high_ready, rest_ready, mid_ready = (
            sem(n) for n in ("item_normed", "high_ready", "rest_ready", "mid_ready"))
        x_in = place(30000, T)
        x_kept, x_added = sem("x_kept"), sem("x_added")

        def pool_attn(pool):
            pool.wait_ge(x_split, NCH)
            pool.wait_ge(normed, 2 * NCH)
            for b in range(B):
                link(pool, pool.memset(arena[64:128, 8448 * b:8448 * b + 8448], 0.0))
                link(pool, pool.memset(arena[64:128, 16896 + 2176 * b:16896 + 2176 * b + 2176], 0.0))
                pool.memset(k9[b][0:64, :, 0:WIN], 0.0)
                pool.memset(k9[b][0:64, :, WIN + L:LP], 0.0)
                pool.memset(q9[b][0:64, :, L:NL * QL], 0.0).then_inc(pads, 1)
                pool.wait_ge(pads, b + 1)
            for c in range(NCH):
                pool.tensor_copy(x_in[:, tok(c)], X[:, tok(c)]).then_inc(x_kept, 1)
            pool_parts(pool, 0)
            for c in range(NCH):
                pool.wait_ge(x_kept, c + 1)
                pool.wait_ge(normed, NCH * 3 + c + 1)
                pool.tensor_tensor(X[:, tok(c)], X[:, tok(c)], x_in[:, tok(c)], ADD).then_inc(x_added, 1)
            pool_parts(pool, 1)
            pool_core(pool)

        def pool_parts(pool, n):
            for i in range(NIT + 1):
                if i < NIT:
                    j = NIT * n + i
                    pool.wait_ge(high_ready, j + 1)
                    pool.tensor_tensor(rot[i], rot[i], parts[slot_of[j]][:, 0], SUB).then_inc(rest_ready, 1)
                if i >= 1:
                    j = NIT * n + i - 1
                    pool.wait_ge(mid_ready, j + 1)
                    pool.tensor_tensor(parts[slot_of[j]][:, 2], rot[i - 1], parts[slot_of[j]][:, 1], SUB)\
                        .then_inc(parts_ready, 1)
        scores_ready, exp_done, masked, pv_done, guessed = (
            sem(n) for n in ("scores_ready", "exp_done", "masked", "pv_done", "den_guessed"))
        masked_by_pool, den_read = sem("masked_by_pool"), sem("den_read")
        osb_ready, den_ready, on_ready, wo_ready, added = (
            sem(n) for n in ("osb_ready", "den_ready", "on_ready", "wo_ready", "added"))
        NIT = 1 + NCH
        sends = [KVH if i == 0 else 1 for i in range(NIT)] * 2
        slot_of = [j % 3 for j in range(2 * NIT)]

        def sent(j):
            return 16 * sum(sends[m] for m in range(j + 1) if slot_of[m] == slot_of[j])

        def item_banks(i):
            return [(4, 5), (2, 3), (0, 1), (2, 3), (0, 1)][i]

        def sp_attn(sp, n):
            if n == 0:
                sp.wait_ge(normed, 2 * NCH)
            else:
                sp.wait_ge(parts_ready, NIT)
            sp.dma_start(rope, dram["rope"][n]).then_inc(rope_in, 16)
            if n == 1:
                sp.wait_ge(pv_done, UG)

            def send(i):
                j = NIT * n + i
                sp.wait_ge(parts_ready, j + 1)
                p = parts[slot_of[j]]
                if i == 0:
                    for c in range(NCH):
                        sp.dma_start(k_dram[n][:, :, tok(c)].rearrange("a r t -> r a t"), p[32 * c:32 * c + 32])\
                            .then_inc(parts_out[slot_of[j]], 16)
                else:
                    sp.dma_start(q_dram[n][:, :, tok(i - 1)].rearrange("a r t -> r a t"), p)\
                        .then_inc(parts_out[slot_of[j]], 16)

            def fetch_k(b):
                sp.wait_ge(parts_out[slot_of[NIT * n]], sent(NIT * n))
                sp.wait_ge(pads, b + 1)
                for a in range(3):
                    for c in range(3):
                        r = slice((3 * a + c) * HD, (3 * a + c) * HD + HD)
                        sp.dma_start(k9[b][r, :, WIN:WIN + L], k_dram[n][a, :, L * b:L * b + L]
                                     .rearrange("(h d) t -> d h t", d=HD)).then_inc(k_in[b], 16)

            def fetch_q(ch):
                j = NIT * n + 1 + ch
                sp.wait_ge(parts_out[slot_of[j]], sent(j))
                b, t0 = ch // 2, ch % 2 * CH
                for a in range(3):
                    for c in range(3):
                        r = slice((3 * a + c) * HD, (3 * a + c) * HD + HD)
                        sp.dma_start(q9[b][r, :, t0:t0 + CH], q_dram[n][c, :, tok(ch)]
                                     .rearrange("(h d) t -> d h t", d=HD)).then_inc(q_in[ch], 16)

            send(0)
            send(1)
            fetch_k(0)
            fetch_q(0)
            send(2)
            send(3)
            send(4)
            fetch_q(1)
            fetch_k(1)
            fetch_q(2)
            fetch_q(3)

        def v_tiles(n):
            return [(b, i) for b in range(B) for i in range(NL if n else NQT)]

        def pe_proj(pe, n):
            kv, q = (wts["g_kv"], wts["g_q"]) if n == 0 else (wts["l_kv"], wts["l_q"])
            for c in range(NCH):
                pe.wait_ge(normed, NCH * (2 + n) + c + 1)
                if n == 0:
                    if c >= 2:
                        pe.wait_ge(lat_copied, c - 1)
                    pe.matmul(bank[c % 2][0:LAT, :], wts["g_down"][:, :], xn_tok(c), start=True, stop=True)\
                        .then_inc(lat_ready, 1)
            if n == 0:
                pe.wait_ge(lat_copied, NCH)
            def project(i):
                j = NIT * n + i
                b0, b1 = item_banks(i)
                if i >= 3:
                    pe.wait_ge(rot_ready, j - 1)
                if i == 0:
                    for w, bk in ((0, b0), (32, b1)):
                        for c in range(NCH):
                            x = lat[:, tok(c)] if n == 0 else xn_tok(c)
                            ins = pe.matmul(bank[bk][32 * c:32 * c + 32, :], kv[:, w:w + 32], x, start=True, stop=True)
                else:
                    for w, bk in ((0, b0), (128, b1)):
                        ins = pe.matmul(bank[bk][:, :], q[:, w:w + 128], xn_tok(i - 1), start=True, stop=True)
                ins.then_inc(pr_ready, 1)

            def mean_square(i):
                j = NIT * n + i
                pe.wait_ge(rsq_ready, j + 1)
                if i >= 2:
                    pe.wait_ge(normed9, j - 1)
                pe.matmul(bank[6 + i % 2][:, :], const(K_HEAD, 128), rsq[i % 2], start=True, stop=True)\
                    .then_inc(ms_ready, 1)

            project(0)
            project(1)
            for i in range(NIT):
                mean_square(i)
                if i + 2 < NIT:
                    project(i + 2)
                if i == 2:
                    for t, (b, m) in enumerate(v_tiles(n)):
                        l = lat[:, (NQT * b + m) * 128:][:, 0:128] if n == 0 else xn[:, b, QL * m:QL * m + 128]
                        ins = pe.matmul(bank[4 + t // 16][:, 32 * (t % 16):32 * (t % 16) + 32], l, kv[:, 64:96],
                                        start=True, stop=True)
                    ins.then_inc(v_ready, 1)

        def act_proj(act, n):
            if n == 0:
                for c in range(NCH):
                    act.wait_ge(lat_ready, c + 1)
                    act.activation(lat[:, tok(c)], bank[c % 2][0:LAT, :], ACT.Copy).then_inc(lat_copied, 1)

            def squares(i):
                j = NIT * n + i
                act.wait_ge(rot_ready, j + 1)
                if i >= 2:
                    act.wait_ge(ms_ready, j - 1)
                act.activation(rsq[i % 2], rot[i], ACT.Square).then_inc(rsq_ready, 1)

            def part(i, m):
                j = NIT * n + i
                act.wait_ge((normed9, rest_ready)[m], j + 1)
                if m == 0 and j >= 3:
                    act.wait_ge(parts_out[slot_of[j]], sent(j - 3))
                act.activation(parts[slot_of[j]][:, m], rot[i], ACT.Copy).then_inc((high_ready, mid_ready)[m], 1)

            squares(0)
            squares(1)
            for i in range(NIT + 2):
                if i < NIT:
                    j = NIT * n + i
                    act.wait_ge(ms_ready, j + 1)
                    if i >= 2:
                        act.wait_ge(normed9, j - 1)
                    link(act, act.activation(rgs[i % 2], bank[6 + i % 2][:, :], ACT.Ln, bias=eps[:, 1:2]))
                    link(act, act.activation(rgs[i % 2], rgs[i % 2], ACT.Exp, scale=-0.5))
                    act.activation(rtm[i % 2], rgs[i % 2], ACT.Square).then_inc(gs_ready, 1)
                if i + 2 < NIT:
                    squares(i + 2)
                if 1 <= i <= NIT:
                    part(i - 1, 0)
                if i >= 2:
                    part(i - 2, 1)

        def dve_proj(dve, n):
            if n == 1:
                dve.wait_ge(pv_done, UG)
            link(dve, dve.memset(vt, 1.0))
            if n == 1:
                for b in range(B):
                    link(dve, dve.memset(vt[0:WIN, NL * b], 0.0))
            dve.wait_ge(rope_in, 16 * (n + 1))

            def rotate(i):
                j = NIT * n + i
                b0, b1 = item_banks(i)
                at = L if i == 0 else (i - 1) % 2 * CH
                dve.wait_ge(pr_ready, j + 1)
                if n:
                    dve.wait_ge(parts_ready, NIT)
                r = rot[i]
                link(dve, dve.tensor_tensor(r, bank[b0][:, :], rope[:, 0, at:at + CH], MUL))
                link(dve, dve.tensor_tensor(rot2, bank[b1][:, :], rope[:, 1, at:at + CH], MUL))
                dve.tensor_tensor(r, r, rot2, ADD).then_inc(rot_ready, 1)

            def finish(i):
                j = NIT * n + i
                r = rot[i]
                dve.wait_ge(gs_ready, j + 1)
                rsqrt_step(dve, rgs[i % 2], rtm[i % 2], bank[6 + i % 2][:, :], EPS_RMS)
                dve.scalar_tensor_tensor(r, r, -0.5, rgs[i % 2], MUL, MUL).then_inc(normed9, 1)

            rotate(0)
            rotate(1)
            for i in range(NIT):
                if i + 2 < NIT:
                    rotate(i + 2)
                finish(i)
            dve.wait_ge(v_ready, n + 1)
            nt = len(v_tiles(n))
            for t0 in range(0, nt, 16):
                m = min(16, nt - t0)
                ins = dve.tensor_copy(vt[:, t0:t0 + m, :, 0:HD], bank[4 + t0 // 16][:, 0:32 * m]
                                      .rearrange("p (t k d) -> p t k d", k=KVH, d=HD))
            ins.then_inc(v_copied, 1)

        def tiles(n):
            if n == 0:
                return [(b, t, t + 1) for b in range(B) for t in range(NQT)]
            return [(b, t, 1) for b in range(B) for t in range(NL)]

        def units(n):
            return [(o, kt) for o, (b, t, nk) in enumerate(tiles(n)) for kt in range(nk)]

        UG, UL = len(units(0)), len(units(1))
        width = (128, QL)
        base_u, base_o = (0, UG), (0, len(tiles(0)))

        def ends(n):
            return {u: o for u, (o, kt) in enumerate(units(n)) if kt == tiles(n)[o][2] - 1}

        D_VALUES, D_COPY, D_DEN, D_NORM, D_OUT = 1, 2, 3, 4, (7, 6)
        D_GUESS = 4

        def wo_group(n, o):
            b, t, _ = tiles(n)[o]
            per = 4 if n == 0 else 5
            w = width[n]
            count = NQT if n == 0 else NL
            first = t // per * per
            full = t % per == per - 1 or t == count - 1
            g = sum(1 for m in range(o) if wo_full(n, m))
            return (t % per) * w, full, (L * b + first * w, min(L * b + (t + 1) * w, L * b + L)), g

        def wo_full(n, o):
            b, t, _ = tiles(n)[o]
            per = 4 if n == 0 else 5
            return t % per == per - 1 or t == (NQT if n == 0 else NL) - 1

        def pe_core(pe, n):
            U, E, TL, w = units(n), ends(n), tiles(n), width[n]
            wo = wts["g_o" if n == 0 else "l_o"]

            def scores(u, hp):
                o, kt = U[u]
                b, t, _ = TL[o]
                if hp == 0 and kt == 0:
                    if t == 0:
                        pe.wait_ge(k_in[b], 9 * 16 * (n + 1))
                        pe.wait_ge(q_in[2 * b], 9 * 16 * (n + 1))
                    if w * t < CH < w * t + w or w * t == CH:
                        pe.wait_ge(q_in[2 * b + 1], 9 * 16 * (n + 1))
                if u == 0:
                    pe.wait_ge(parts_ready, NIT * (n + 1))
                else:
                    pe.wait_ge(exp_done, 2 * (base_u[n] + u) + hp - 1)
                k0 = WIN + 128 * kt if n == 0 else QL * t
                for kv in (2 * hp, 2 * hp + 1):
                    out_ = bank[kv][:, 0:4 * w].rearrange("p (h q) -> p h q", h=4)
                    ins = pe.matmul(out_, k9[b][:, kv, k0:k0 + 128],
                                    q9[b][:, 4 * kv:4 * kv + 4, w * t:w * t + w], start=True, stop=True)
                ins.then_inc(scores_ready, 1)

            def values(u):
                o, kt = U[u]
                b, t, nk = TL[o]
                if kt == nk - 1:
                    if n == 0:
                        pe.wait_ge(masked, 2 * (o + 1))
                    else:
                        pe.wait_ge(masked, 2 * base_o[n] + o + 1)
                        pe.wait_ge(masked_by_pool, o + 1)
                else:
                    pe.wait_ge(exp_done, 2 * (base_u[n] + u + 1))
                if kt == 0 and o >= 2:
                    pe.wait_ge(osb_ready, base_o[n] + o - 1)
                if u == 0:
                    pe.wait_ge(v_copied, n + 1)
                tile = (NQT if n == 0 else NL) * b + (kt if n == 0 else t)
                for kv in range(KVH):
                    p = probs[(2 * u + kv // 2) % RING]
                    ins = pe.matmul(bank[4 + o % 2][32 * kv:32 * kv + 32, 0:4 * w], vt[:, tile, kv, :],
                                    p[:, kv % 2 * CH:kv % 2 * CH + 4 * w], start=(kt == 0), stop=(kt == nk - 1))
                ins.then_inc(pv_done, 1)

            def denominators(o):
                pe.wait_ge(osb_ready, base_o[n] + o + 1)
                if o >= 1:
                    pe.wait_ge(den_read, base_o[n] + o)
                pe.matmul(bank[6][:, 0:4 * w], const(K_DEN, 128), osb[o % 3][:, 0:4 * w], start=True, stop=True)\
                    .then_inc(den_ready, 1)

            def outputs(o):
                at, full, cols, g = wo_group(n, o)
                pe.wait_ge(on_ready, base_o[n] + o + 1)
                if at == 0 and g >= 1:
                    if n == 0:
                        pe.wait_ge(resid_ready, NCH * 2 + g)
                    elif (g - 1) % 3 == 0:
                        pe.wait_ge(added, (g - 1) // 3 + 1)
                    else:
                        pe.wait_ge(resid_ready, NCH * 3 + (g - 1) // 3 * 2 + (g - 1) % 3)
                for h in range(4):
                    ins = pe.matmul(bank[7][:, at:at + w], wo[:, 128 * h:128 * h + 128],
                                    onrm[o % 2][:, w * h:w * h + w], start=(h == 0), stop=(h == 3))
                ins.then_inc(wo_ready, 1)

            scores(0, 0)
            scores(0, 1)
            for u in range(len(U) + D_OUT[n]):
                if u + 1 < len(U):
                    scores(u + 1, 0)
                if D_VALUES <= u < len(U) + D_VALUES:
                    values(u - D_VALUES)
                if u + 1 < len(U):
                    scores(u + 1, 1)
                if u - D_OUT[n] in E:
                    outputs(E[u - D_OUT[n]])
                if u - D_DEN in E:
                    denominators(E[u - D_DEN])

        def act_core(act, n):
            U, E, w = units(n), ends(n), width[n]
            for u in range(len(U) + D_GUESS):
                for hp in range(2 if u < len(U) else 0):
                    s = 2 * u + hp
                    act.wait_ge(scores_ready, 2 * base_u[n] + s + 1)
                    if s >= RING:
                        act.wait_ge(pv_done, base_u[n] + (s - RING) // 2 + 1)
                    p = probs[s % RING].rearrange("p (k c) -> p k c", k=2)[:, :, 0:4 * w]
                    act.activation(p, two[hp][:, :, 0:4 * w], ACT.Exp, scale=HD ** -0.5).then_inc(exp_done, 1)
                if n == 1 and u - D_GUESS in E:
                    o = E[u - D_GUESS]
                    r = rec[o % 2][:, 0:4 * w]
                    act.wait_ge(den_ready, base_o[n] + o + 1)
                    if o >= 2:
                        act.wait_ge(on_ready, base_o[n] + o - 1)
                    link(act, act.activation(r, bank[6][:, 0:4 * w], ACT.Ln))
                    act.activation(r, r, ACT.Exp, scale=-1.0).then_inc(guessed, 1)
                if u - D_COPY in E:
                    o = E[u - D_COPY]
                    act.wait_ge(pv_done, base_u[n] + u - D_COPY + 1)
                    if o >= 3:
                        act.wait_ge(on_ready, base_o[n] + o - 2)
                    act.activation(osb[o % 3][:, 0:4 * w], bank[4 + o % 2][:, 0:4 * w], ACT.Copy)\
                        .then_inc(osb_ready, 1)

        def core_mask(n):
            return spread(spread(const(K_CAUS, 128) if n == 0 else const(K_BAND, QL), 1, 4), 1, 2)

        def masked_part(s, w):
            return probs[s % RING].rearrange("p (k c) -> p k c", k=2)[:, :, 0:4 * w]\
                .rearrange("p k (h q) -> p k h q", h=4)

        def pool_core(pool):
            for u in range(UL):
                pool.wait_ge(exp_done, 2 * (UG + u) + 2)
                v = masked_part(2 * u + 1, width[1])
                pool.tensor_tensor(v, v, core_mask(1), MUL).then_inc(masked_by_pool, 1)

        def dve_core(dve, n):
            U, E, TL, w = units(n), ends(n), tiles(n), width[n]
            if n == 1:
                dve.wait_ge(parts_out[0], sent(max(j for j in range(2 * NIT) if slot_of[j] == 0)))
            mask, r2 = core_mask(n), rec2[:, 0:4 * w]

            def weigh(o, sign, r):
                if o >= 2:
                    dve.wait_ge(wo_ready, base_o[n] + o - 1)
                dve.scalar_tensor_tensor(onrm[o % 2][:, 0:4 * w], osb[o % 3][:, 0:4 * w], sign, r, MUL, MUL)\
                    .then_inc(on_ready, 1)

            for u in range(len(U) + D_OUT[n]):
                if u < len(U) and u in E:
                    s = 2 * u
                    for hp in range(2 if n == 0 else 1):
                        dve.wait_ge(exp_done, 2 * base_u[n] + s + hp + 1)
                        v = masked_part(s + hp, w)
                        dve.tensor_tensor(v, v, mask, MUL).then_inc(masked, 1)
                if n == 1 and u - D_NORM in E:
                    o = E[u - D_NORM]
                    r = rec[o % 2][:, 0:4 * w]
                    dve.wait_ge(guessed, o + 1)
                    if o >= 1:
                        dve.wait_ge(on_ready, base_o[n] + o)
                    dve.tensor_tensor(r2, bank[6][:, 0:4 * w], r, MUL).then_inc(den_read, 1)
                    dve.wait_ge(den_read, base_o[n] + o + 1)
                    link(dve, dve.scalar_tensor_tensor(r2, r2, 2.0, r, SUB, MUL))
                    weigh(o, -1.0, r2)
                if n == 0 and u - D_NORM in E:
                    o = E[u - D_NORM]
                    dve.wait_ge(den_ready, base_o[n] + o + 1)
                    if o >= 1:
                        dve.wait_ge(on_ready, base_o[n] + o)
                    dve.reciprocal(rec[0], bank[6][:, 0:4 * w]).then_inc(den_read, 1)
                    dve.wait_ge(den_read, base_o[n] + o + 1)
                    weigh(o, 1.0, rec[0])
                if u - D_OUT[n] in E:
                    o = E[u - D_OUT[n]]
                    at, full, (x0, x1), g = wo_group(n, o)
                    if full:
                        dve.wait_ge(wo_ready, base_o[n] + o + 1)
                        dve.wait_ge(x_kept if n == 0 else x_added, NCH)
                        ins = dve.tensor_tensor(X[:, x0:x1], X[:, x0:x1], bank[7][:, 0:x1 - x0], ADD)
                        ins.then_inc(resid_ready if n == 0 or g % 3 > 0 else added, 1)

        r2w, r2b, firstw, sel2f = wts["r2_w"], wts["r2_b"], wts["first"], wts["sel2"]
        m2_w1 = place(0, E2 * FF2)
        m2_w2 = place(E2 * FF2, E2 * 4, 128)
        D0 = 16896
        rt = place(D0, NT, E2)
        mk = place(D0 + 128, NT, E2)
        mk2 = place(D0 + 256, NT, 2 * E2)
        mrow = place(D0 + 512, 2, NT)
        mt = place(D0 + 1024, T)
        mtb = place(D0 + 3072, T, dt=bf16)
        selb = place(D0 + 4096, E2 + 1, 128, dt=bf16)
        pbx = place(D0 + 4864, T)
        ge = [work[:, 3 * T + CH * n:3 * T + CH * n + CH] for n in range(4)]
        up_halves = [place_half(D, E2 * FF2) for D in (2 * E2 * FF2, 0)]
        down_halves = [place_half(D, E2 * 4, 128) for D in (3 * E2 * FF2, E2 * FF2)]
        x2_halves = [[place_half(D0 + 6912 + CH * (2 * n + a), CH) for a in range(2)] for n in range(2)]
        xe = [[place_half(D0 + 8960 + CH * (2 * n + a), CH) for a in range(2)] for n in range(2)]
        g_halves = [[place_half(D0 + 11008 + CH * (2 * n + a), CH) for a in range(2)] for n in range(4)]
        w2_split, x2_split, gelu_split = (sem(n) for n in ("w_split_2", "x_split_2", "gelu_split"))
        route2_ready, sig_in, sig_out, mk_ready, mt_ready, mt_copied = (
            sem(n) for n in ("route2_ready", "sig_in", "sig_out", "mk_ready", "mt_ready", "mt_copied"))
        mb_ready, xe_ready, up2_ready, gelu_done, down2, m2_out, pb_ready, pb_copied = (
            sem(n) for n in ("mb_ready", "xe_ready", "up2_ready", "gelu_done", "down2", "m2_out", "pb_ready", "pb_copied"))
        KBE = FF2 // 128
        XFIRST = 5

        def sp_moe2(sp):
            sp.wait_ge(pv_done, UG + NL)
            sp.dma_start(m2_w1, dram["m2_w1"]).then_inc(m2_in, 16)
            sp.dma_start(m2_w2, dram["m2_w2"].rearrange("p (a b) -> p a b", b=128)).then_inc(m2_in, 16)

        def pe_moe2(pe):
            for t in range(NT):
                pe.wait_ge(normed, NCH * 4 + t // 4 + 1)
                ins = pe.matmul(bank[0][:, 8 * t:8 * t + 8], X[:, 128 * t:128 * t + 128], r2w[:, :],
                                start=True, stop=True)
            ins.then_inc(route2_ready, 1)
            pe.wait_ge(mk_ready, 1)
            for g in range(NCH):
                if g >= 2:
                    pe.wait_ge(mt_copied, g - 1)
                for t in range(4 * g, 4 * g + 4):
                    ins = pe.transpose(bank[1 + g % 2][0:16, 128 * (t % 4):128 * (t % 4) + 128], mk2[:, t], const(K_ID, 128))
                ins.then_inc(mt_ready, 1)
            pe.wait_ge(mt_copied, NCH)
            pe.wait_ge(m2_in, 32)

            def masks(n):
                c, e = n // E2, n % E2
                if n >= 1:
                    pe.wait_ge(xe_ready, n)
                pe.matmul(bank[0][:, :], selb[0:16, e, :], mtb[0:16, tok(c)], start=True, stop=True)\
                    .then_inc(mb_ready, 1)

            def up(m):
                n, k = m // KBE, m % KBE
                e = n % E2
                pe.wait_ge(xe_ready, n + 1)
                if m >= 4:
                    pe.wait_ge(gelu_done, m - 3)
                pe.wait_ge(w2_split, 2 * e + 1)
                at = FF2 * e + 128 * k
                product(pe, bank[1 + m % 4][:, :], [w[:, at:at + 128] for w in up_halves], xe[n % 2],
                        True, True).then_inc(up2_ready, 1)

            def down(m):
                n, k = m // KBE, m % KBE
                c, e = n // E2, n % E2
                if e == 0 and k == 0:
                    if c == 1:
                        pe.wait_ge(pb_copied, NCH)
                    if c >= 2:
                        pe.wait_ge(resid_ready, NCH * 4 + c - 1)
                pe.wait_ge(gelu_split, m + 1)
                pe.wait_ge(w2_split, 2 * e + 2)
                product(pe, bank[6 + c % 2][:, :], [w[:, KBE * e + k, :] for w in down_halves], g_halves[m % 4],
                        e == 0 and k == 0, e == E2 - 1 and k == KBE - 1).then_inc(down2, 1)

            masks(0)
            masks(1)
            M = NCH * E2 * KBE
            for m in range(4):
                up(m)
            for m in range(M):
                if m + 4 < M:
                    up(m + 4)
                if m % KBE == 0 and m // KBE + 2 < NCH * E2:
                    masks(m // KBE + 2)
                if m % KBE == 0 and 1 <= m // KBE <= NCH:
                    c = m // KBE - 1
                    if c >= 1:
                        pe.wait_ge(pb_copied, c)
                    pe.matmul(bank[7][:, :], sel2f[:, 128 * E2:128 * E2 + 128], mt[0:16, tok(c)],
                              start=True, stop=True).then_inc(pb_ready, 1)
                down(m)

        def act_moe2(act):
            act.wait_ge(sig_in, 1)
            act.activation(rt, rt, ACT.Sigmoid).then_inc(sig_out, 1)
            for m in range(NCH * E2 * KBE):
                act.wait_ge(up2_ready, m + 1)
                if m >= 4:
                    act.wait_ge(down2, m - 3)
                act.activation(g_halves[m % 4][0], bank[1 + m % 4][:, :], ACT.Gelu)
                act.activation(ge[m % 4], bank[1 + m % 4][:, :], ACT.Gelu).then_inc(gelu_done, 1)

        def pool_moe2(pool):
            pool.wait_ge(m2_in, 32)
            pool.wait_ge(pv_done, UG + UL)

            def chunk(c):
                pool.wait_ge(normed, NCH * 4 + c + 1)
                if c >= 2:
                    pool.wait_ge(xe_ready, E2 * (c - 1))
                halve(pool, x2_halves[c % 2][0], x2_halves[c % 2][1], X[:, tok(c)], x2_split)

            for e in range(E2):
                w = slice(FF2 * e, FF2 * e + FF2)
                halve(pool, up_halves[0][:, w], up_halves[1][:, w], m2_w1[:, w], w2_split)
                w = slice(KBE * e, KBE * e + KBE)
                halve(pool, down_halves[0][:, w], down_halves[1][:, w], m2_w2[:, w], w2_split)
                if e >= XFIRST:
                    chunk(e - XFIRST)
            for c in range(E2 - XFIRST, NCH):
                chunk(c)

        def dve_moe2(dve):
            dve.wait_ge(route2_ready, 1)
            g = "p (t e) -> p t e"
            dve.tensor_tensor(rt, bank[0][:, 0:128].rearrange(g, e=E2), spread(r2b[:, :], 1, NT), ADD)\
                .then_inc(sig_in, 1)
            link(dve, dve.tensor_copy(selb[0:16], sel2f[:, :].rearrange("p (a b) -> p a b", b=128)))
            dve.wait_ge(sig_out, 1)
            link(dve, dve.tensor_reduce(mrow[:, 0], rt, AX.X, ALU.max))
            link(dve, dve.tensor_tensor(mk, rt, spread(mrow[:, 0], 2, E2), ALU.is_equal))
            link(dve, dve.tensor_tensor(mk, mk, firstw[:, :].rearrange(g, e=E2), MUL))
            link(dve, dve.tensor_reduce(mrow[:, 1], mk, AX.X, ALU.max))
            link(dve, dve.tensor_tensor(mk2[:, :, 0:E2], mk, spread(mrow[:, 1], 2, E2), ALU.is_equal))
            dve.tensor_tensor(mk2[:, :, E2:], mk2[:, :, 0:E2], spread(mrow[:, 0], 2, E2), MUL).then_inc(mk_ready, 1)
            for c in range(NCH):
                dve.wait_ge(mt_ready, c + 1)
                link(dve, dve.tensor_copy(mt[0:16, tok(c)], bank[1 + c % 2][0:16, :]))
                dve.tensor_copy(mtb[0:16, tok(c)], mt[0:16, tok(c)]).then_inc(mt_copied, 1)
            def result(c):
                dve.wait_ge(m2_out_at(c)[0], m2_out_at(c)[1])
                t = pbx[:, tok(c)]
                link(dve, dve.tensor_tensor(t, t, bank[6 + c % 2][:, :], MUL))
                dve.tensor_tensor(X[:, tok(c)], X[:, tok(c)], t, ADD).then_inc(resid_ready, 1)

            def masked_tokens(n):
                c = n // E2
                dve.wait_ge(mb_ready, n + 1)
                dve.wait_ge(x2_split, c + 1)
                if n >= 2:
                    dve.wait_ge(up2_ready, KBE * (n - 1))
                for a in range(2):
                    ins = dve.tensor_tensor(xe[n % 2][a], x2_halves[c % 2][a].bitcast(f32), bank[0][:, :], MUL)
                ins.then_inc(xe_ready, 1)

            masked_tokens(0)
            masked_tokens(1)
            for m in range(NCH * E2 * KBE):
                dve.wait_ge(gelu_done, m + 1)
                if m >= 4:
                    dve.wait_ge(down2, m - 3)
                high, low = g_halves[m % 4]
                dve.tensor_tensor(low, ge[m % 4], high.bitcast(f32), SUB).then_inc(gelu_split, 1)
                n = m // KBE + 2
                if m % KBE == 1 and n < NCH * E2:
                    masked_tokens(n)
                if m % KBE == 2 and 1 <= m // KBE <= NCH:
                    c = m // KBE - 1
                    dve.wait_ge(pb_ready, c + 1)
                    dve.tensor_copy(pbx[:, tok(c)], bank[7][:, :]).then_inc(pb_copied, 1)
                if m % (KBE * E2) == KBE * 2 and m > KBE * E2:
                    result(m // (KBE * E2) - 1)
            result(NCH - 1)

        def m2_out_at(c):
            return down2, KBE * E2 * (c + 1)

        block = stack.enter_context(nc.Block())

        @block.sync
        def _(sp):
            sp_ssm(sp)
            n_norms = 1
            if stages >= 2:
                sp_moe1(sp)
                n_norms = 2
            if stages >= 3:
                sp_attn(sp, 0)
                sp_attn(sp, 1)
                sp_moe2(sp)
                n_norms = 5
            if stages >= 4:
                n_norms = 6
            for c in range(NCH):
                sp.wait_ge(normed, NCH * (n_norms - 1) + c + 1)
                sp.dma_start(out[:, tok(c)], X[:, tok(c)]).then_inc(sem_out, 16)
            sp.wait_ge(m2_in, 32) if stages >= 3 else None
            sp.wait_ge(sem_out, 16 * NCH)

        @block.gpsimd
        def _(pool):
            pool_ssm(pool)
            if stages >= 2:
                pool_moe1(pool)
            if stages >= 3:
                pool_attn(pool)
            if stages >= 4:
                pool_moe2(pool)

        @block.tensor
        def _(pe):
            pe_ssm(pe)
            pe_norm(pe, 0, False)
            if stages >= 2:
                pe_moe1(pe)
                pe_norm(pe, 1, False)
            if stages >= 3:
                for n in range(2):
                    pe_norm(pe, 2 + n, True)
                    pe_proj(pe, n)
                    pe_core(pe, n)
                pe_norm(pe, 4, False)
            if stages >= 4:
                pe_moe2(pe)
                pe_norm(pe, 5, False)

        @block.scalar
        def _(act):
            act_ssm(act)
            act_norm(act, 0, 0)
            if stages >= 2:
                act_moe1(act)
                act_norm(act, 1, 0)
            if stages >= 3:
                for n in range(2):
                    act_norm(act, 2 + n, 1)
                    act_proj(act, n)
                    act_core(act, n)
                act_norm(act, 4, 0)
            if stages >= 4:
                act_moe2(act)
                act_norm(act, 5, 0)

        @block.vector
        def _(dve):
            dve_tables(dve)
            dve_ssm(dve)
            dve_norm(dve, 0, 0)
            if stages >= 2:
                dve_moe1(dve)
                dve_norm(dve, 1, 0)
            if stages >= 3:
                for n in range(2):
                    dve_norm(dve, 2 + n, 1)
                    dve_proj(dve, n)
                    dve_core(dve, n)
                dve_norm(dve, 4, 0)
            if stages >= 4:
                dve_moe2(dve)
                dve_norm(dve, 5, 0)


def kernel(**inputs):
    from concourse import bacc
    from concourse.bass_utils import run_bass_kernel_spmd

    nc = bacc.Bacc("TRN2", target_bir_lowering=False, num_devices=1)
    arrays = {"in_" + k: v for k, v in lay_out({k: np.asarray(v) for k, v in inputs.items()}).items()}
    dram = {k[3:]: nc.dram_tensor(k, v.shape, mybir.dt.from_np(v.dtype), kind="ExternalInput").ap()
            for k, v in arrays.items()}
    out = nc.dram_tensor("out", (DM, T), mybir.dt.float32, kind="ExternalOutput").ap()
    build(nc, dram, out)
    r = run_bass_kernel_spmd(nc, [arrays], core_ids=[0])
    return np.ascontiguousarray(np.asarray(r.results[0]["out"]).T).reshape(B, L, DM)
```
